# Optimizing a Trainium2 kernel written in Bass

```python
import numpy as np
import jax
import jax.numpy as jnp

def _softmax(x, axis=-1):
    return jax.nn.softmax(x, axis=axis)

def _gelu(x):
    return jax.nn.gelu(x, approximate=True)

def _silu(x):
    return jax.nn.silu(x)

def _sigmoid(x):
    return jax.nn.sigmoid(x)

def _layernorm(x, axis=-1, eps=1e-05):
    m = jnp.mean(x, axis=axis, keepdims=True)
    v = jnp.var(x, axis=axis, keepdims=True)
    return (x - m) / jnp.sqrt(v + eps)

def _scatter_add(tgt, idx, src, axis=0):
    return tgt.at[idx].add(src)

def _segment_sum(src, seg, n):
    return jax.ops.segment_sum(src, seg, n)
kernel_name = 'mk_gnn_ffn_d2_gnn_r8_456778'

def setup_inputs(seed: int=0):
    np.random.seed(seed)
    _w = jnp.asarray

    def _rec_inputs():
        import jax
        import jax.numpy as jnp
        _gk = jax.random.key(seed)
        x = -0.0003713 + 1 * jax.random.normal(jax.random.fold_in(_gk, 1), (12500, 256), jnp.float32)
        _s = jax.random.randint(jax.random.fold_in(_gk, 2), (100000,), 0, 12500, jnp.int32)
        _d = jax.random.randint(jax.random.fold_in(_gk, 3), (100000,), 0, 12500, jnp.int32)
        _loop = jnp.arange(12500, dtype=jnp.int32)
        src = jnp.concatenate([_s, _d, _loop])
        dst = jnp.concatenate([_d, _s, _loop])
        _o = jnp.argsort(dst, stable=True)
        src = src[_o]
        dst = dst[_o]
        edge_type_8 = jax.random.randint(jax.random.fold_in(_gk, 13), (212500,), 0, 8, jnp.int32)
        edge_weight = jax.random.uniform(jax.random.fold_in(_gk, 14), (212500,), jnp.float32, 0.0, 1)
        return (x, src, dst, edge_type_8, edge_weight)
    x, src, dst, edge_type_8, edge_weight = _rec_inputs()

    def _L0_gnn_setup():
        import jax, jax.numpy as jnp
        import numpy as np
        N_NODES = 6250
        N_EDGES = 100000
        IN_FEAT = 256
        OUT_FEAT = 256
        NUM_RELS = 8
        NUM_BASES = 8
        SUBMAT_IN = IN_FEAT // NUM_BASES
        SUBMAT_OUT = OUT_FEAT // NUM_BASES
        key = jax.random.key(seed)
        k_h, k_w, k_src, k_dst, k_rel, k_norm = jax.random.split(key, 6)
        h = jax.random.normal(k_h, (N_NODES, IN_FEAT), dtype=jnp.float32)
        weight = jax.random.normal(k_w, (NUM_RELS, NUM_BASES * SUBMAT_IN * SUBMAT_OUT), dtype=jnp.float32) * 0.05
        edge_src = jax.random.randint(k_src, (N_EDGES,), 0, N_NODES, dtype=jnp.int32)
        edge_dst = jax.random.randint(k_dst, (N_EDGES,), 0, N_NODES, dtype=jnp.int32)
        edge_rel = jax.random.randint(k_rel, (N_EDGES,), 0, NUM_RELS, dtype=jnp.int32)
        edge_norm = jax.random.uniform(k_norm, (N_EDGES,), dtype=jnp.float32)
        return {'h': h, 'weight': weight, 'edge_src': edge_src, 'edge_dst': edge_dst, 'edge_rel': edge_rel, 'edge_norm': edge_norm}
    _L0_gnn_all = _L0_gnn_setup()
    _L0_gnn_in = {k: v for k, v in _L0_gnn_all.items() if k in ('weight',)}
    del _L0_gnn_all

    def _L0_ffn_setup():
        import jax, jax.numpy as jnp
        import numpy as np
        B, S, D = (8, 512, 256)
        H = 4 * D
        CAPACITY = 0.5
        key = jax.random.key(seed)
        ks = jax.random.split(key, 6)
        x = jax.random.normal(ks[0], (B, S, D), dtype=jnp.float32)
        attention_mask = jnp.zeros((B, 1, 1, S), dtype=jnp.float32)
        wr = jax.random.normal(ks[1], (D, 1), dtype=jnp.float32) * 0.02
        br = jnp.zeros((1,), dtype=jnp.float32)
        w1 = jax.random.normal(ks[2], (D, H), dtype=jnp.float32) * 0.02
        b1 = jnp.zeros((H,), dtype=jnp.float32)
        w2 = jax.random.normal(ks[3], (H, D), dtype=jnp.float32) * 0.02
        b2 = jnp.zeros((D,), dtype=jnp.float32)
        return {'x': x, 'attention_mask': attention_mask, 'wr': wr, 'br': br, 'w1': w1, 'b1': b1, 'w2': w2, 'b2': b2}
    _L0_ffn_all = _L0_ffn_setup()
    _L0_ffn_in = {k: v for k, v in _L0_ffn_all.items() if k in ('attention_mask', 'wr', 'br', 'w1', 'b1', 'w2', 'b2')}
    del _L0_ffn_all

    def _L1_gnn_setup():
        import jax, jax.numpy as jnp
        import numpy as np
        N = 12500
        E = 200000
        IN = 256
        H = 4
        C = 64
        key = jax.random.key(seed)
        k1, k2, k3, k4, k5, k6 = jax.random.split(key, 6)
        x = jax.random.normal(k1, (N, IN), dtype=jnp.float32)
        edge_index = jax.random.randint(k2, (2, E), 0, N, dtype=jnp.int64)
        W = jax.random.normal(k3, (IN, H * C), dtype=jnp.float32) * (1.0 / np.sqrt(IN))
        att_src = jax.random.normal(k4, (H, C), dtype=jnp.float32) * 0.1
        att_dst = jax.random.normal(k5, (H, C), dtype=jnp.float32) * 0.1
        bias = jax.random.normal(k6, (H * C,), dtype=jnp.float32) * 0.01
        return {'x': x, 'edge_index': edge_index, 'W': W, 'att_src': att_src, 'att_dst': att_dst, 'bias': bias}
    _L1_gnn_all = _L1_gnn_setup()
    _L1_gnn_in = {k: v for k, v in _L1_gnn_all.items() if k in ('W', 'att_src', 'att_dst', 'bias')}
    del _L1_gnn_all

    def _L1_ffn_setup():
        import jax, jax.numpy as jnp
        import numpy as np
        B, S, D, E, H, K = (4, 512, 256, 8, 512, 2)
        key = jax.random.key(seed)
        ks = jax.random.split(key, 6)
        x = jax.random.normal(ks[0], (B, S, D), jnp.float32)
        Wg = jax.random.normal(ks[1], (D, E), jnp.float32) * 0.02
        bg = jnp.zeros((E,), jnp.float32)
        W1 = jax.random.normal(ks[2], (E, D, H), jnp.float32) * 0.02
        b1 = jnp.zeros((E, H), jnp.float32)
        W2 = jax.random.normal(ks[3], (E, H, D), jnp.float32) * 0.02
        b2 = jnp.zeros((E, D), jnp.float32)
        return {'x': x, 'Wg': Wg, 'bg': bg, 'W1': W1, 'b1': b1, 'W2': W2, 'b2': b2}
    _L1_ffn_all = _L1_ffn_setup()
    _L1_ffn_in = {k: v for k, v in _L1_ffn_all.items() if k in ('Wg', 'bg', 'W1', 'b1', 'W2', 'b2')}
    del _L1_ffn_all
    return {'x': x, 'src': src, 'dst': dst, 'edge_type_8': edge_type_8, 'edge_weight': edge_weight, 'L0_gnn_weight': _L0_gnn_in['weight'], 'L0_ffn_attention_mask': _L0_ffn_in['attention_mask'], 'L0_ffn_wr': _L0_ffn_in['wr'], 'L0_ffn_br': _L0_ffn_in['br'], 'L0_ffn_w1': _L0_ffn_in['w1'], 'L0_ffn_b1': _L0_ffn_in['b1'], 'L0_ffn_w2': _L0_ffn_in['w2'], 'L0_ffn_b2': _L0_ffn_in['b2'], 'L1_gnn_W': _L1_gnn_in['W'], 'L1_gnn_att_src': _L1_gnn_in['att_src'], 'L1_gnn_att_dst': _L1_gnn_in['att_dst'], 'L1_gnn_bias': _L1_gnn_in['bias'], 'L1_ffn_Wg': _L1_ffn_in['Wg'], 'L1_ffn_bg': _L1_ffn_in['bg'], 'L1_ffn_W1': _L1_ffn_in['W1'], 'L1_ffn_b1': _L1_ffn_in['b1'], 'L1_ffn_W2': _L1_ffn_in['W2'], 'L1_ffn_b2': _L1_ffn_in['b2']}

def reference(x, src, dst, edge_type_8, edge_weight, L0_gnn_weight, L0_ffn_attention_mask, L0_ffn_wr, L0_ffn_br, L0_ffn_w1, L0_ffn_b1, L0_ffn_w2, L0_ffn_b2, L1_gnn_W, L1_gnn_att_src, L1_gnn_att_dst, L1_gnn_bias, L1_ffn_Wg, L1_ffn_bg, L1_ffn_W1, L1_ffn_b1, L1_ffn_W2, L1_ffn_b2):
    import jax
    import jax.numpy as jnp

    def _L0_gnn_ref(h, weight, edge_src, edge_dst, edge_rel, edge_norm):
        import jax, jax.numpy as jnp
        import numpy as np
        N_NODES = 6250
        N_EDGES = 100000
        IN_FEAT = 256
        OUT_FEAT = 256
        NUM_RELS = 8
        NUM_BASES = 8
        SUBMAT_IN = IN_FEAT // NUM_BASES
        SUBMAT_OUT = OUT_FEAT // NUM_BASES
        'RGCNBlockLayer forward (self_loop=False, bias=None, activation=None).\n\n            Per relation r: agg_r[v] = sum_{(u->v) in rel r} norm_e * h[u]\n            then block-diagonal matmul out_r = blockmm(agg_r, W_r); output = sum_r out_r.\n            '
        N, in_feat = h.shape
        R = weight.shape[0]
        msg = h[edge_src] * edge_norm[:, None]
        seg = edge_rel * N + edge_dst
        agg = jax.ops.segment_sum(msg, seg, num_segments=R * N)
        agg = agg.reshape(R, N, NUM_BASES, SUBMAT_IN)
        W = weight.reshape(R, NUM_BASES, SUBMAT_IN, SUBMAT_OUT)
        out = jnp.einsum('rnbi,rbio->nbo', agg, W)
        return out.reshape(N, NUM_BASES * SUBMAT_OUT)

    def _L0_ffn_ref(x, attention_mask, wr, br, w1, b1, w2, b2):
        import jax, jax.numpy as jnp
        import numpy as np
        B, S, D = (8, 512, 256)
        H = 4 * D
        CAPACITY = 0.5
        b, s, d = x.shape
        weights = (jnp.einsum('bsd,do->bso', x, wr) + br)[..., 0]
        k = max(1, int(CAPACITY * s))
        kk = k - 1 if k > 1 else 1
        _, idx = jax.lax.top_k(weights, k)
        sel_idx = idx[:, :kk]
        sel = jnp.take_along_axis(x, sel_idx[:, :, None], axis=1)
        h = jax.nn.gelu(jnp.einsum('bkd,dh->bkh', sel, w1) + b1)
        y = jnp.einsum('bkh,hd->bkd', h, w2) + b2
        w_sel = jnp.take_along_axis(weights, sel_idx, axis=1)
        y = y * w_sel[..., None]
        batch_idx = jnp.arange(b)[:, None]
        processed = jnp.zeros_like(x).at[batch_idx, sel_idx].set(y)
        return processed + x

    def _L1_gnn_ref(x, edge_index, W, att_src, att_dst, bias):
        import jax, jax.numpy as jnp
        import numpy as np
        N = 12500
        E = 200000
        IN = 256
        H = 4
        C = 64
        n = x.shape[0]
        loops = jnp.arange(n, dtype=edge_index.dtype)
        src = jnp.concatenate([edge_index[0], loops])
        dst = jnp.concatenate([edge_index[1], loops])
        xp = (x @ W).reshape(n, H, C)
        a_src = jnp.einsum('nhc,hc->nh', xp, att_src)
        a_dst = jnp.einsum('nhc,hc->nh', xp, att_dst)
        alpha = jax.nn.leaky_relu(a_src[src] + a_dst[dst], negative_slope=0.2)
        amax = jax.ops.segment_max(alpha, dst, num_segments=n)
        amax = jnp.where(jnp.isfinite(amax), amax, 0.0)
        ex = jnp.exp(alpha - amax[dst])
        denom = jax.ops.segment_sum(ex, dst, num_segments=n)
        w = ex / denom[dst]
        msg = xp[src] * w[..., None]
        agg = jax.ops.segment_sum(msg, dst, num_segments=n)
        out = agg.reshape(n, H * C) + bias
        return jax.nn.elu(out)

    def _L1_ffn_ref(x, Wg, bg, W1, b1, W2, b2):
        import jax, jax.numpy as jnp
        import numpy as np
        B, S, D, E, H, K = (4, 512, 256, 8, 512, 2)
        Bv, Sv, Dv = x.shape
        gate_scores = x @ Wg + bg
        _, idx = jax.lax.top_k(gate_scores, K)
        mask = jax.nn.one_hot(idx, E, dtype=x.dtype).sum(axis=-2)
        xf = x.reshape(-1, Dv)
        mf = mask.reshape(-1, E)
        h = jax.nn.gelu(jnp.einsum('td,edh->teh', xf, W1) + b1[None], approximate=False)
        y = jnp.einsum('teh,ehd->ted', h, W2) + b2[None]
        out = jnp.einsum('ted,te->td', y, mf)
        return out.reshape(Bv, Sv, Dv)
    edge_index = jnp.stack([src, dst])
    x = x + _L0_gnn_ref(_layernorm(x, axis=-1), L0_gnn_weight, src, dst, edge_type_8, edge_weight)
    x = x + _L0_ffn_ref(_layernorm(x, axis=-1)[None], L0_ffn_attention_mask, L0_ffn_wr, L0_ffn_br, L0_ffn_w1, L0_ffn_b1, L0_ffn_w2, L0_ffn_b2)[0]
    x = x + _L1_gnn_ref(_layernorm(x, axis=-1), edge_index, L1_gnn_W, L1_gnn_att_src, L1_gnn_att_dst, L1_gnn_bias)
    x = x + _L1_ffn_ref(_layernorm(x, axis=-1)[None], L1_ffn_Wg, L1_ffn_bg, L1_ffn_W1, L1_ffn_b1, L1_ffn_W2, L1_ffn_b2)[0]
    return x

_drawn_inputs = setup_inputs


def setup_inputs(seed=0):
    import zlib

    import numpy as np

    out = dict(_drawn_inputs(seed))
    spreads = {'L0_ffn_b1': (0.0, 0.8),
     'L0_ffn_b2': (0.0, 0.646),
     'L1_ffn_bg': (0.0, 0.1),
     'L1_ffn_b1': (0.0, 0.491),
     'L1_ffn_b2': (0.0, 0.1)}
    factors = {'L0_ffn_wr': 3.734,
     'L0_ffn_w1': 4.25,
     'L0_ffn_w2': 3.976,
     'L1_gnn_bias': 8.0,
     'L1_gnn_att_dst': 3.38}
    for name, (base, spread) in spreads.items():
        noise = np.random.default_rng([zlib.crc32(name.encode()), seed]).standard_normal(out[name].shape)
        drawn = base * np.exp(spread * noise) if base else spread * noise
        out[name] = jnp.asarray(drawn.astype(out[name].dtype))
    for name, factor in factors.items():
        out[name] = (out[name] * factor).astype(out[name].dtype)
    return out
```

```python
from contextlib import ExitStack

import concourse.bass as bass
from concourse import mybir

F32 = mybir.dt.float32
I32 = mybir.dt.int32
ALU = mybir.AluOpType
ACT = mybir.ActivationFunctionType
AX = mybir.AxisListType
ds = bass.ds

P = 128
N = 12500
E = 212500
D = 256
HALVES = D // P
R = 8
NB, SB = 8, 32
H0 = 1024
KEEP = 12500 // 2 - 1
HEADS, CH = 4, 64
X, H1 = 8, 512
NT = -(-N // P)
NP = NT * P
ACC = NP + P
ROW = -(-(-(-E // P)) // P) * P
CHUNKS = ROW
KR = ROW // P
EPS = 1e-5
BIG = 1e30
U = 16
GRP = 4
ITER = CHUNKS // U
SELS = 4
PICKS = 8
PAIRS = NT // 2


def by_tiles(eng, step):
    step(0, 0, 0, 2)
    step(1, 0, 1, 2)
    with eng.Fori(1, PAIRS - 1) as i:
        step(2 * i, i, 0, 2)
        step(2 * i + 1, i, 1, 2)
    step(NT - 2, PAIRS - 1, 0, 1)
    step(NT - 1, PAIRS - 1, 1, 0)


def wait_past(eng, semaphore, n):
    if not isinstance(n, int) or n > 0:
        eng.wait_ge(semaphore, n)


def gnn_kernel(nc, a, out):
    ctx = ExitStack()

    def dram(name, shape, dt=F32):
        return nc.dram_tensor(name, shape, dt, kind="Internal").ap()

    rel_table = dram("rel_table", [R * NP, D])
    skip1 = dram("skip1", [NP, D])
    ffn1 = dram("ffn1", [NP, D])
    x2_rows = dram("x2_rows", [NP, D])
    xp_table = dram("xp_table", [NP, D])
    share_rows = dram("share_rows", [P, CHUNKS, HEADS])
    logit_table = dram("logit_table", [NP, 2 * HEADS])

    with ctx:
        in_use = []

        def sem(name):
            in_use.append(nc.alloc_semaphore(name=name))
            return in_use[-1]

        def end_stage():
            nc.clear_and_free_semaphores(in_use)
            in_use.clear()
            nc.all_engine_barrier()

        def at(stack, name, shape, dt=F32):
            return stack.enter_context(nc.sbuf_tensor(name, shape, dt))

        def bank(stack, name, *shape, banks=1):
            t = stack.enter_context(nc.psum_tensor(name, [P, 512 * banks], F32))
            size = 1
            for n in shape:
                size *= n
            view = t[:, 0:size]
            return view.rearrange("p (a b) -> p a b", a=shape[0]) if len(shape) == 2 else view

        ident = at(ctx, "ident", [P, P])
        iota_i = at(ctx, "iota_i", [P, P], I32)
        window = at(ctx, "window", [P, P])
        ones = at(ctx, "ones", [P, P])
        neg_half = at(ctx, "neg_half", [P, 1])
        eps = at(ctx, "eps", [P, 1])
        logits = at(ctx, "logits", [P, NT])
        made = sem("made")
        made_v = sem("made_v")

        with nc.Block() as block:
            @block.gpsimd
            def _(pool):
                pool.memset(ident[:, :], 0.0).then_inc(made, 1)
                pool.iota(iota_i[:, :], pattern=[[1, P]], base=0, channel_multiplier=0).then_inc(made, 1)
                pool.memset(neg_half[:, :], -0.5).then_inc(made, 1)
                pool.memset(eps[:, :], EPS).then_inc(made, 1)
                pool.wait_ge(made, 4)
                pool.affine_select(out=ident[:, :], in_=ident[:, :], compare_op=ALU.not_equal, fill=1.0,
                                   base=0, pattern=[[-1, P]], channel_multiplier=1).then_inc(made, 1)

            @block.vector
            def _(v):
                v.memset(ones[:, :], 1.0).then_inc(made_v, 1)
                v.wait_ge(made, 5)
                v.tensor_copy(window[:, :], iota_i[:, :]).then_inc(made_v, 1)

        end_stage()

        with ExitStack() as st:
            rel_w = at(st, "rel_w", [P, HALVES, R * P])
            xt = at(st, "s1_x", [P, 2, D])
            stat = at(st, "s1_stat", [P, 2, 6])
            mv = at(st, "s1_mv", [P, 2, 2])
            ve = at(st, "s1_ve", [P, 2, 1])
            rstd = at(st, "s1_rstd", [P, 2, 1])
            h = at(st, "s1_h", [P, 2, D])
            hT = at(st, "s1_hT", [P, 2, HALVES, P])
            rows = at(st, "s1_rows", [P, 2, R, D])
            psT = [bank(st, f"s1_psT{b}", HALVES, P) for b in range(2)]
            psO = [bank(st, f"s1_psO{k}", R * P, banks=2) for k in range(HALVES)]
            w_in, x_in = sem("s1_w_in"), [sem(f"s1_x_in{b}") for b in range(2)]
            stats_done, stats_seen, moments, rstd_step, normed = sem("s1_stats"), sem("s1_stats_seen"), sem("s1_moments"), sem("s1_rstd_step"), sem("s1_normed")
            turned, hT_ready = sem("s1_turned"), sem("s1_hT_ready")
            product = [sem(f"s1_product{k}") for k in range(HALVES)]
            evicted = [sem(f"s1_evicted{k}") for k in range(HALVES)]
            stored = [sem(f"s1_stored{b}") for b in range(2)]
            x_tiles = a["x"]
            table_tiles = rel_table.rearrange("(r n) d -> n r d", r=R)

            with nc.Block() as block:
                @block.sync
                def _(sp):
                    sp.dma_start(rel_w[:, :, :], a["rel_w"]).then_inc(w_in, 16)

                    def load(t, i, b):
                        sp.dma_start(xt[:, b, :], x_tiles[ds(t * P, P), :]).then_inc(x_in[b], 16)

                    load(0, 0, 0)
                    load(1, 0, 1)
                    with sp.Fori(0, PAIRS - 1) as i:
                        for b in range(2):
                            sp.wait_ge(normed, 2 * i + b + 1)
                            load(2 * i + b + 2, i + 1, b)

                @block.gpsimd
                def _(pool):
                    def step(t, i, b, left):
                        pool.wait_ge(moments, t + 1)
                        pool.tensor_tensor(ve[:, b, :], mv[:, b, 1:2], eps[:, :], ALU.add).then_inc(rstd_step, 1)
                        pool.wait_ge(rstd_step, 2 * t + 1)
                        pool.tensor_tensor(rstd[:, b, :], ve[:, b, :], neg_half[:, :], ALU.pow).then_inc(rstd_step, 1)

                    by_tiles(pool, step)

                @block.vector
                def _(v):
                    def norm(t, i, b):
                        v.wait_ge(x_in[b], 16 * i + 16)
                        v.bn_stats(stat[:, b, :], xt[:, b, :]).then_inc(stats_done, 1)
                        v.wait_ge(stats_done, t + 1)
                        v.sem_inc(stats_seen, 1)
                        v.bn_aggr(mv[:, b, :], stat[:, b, :]).then_inc(moments, 1)
                        v.wait_ge(rstd_step, 2 * t + 2)
                        v.tensor_scalar(h[:, b, :], xt[:, b, :], mv[:, b, 0:1], rstd[:, b, :],
                                        ALU.subtract, ALU.mult).then_inc(normed, 1)

                    def evict(t, i, b):
                        v.wait_ge(product[0], t + 1)
                        wait_past(v, stored[b], 16 * i)
                        v.tensor_copy(rows[:, b, :, 0:P], psO[0][:, :].rearrange("p (r o) -> p r o", r=R)).then_inc(evicted[0], 1)

                    def step(t, i, b, left):
                        if left:
                            wait_past(v, turned, t)
                            norm(t + 1, i + b, 1 - b)
                        evict(t, i, b)

                    norm(0, 0, 0)
                    by_tiles(v, step)

                @block.scalar
                def _(act):
                    def copy_hT(t, b):
                        act.wait_ge(turned, t + 1)
                        act.activation(hT[:, b, :, :], psT[b][:, :, :], ACT.Copy).then_inc(hT_ready, 1)

                    def step(t, i, b, left):
                        if left:
                            wait_past(act, product[1], t)
                            copy_hT(t + 1, 1 - b)
                        act.wait_ge(product[1], t + 1)
                        wait_past(act, stored[b], 16 * i)
                        act.activation(rows[:, b, :, P:D], psO[1][:, :].rearrange("p (r o) -> p r o", r=R), ACT.Copy).then_inc(evicted[1], 1)
                        act.wait_ge(evicted[0], t + 1)
                        act.wait_ge(evicted[1], t + 1)
                        act.dma_start(table_tiles[ds(t * P, P), :, :], rows[:, b, :, :]).then_inc(stored[b], 16)

                    copy_hT(0, 0)
                    by_tiles(act, step)
                    for b in range(2):
                        act.wait_ge(stored[b], 16 * PAIRS)

                @block.tensor
                def _(pe):
                    def turn(t, b):
                        pe.wait_ge(normed, t + 1)
                        for k in range(HALVES):
                            mm = pe.transpose(psT[b][:, k, :], h[:, b, k * P:(k + 1) * P], ident[:, :])
                        mm.then_inc(turned, 1)

                    def step(t, i, b, left):
                        if left:
                            wait_past(pe, hT_ready, t)
                            turn(t + 1, 1 - b)
                        pe.wait_ge(hT_ready, t + 1)
                        for k in range(HALVES):
                            wait_past(pe, evicted[k], t)
                            for c in range(R * P // 512):
                                mm = pe.matmul(psO[k][:, c * 512:(c + 1) * 512], hT[:, b, k, :],
                                               rel_w[:, k, c * 512:(c + 1) * 512], start=True, stop=True)
                            mm.then_inc(product[k], 1)

                    pe.wait_ge(w_in, 16)
                    turn(0, 0)
                    by_tiles(pe, step)
        end_stage()

        def aggregate(name, table, sums, index, local, first, scale, per_head):
            with ExitStack() as st:
                rows = at(st, f"{name}_rows", [P, U, D])
                staged = at(st, f"{name}_staged", [P, U], I32)
                pick = at(st, f"{name}_pick", [P, PICKS, P])
                apart = at(st, f"{name}_apart", [P, PICKS, P]) if per_head else None
                scaled = at(st, f"{name}_scaled", [P, SELS, D]) if per_head else None
                part = [bank(st, f"{name}_part{k}", HALVES, P) for k in range(SELS)]
                idx_taken, idx_ready, idx_seen = sem(f"{name}_idx_taken"), sem(f"{name}_idx_ready"), sem(f"{name}_idx_seen")
                gathered = [sem(f"{name}_gathered{s}") for s in range(U)]
                rows_scaled = sem(f"{name}_rows_scaled")
                picked, apart_go, apart_done = sem(f"{name}_picked"), sem(f"{name}_apart_go"), sem(f"{name}_apart_done")
                product, added, cleared = sem(f"{name}_product"), sem(f"{name}_added"), sem(f"{name}_cleared")
                rows_used, used_from = (rows_scaled, 0) if per_head else (product, 1)
                GROUPS = U // GRP

                with nc.Block() as block:
                    @block.scalar
                    def _(act):
                        def matrices(n, half, first_pass=False):
                            if not first_pass:
                                act.wait_ge(product, n * GRP - GRP + 1)
                            act.sem_inc(apart_go, 1)
                            for j in range(GRP):
                                act.activation(apart[:, half * GRP + j, :], window[:, :], ACT.Abs,
                                               bias=local[:, ds(n * GRP + j, 1)]).then_inc(apart_done, 1)
                            act.wait_ge(apart_done, n * GRP + GRP)
                            act.activation(pick[:, half * GRP:(half + 1) * GRP, :], apart[:, half * GRP:(half + 1) * GRP, :],
                                           ACT.Relu, bias=ones[:, 0:1], scale=-1.0).then_inc(picked, 1)

                        for g in range(GROUPS):
                            act.activation(staged[:, g * GRP:(g + 1) * GRP], index[:, g * GRP:(g + 1) * GRP],
                                           ACT.Copy).then_inc(idx_ready, 1)
                        if per_head:
                            matrices(0, 0, True)
                            matrices(1, 1, True)
                        with act.Fori(1, ITER) as i:
                            for g in range(GROUPS):
                                for s in range(g * GRP, (g + 1) * GRP):
                                    act.wait_ge(gathered[s], 16 * i)
                                act.sem_inc(idx_taken, 1)
                                act.activation(staged[:, g * GRP:(g + 1) * GRP], index[:, ds(i * U + g * GRP, GRP)],
                                               ACT.Copy).then_inc(idx_ready, 1)
                                if per_head:
                                    matrices(GROUPS * i - GROUPS + g + 2, g % 2)
                        if per_head:
                            for g in range(GROUPS):
                                if GROUPS * (ITER - 1) + g + 2 < GROUPS * ITER:
                                    matrices(GROUPS * (ITER - 1) + g + 2, g % 2)

                    @block.gpsimd
                    def _(pool):
                        def gathers(i, g, first_pass):
                            if not first_pass:
                                pool.wait_ge(rows_used, U * i - U + (g + 1) * GRP + used_from)
                            pool.wait_ge(idx_ready, GROUPS * i + g + 1)
                            pool.sem_inc(idx_seen, 1)
                            for s in range(g * GRP, (g + 1) * GRP):
                                pool.indirect_dma_start(
                                    out=rows[:, s, :], out_offset=None, in_=table[:, :],
                                    in_offset=bass.IndirectOffsetOnAxis(ap=staged[:, s:s + 1], axis=0),
                                ).then_inc(gathered[s], 16)

                        for g in range(GROUPS):
                            gathers(0, g, True)
                        with pool.Fori(1, ITER) as i:
                            for g in range(GROUPS):
                                gathers(i, g, False)

                    @block.tensor
                    def _(pe):
                        pe.sem_inc(product, 1)
                        with pe.Fori(0, ITER) as i:
                            for s in range(U):
                                c = i * U + s
                                if per_head:
                                    pe.wait_ge(rows_scaled, c + 1)
                                    pe.wait_ge(picked, i * GROUPS + s // GRP + 1)
                                else:
                                    pe.wait_ge(gathered[s], 16 * i + 16)
                                    pe.wait_ge(picked, c + 1)
                                pe.wait_ge(added, c + 1)
                                for k in range(HALVES):
                                    left = scaled[:, s % SELS, k * P:(k + 1) * P] if per_head else rows[:, s, k * P:(k + 1) * P]
                                    mm = pe.matmul(part[s % SELS][:, k, :], left, pick[:, s % PICKS, :], start=True, stop=True)
                                mm.then_inc(product, 1)

                    @block.vector
                    def _(v):
                        def matrix(c, s):
                            v.tensor_scalar(pick[:, s % PICKS, :], window[:, :], local[:, ds(c, 1)], scale[:, ds(c, 1)],
                                            ALU.is_equal, ALU.mult).then_inc(picked, 1)

                        def scaling(i, s):
                            c = i * U + s
                            v.wait_ge(gathered[s], 16 * i + 16)
                            v.tensor_tensor(scaled[:, s % SELS, :].rearrange("p (h c) -> p h c", h=HEADS),
                                            rows[:, s, :].rearrange("p (h c) -> p h c", h=HEADS),
                                            scale[:, ds(c, 1), :].rearrange("p o h -> p (o h)").unsqueeze(2).broadcast_to([P, HEADS, CH]),
                                            ALU.mult).then_inc(rows_scaled, 1)

                        def add(c, s, at_node):
                            v.wait_ge(product, c + 1)
                            v.wait_ge(added, c + 3)
                            v.tensor_tensor(sums[:, :, ds(at_node, P)], sums[:, :, ds(at_node, P)],
                                            part[(s - 1) % SELS][:, :, :], ALU.add).then_inc(added, 1)

                        v.memset(sums[:, :, :], 0.0).then_inc(cleared, 1)
                        v.memset(part[SELS - 1][:, :, :], 0.0).then_inc(cleared, 1)
                        v.sem_inc(added, 3)
                        if not per_head:
                            matrix(0, 0)
                            matrix(1, 1)
                        v.wait_ge(cleared, 2)
                        with v.Fori(0, ITER) as i:
                            for s in range(0, U, 2):
                                c = i * U + s
                                for j in range(2):
                                    if per_head:
                                        scaling(i, s + j)
                                    else:
                                        matrix(c + j + 2, (s + j + 2) % U)
                                both = v.value_load(first[0:1, ds(i * (U // 2) + s // 2, 1)], min_val=0, max_val=2 ** 31 - 1)
                                for j, at_node in enumerate((both & 0xffff, both >> 16)):
                                    add(c + j, s + j, nc.s_assert_within(at_node, min_val=0, max_val=N,
                                                                         skip_runtime_bounds_check_because="a destination, at most N"))
                        at_node = v.value_load(first[0:1, CHUNKS // 2:CHUNKS // 2 + 1], min_val=0, max_val=N)
                        add(CHUNKS, 0, at_node)

        def pair_up(v, first, alone, done):
            lower, upper = alone[:, 0:CHUNKS:2], alone[:, 1:CHUNKS:2]
            v.tensor_scalar(first[:, 0:CHUNKS // 2], upper, 16, None, ALU.logical_shift_left).then_inc(done, 1)
            v.wait_ge(done, 1)
            v.tensor_tensor(first[:, 0:CHUNKS // 2], first[:, 0:CHUNKS // 2], lower, ALU.bitwise_or).then_inc(done, 1)
            v.tensor_copy(first[:, CHUNKS // 2:CHUNKS // 2 + 1], alone[:, CHUNKS:CHUNKS + 1]).then_inc(done, 1)

        sums_of = ExitStack()
        sums = at(sums_of, "sums", [P, HALVES, ACC])
        with ExitStack() as st:
            first = at(st, "s2_first", [1, CHUNKS // 2 + 1], I32)
            alone = at(st, "s2_alone", [1, CHUNKS + 1], I32)
            first_all = at(st, "s2_first_all", [P, CHUNKS], I32)
            index = at(st, "s2_index", [P, CHUNKS], I32)
            source = at(st, "s2_source", [P, CHUNKS], I32)
            local = at(st, "s2_local", [P, CHUNKS + 2])
            weight = at(st, "s2_weight", [P, CHUNKS + 2])
            ends = at(st, "s2_ends", [P, CHUNKS], I32)
            edges_in, edges_ready = sem("s2_edges_in"), sem("s2_edges_ready")
            with nc.Block() as block:
                @block.sync
                def _(sp):
                    sp.dma_start(alone[:, :], a["dst_first"]).then_inc(edges_in, 16)
                    sp.dma_start(first_all[:, :], a["dst_first"][0:1, 1:CHUNKS + 1].broadcast_to([P, CHUNKS])).then_inc(edges_in, 16)
                    sp.dma_start(index[:, :], a["type_chunk"]).then_inc(edges_in, 16)
                    sp.dma_start(source[:, :], a["src_chunk"]).then_inc(edges_in, 16)
                    sp.dma_start(ends[:, :], a["dst_chunk"]).then_inc(edges_in, 16)
                    sp.dma_start(weight[:, 0:CHUNKS], a["weight_chunk"]).then_inc(edges_in, 16)
                    sp.wait_ge(edges_in, 16 * 6)

                @block.vector
                def _(v):
                    v.memset(local[:, CHUNKS:CHUNKS + 2], 0.0)
                    v.memset(weight[:, CHUNKS:CHUNKS + 2], 0.0)
                    v.wait_ge(edges_in, 16 * 6)
                    pair_up(v, first, alone, edges_ready)
                    v.scalar_tensor_tensor(out=index[:, :], in0=index[:, :], scalar=float(NP), in1=source[:, :],
                                           op0=ALU.mult, op1=ALU.add).then_inc(edges_ready, 1)
                    v.tensor_tensor(local[:, 0:CHUNKS], ends[:, :], first_all[:, :], ALU.subtract).then_inc(edges_ready, 1)
            aggregate("s2", rel_table, sums, index, local, first, weight, False)
        end_stage()

        with ExitStack() as st:
            w1 = at(st, "s3_w1", [P, HALVES, H0])
            w2 = at(st, "s3_w2", [P, H0 // P, D])
            b1 = at(st, "s3_b1", [P, H0 // P])
            b2 = at(st, "s3_b2", [P, D])
            wr = at(st, "s3_wr", [P, D])
            xt = at(st, "s3_x", [P, 2, D])
            fixed = at(st, "s3_fixed", [P, 2, HALVES, P])
            x1 = at(st, "s3_x1", [P, 2, D])
            stat = at(st, "s3_stat", [P, 2, 6])
            mv = at(st, "s3_mv", [P, 2, 2])
            ve = at(st, "s3_ve", [P, 2, 1])
            rstd = at(st, "s3_rstd", [P, 2, 1])
            h = at(st, "s3_h", [P, 2, D])
            skip = at(st, "s3_skip", [P, 2, D])
            routed = at(st, "s3_routed", [P, 2, D])
            logit = at(st, "s3_logit", [P, 2, 1])
            hT = at(st, "s3_hT", [P, 2, HALVES, P])
            hid = at(st, "s3_hid", [P, 2, H0 // P, P])
            y = at(st, "s3_y", [P, 2, D])
            psX = [bank(st, f"s3_psX{b}", D) for b in range(2)]
            psH = bank(st, "s3_psH", HALVES, P)
            psG = [bank(st, f"s3_psG{k}", 4, P) for k in range(2)]
            psY = bank(st, "s3_psY", D)
            w_in, x_in = sem("s3_w_in"), [sem(f"s3_x_in{b}") for b in range(2)]
            held, held_go, unturned, x1_done = sem("s3_held"), sem("s3_held_go"), sem("s3_unturned"), sem("s3_x1_done")
            stats_done, stats_seen, moments, rstd_step = sem("s3_stats"), sem("s3_stats_seen"), sem("s3_moments"), sem("s3_rstd_step")
            normed, skipped, logit_done, logit_go = sem("s3_normed"), sem("s3_skipped"), sem("s3_logit_done"), sem("s3_logit_go")
            turned, hT_ready = sem("s3_turned"), sem("s3_hT_ready")
            up_done, active = [sem(f"s3_up_done{k}") for k in range(2)], [sem(f"s3_active{k}") for k in range(2)]
            down_done, y_done = sem("s3_down_done"), sem("s3_y_done")
            skip_out, y_out = [sem(f"s3_skip_out{b}") for b in range(2)], [sem(f"s3_y_out{b}") for b in range(2)]
            with nc.Block() as block:
                @block.sync
                def _(sp):
                    def load(t, b):
                        sp.dma_start(xt[:, b, :], a["x"][ds(t * P, P), :]).then_inc(x_in[b], 16)

                    def step(t, i, b, left):
                        if left == 2:
                            sp.wait_ge(x1_done, t + 1)
                            load(t + 2, b)
                        sp.wait_ge(skipped, t + 1)
                        sp.dma_start(skip1[ds(t * P, P), :], skip[:, b, :]).then_inc(skip_out[b], 16)
                        sp.wait_ge(y_done, t + 1)
                        sp.dma_start(ffn1[ds(t * P, P), :], y[:, b, :]).then_inc(y_out[b], 16)

                    load(0, 0)
                    load(1, 1)
                    sp.dma_start(wr[:, :], a["wr"].broadcast_to([P, D])).then_inc(w_in, 16)
                    sp.dma_start(w1[:, :, :], a["ffn_w1"]).then_inc(w_in, 16)
                    sp.dma_start(b1[:, :], a["ffn_b1"]).then_inc(w_in, 16)
                    sp.dma_start(w2[:, :, :], a["ffn_w2"]).then_inc(w_in, 16)
                    sp.dma_start(b2[:, :], a["ffn_b2"].broadcast_to([P, D])).then_inc(w_in, 16)
                    by_tiles(sp, step)
                    for b in range(2):
                        sp.wait_ge(skip_out[b], 16 * PAIRS)
                        sp.wait_ge(y_out[b], 16 * PAIRS)

                @block.gpsimd
                def _(pool):
                    def step(t, i, b, left):
                        pool.wait_ge(moments, t + 1)
                        pool.tensor_tensor(ve[:, b, :], mv[:, b, 1:2], eps[:, :], ALU.add).then_inc(rstd_step, 1)
                        pool.wait_ge(rstd_step, 2 * t + 1)
                        pool.tensor_tensor(rstd[:, b, :], ve[:, b, :], neg_half[:, :], ALU.pow).then_inc(rstd_step, 1)

                    by_tiles(pool, step)

                @block.scalar
                def _(act):
                    def hold(t, b):
                        act.sem_inc(held_go, 1)
                        act.activation(fixed[:, b, :, :], sums[:, :, ds(t * P, P)], ACT.Copy).then_inc(held, 1)

                    def copy_hT(t, b):
                        act.wait_ge(turned, t + 1)
                        act.activation(hT[:, b, :, :], psH, ACT.Copy).then_inc(hT_ready, 1)
                        act.wait_ge(logit_done, t + 1)
                        act.sem_inc(logit_go, 1)
                        act.activation(logits[:, ds(t, 1)], logit[:, b, :], ACT.Copy)

                    def step(t, i, b, left):
                        if left == 2:
                            act.wait_ge(unturned, t + 1)
                            hold(t + 2, b)
                        for k in range(2):
                            act.wait_ge(up_done[k], t + 1)
                            for c in range(4):
                                g = act.activation(hid[:, b, 4 * k + c, :], psG[k][:, c, :], ACT.Gelu_apprx_tanh,
                                                   bias=b1[:, 4 * k + c:4 * k + c + 1])
                            g.then_inc(active[k], 1)
                        if left:
                            copy_hT(t + 1, 1 - b)

                    hold(0, 0)
                    hold(1, 1)
                    act.wait_ge(w_in, 16 * 5)
                    copy_hT(0, 0)
                    by_tiles(act, step)

                @block.tensor
                def _(pe):
                    def unturn(t, b):
                        pe.wait_ge(held, t + 1)
                        for k in range(HALVES):
                            mm = pe.transpose(psX[b][:, k * P:(k + 1) * P], fixed[:, b, k, :], ident[:, :])
                        mm.then_inc(unturned, 1)

                    def turn(t, b):
                        pe.wait_ge(normed, t + 1)
                        for k in range(HALVES):
                            mm = pe.transpose(psH[:, k, :], h[:, b, k * P:(k + 1) * P], ident[:, :])
                        mm.then_inc(turned, 1)

                    def step(t, i, b, left):
                        if left == 2:
                            pe.wait_ge(x1_done, t + 1)
                            unturn(t + 2, b)
                        pe.wait_ge(hT_ready, t + 1)
                        for k in range(2):
                            wait_past(pe, active[k], t)
                            for c in range(4):
                                for half in range(HALVES):
                                    mm = pe.matmul(psG[k][:, c, :], w1[:, half, (4 * k + c) * P:(4 * k + c + 1) * P],
                                                   hT[:, b, half, :], start=(half == 0), stop=(half == HALVES - 1))
                            mm.then_inc(up_done[k], 1)
                        if left:
                            turn(t + 1, 1 - b)
                        wait_past(pe, y_done, t)
                        for k in range(2):
                            pe.wait_ge(active[k], t + 1)
                            for c in range(4 * k, 4 * k + 4):
                                mm = pe.matmul(psY, hid[:, b, c, :], w2[:, c, :], start=(c == 0), stop=(c == H0 // P - 1))
                        mm.then_inc(down_done, 1)

                    unturn(0, 0)
                    unturn(1, 1)
                    pe.wait_ge(w_in, 16 * 5)
                    turn(0, 0)
                    by_tiles(pe, step)

                @block.vector
                def _(v):
                    def front(t, i, b):
                        v.wait_ge(x_in[b], 16 * i + 16)
                        wait_past(v, skip_out[b], 16 * i)
                        v.wait_ge(unturned, t + 1)
                        v.tensor_tensor(x1[:, b, :], psX[b], xt[:, b, :], ALU.add).then_inc(x1_done, 1)
                        v.wait_ge(x1_done, t + 1)
                        v.bn_stats(stat[:, b, :], x1[:, b, :]).then_inc(stats_done, 1)
                        v.wait_ge(stats_done, t + 1)
                        v.sem_inc(stats_seen, 1)
                        v.bn_aggr(mv[:, b, :], stat[:, b, :]).then_inc(moments, 1)
                        v.wait_ge(rstd_step, 2 * t + 2)
                        v.tensor_scalar(h[:, b, :], x1[:, b, :], mv[:, b, 0:1], rstd[:, b, :],
                                        ALU.subtract, ALU.mult).then_inc(normed, 1)
                        v.wait_ge(normed, t + 1)
                        v.tensor_tensor(skip[:, b, :], x1[:, b, :], h[:, b, :], ALU.add).then_inc(skipped, 1)
                        v.tensor_tensor_reduce(routed[:, b, :], h[:, b, :], wr[:, :], 1.0, 0.0, ALU.mult, ALU.add,
                                               logit[:, b, :]).then_inc(logit_done, 1)

                    def step(t, i, b, left):
                        if left:
                            front(t + 1, i + b, 1 - b)
                        v.wait_ge(down_done, t + 1)
                        wait_past(v, y_out[b], 16 * i)
                        v.tensor_tensor(y[:, b, :], psY, b2[:, :], ALU.add).then_inc(y_done, 1)

                    v.wait_ge(w_in, 16 * 5)
                    front(0, 0, 0)
                    by_tiles(v, step)
        sums_of.close()
        end_stage()

        with ExitStack() as st:
            br = at(st, "s4_br", [P, 1])
            upto = at(st, "s4_upto", [P, P])
            prefix = at(st, "s4_prefix", [P, 1], I32)
            bit = at(st, "s4_bit", [P, 1], I32)
            cand = at(st, "s4_cand", [P, 1], I32)
            flip = at(st, "s4_flip", [P, 1], I32)
            value = at(st, "s4_value", [P, 1], I32)
            taken = at(st, "s4_taken", [P, 1], I32)
            over = at(st, "s4_over", [P, NT])
            same = at(st, "s4_same", [P, NT])
            count = at(st, "s4_count", [P, 1])
            left_over = at(st, "s4_left_over", [P, 1])
            before = at(st, "s4_before", [P, NT])
            rank = at(st, "s4_rank", [P, NT])
            zeros = at(st, "s4_zeros", [P, NT])
            psC = bank(st, "s4_psC", 1)
            psU = bank(st, "s4_psU", NT)
            psA = bank(st, "s4_psA", NT)
            br_in, tri, biased, padded = sem("s4_br_in"), sem("s4_tri"), sem("s4_biased"), sem("s4_padded")
            done, counted, total = sem("s4_done"), sem("s4_counted"), sem("s4_total")
            OPS = 9
            with nc.Block() as block:
                @block.sync
                def _(sp):
                    sp.dma_start(br[:, :], a["br"].broadcast_to([P, 1])).then_inc(br_in, 16)
                    sp.wait_ge(br_in, 16)

                @block.gpsimd
                def _(pool):
                    pool.affine_select(out=upto[:, :], in_=ones[:, :], compare_op=ALU.is_ge, fill=0.0,
                                       base=0, pattern=[[1, P]], channel_multiplier=-1).then_inc(tri, 1)
                    pool.wait_ge(biased, 1)
                    pool.affine_select(out=logits[:, :], in_=logits[:, :], compare_op=ALU.is_ge, fill=-3.4e38,
                                       base=N - 1, pattern=[[-P, NT]], channel_multiplier=-1).then_inc(padded, 1)

                @block.tensor
                def _(pe):
                    with pe.Fori(0, 33) as i:
                        pe.wait_ge(counted, i + 1)
                        pe.matmul(psC, ones[:, :], count[:, :], start=True, stop=True).then_inc(total, 1)
                    pe.wait_ge(counted, 34)
                    pe.wait_ge(tri, 1)
                    pe.matmul(psU, upto[:, :], same[:, :], start=True, stop=True)
                    pe.matmul(psA, ones[:, :], same[:, :], start=True, stop=True).then_inc(total, 1)

                @block.vector
                def _(v):
                    v.wait_ge(br_in, 16)
                    v.tensor_scalar(logits[:, :], logits[:, :], br[:, :], None, ALU.add).then_inc(biased, 1)
                    v.memset(zeros[:, :], 0.0)
                    v.memset(prefix[:, :], 0).then_inc(done, 1)
                    v.memset(bit[:, :], -2 ** 31).then_inc(done, 1)
                    v.wait_ge(padded, 1)

                    def as_value(k):
                        v.wait_ge(done, k)
                        v.tensor_scalar(flip[:, :], cand[:, :], 31, -1, ALU.arith_shift_right, ALU.bitwise_xor).then_inc(done, 1)
                        v.wait_ge(done, k + 1)
                        v.scalar_tensor_tensor(out=value[:, :], in0=flip[:, :], scalar=-2 ** 31, in1=cand[:, :],
                                               op0=ALU.bitwise_or, op1=ALU.bitwise_xor).then_inc(done, 1)

                    with v.Fori(0, 32) as i:
                        k = i * (OPS - 1) + 2
                        v.wait_ge(done, k)
                        v.tensor_tensor(cand[:, :], prefix[:, :], bit[:, :], ALU.bitwise_or).then_inc(done, 1)
                        as_value(k + 1)
                        v.wait_ge(done, k + 3)
                        v.tensor_scalar(over[:, :], logits[:, :], value[:, :].bitcast(F32), None, ALU.is_ge).then_inc(done, 1)
                        v.wait_ge(done, k + 4)
                        v.tensor_reduce(count[:, :], over[:, :], AX.X, ALU.add).then_inc(counted, 1)
                        v.wait_ge(total, i + 1)
                        v.tensor_scalar(taken[:, :], psC, float(KEEP), -1.0, ALU.is_ge, ALU.mult).then_inc(done, 1)
                        v.wait_ge(done, k + 5)
                        v.tensor_tensor(taken[:, :], taken[:, :], bit[:, :], ALU.bitwise_and).then_inc(done, 1)
                        v.wait_ge(done, k + 6)
                        v.tensor_tensor(prefix[:, :], prefix[:, :], taken[:, :], ALU.bitwise_or).then_inc(done, 1)
                        v.tensor_scalar(bit[:, :], bit[:, :], 1, None, ALU.logical_shift_right).then_inc(done, 1)
                    k = 32 * (OPS - 1) + 2
                    v.wait_ge(done, k)
                    v.tensor_copy(cand[:, :], prefix[:, :]).then_inc(done, 1)
                    as_value(k + 1)
                    v.wait_ge(done, k + 3)
                    threshold = value[:, :].bitcast(F32)
                    v.tensor_scalar(over[:, :], logits[:, :], threshold, None, ALU.is_gt).then_inc(done, 1)
                    v.wait_ge(done, k + 4)
                    v.tensor_reduce(count[:, :], over[:, :], AX.X, ALU.add).then_inc(counted, 1)
                    v.tensor_scalar(same[:, :], logits[:, :], threshold, None, ALU.is_equal).then_inc(counted, 1)
                    v.wait_ge(total, 33)
                    v.tensor_scalar(left_over[:, :], psC, -1.0, float(KEEP), ALU.mult, ALU.add).then_inc(done, 1)
                    v.wait_ge(total, 34)
                    v.tensor_tensor_scan(before[:, :], psA, zeros[:, :], 0.0, ALU.add, ALU.add).then_inc(done, 1)
                    v.wait_ge(done, k + 6)
                    v.tensor_tensor(rank[:, :], before[:, :], psA, ALU.subtract).then_inc(done, 1)
                    v.wait_ge(done, k + 7)
                    v.tensor_tensor(rank[:, :], rank[:, :], psU, ALU.add).then_inc(done, 1)
                    v.wait_ge(done, k + 8)
                    v.scalar_tensor_tensor(out=same[:, :], in0=rank[:, :], scalar=left_over[:, :], in1=same[:, :],
                                           op0=ALU.is_le, op1=ALU.mult).then_inc(done, 1)
                    v.wait_ge(done, k + 9)
                    v.tensor_tensor(over[:, :], over[:, :], same[:, :], ALU.add).then_inc(done, 1)
                    v.wait_ge(done, k + 10)
                    v.tensor_tensor(logits[:, :], logits[:, :], over[:, :], ALU.mult).then_inc(done, 1)
        end_stage()

        with ExitStack() as st:
            wp = at(st, "s5_wp", [P, HALVES, D])
            att = at(st, "s5_att", [P, 2, D])
            yt = at(st, "s5_y", [P, 2, D])
            sk = at(st, "s5_skip", [P, 2, D])
            x2 = at(st, "s5_x2", [P, 2, D])
            stat = at(st, "s5_stat", [P, 2, 6])
            mv = at(st, "s5_mv", [P, 2, 2])
            ve = at(st, "s5_ve", [P, 2, 1])
            rstd = at(st, "s5_rstd", [P, 2, 1])
            h = at(st, "s5_h", [P, 2, D])
            hT = at(st, "s5_hT", [P, 2, HALVES, P])
            xp = at(st, "s5_xp", [P, 2, D])
            terms = at(st, "s5_terms", [P, 2, 2, D])
            head_logits = at(st, "s5_head_logits", [P, 2, 2 * HEADS])
            psH = [bank(st, f"s5_psH{b}", HALVES, P) for b in range(2)]
            psP = [bank(st, f"s5_psP{b}", D) for b in range(2)]
            w_in, y_in, sk_in = sem("s5_w_in"), [sem(f"s5_y_in{b}") for b in range(2)], [sem(f"s5_sk_in{b}") for b in range(2)]
            x2_done, stats_done, stats_seen, moments, rstd_step = sem("s5_x2_done"), sem("s5_stats"), sem("s5_stats_seen"), sem("s5_moments"), sem("s5_rstd_step")
            normed, turned, hT_ready, product = sem("s5_normed"), sem("s5_turned"), sem("s5_hT_ready"), sem("s5_product")
            xp_done, terms_done, logits_done = sem("s5_xp_done"), sem("s5_terms_done"), sem("s5_logits_done")
            x2_out, xp_out, logits_out = ([sem(f"s5_{n}_out{b}") for b in range(2)] for n in ("x2", "xp", "logits"))
            with nc.Block() as block:
                @block.sync
                def _(sp):
                    def load(t, b):
                        sp.dma_start(yt[:, b, :], ffn1[ds(t * P, P), :]).then_inc(y_in[b], 16)
                        sp.dma_start(sk[:, b, :], skip1[ds(t * P, P), :]).then_inc(sk_in[b], 16)

                    def step(t, i, b, left):
                        sp.wait_ge(x2_done, t + 1)
                        if left == 2:
                            load(t + 2, b)
                        sp.dma_start(x2_rows[ds(t * P, P), :], x2[:, b, :]).then_inc(x2_out[b], 16)
                        sp.wait_ge(xp_done, t + 1)
                        sp.dma_start(xp_table[ds(t * P, P), :], xp[:, b, :]).then_inc(xp_out[b], 16)
                        sp.wait_ge(logits_done, t + 1)
                        sp.dma_start(logit_table[ds(t * P, P), :], head_logits[:, b, :]).then_inc(logits_out[b], 16)

                    load(0, 0)
                    load(1, 1)
                    sp.dma_start(wp[:, :, :], a["att_w"]).then_inc(w_in, 16)
                    sp.dma_start(att[:, :, :], a["att"].broadcast_to([P, 2 * D]).rearrange("p (s c) -> p s c", s=2)).then_inc(w_in, 16)
                    by_tiles(sp, step)
                    for b in range(2):
                        sp.wait_ge(x2_out[b], 16 * PAIRS)
                        sp.wait_ge(xp_out[b], 16 * PAIRS)
                        sp.wait_ge(logits_out[b], 16 * PAIRS)

                @block.gpsimd
                def _(pool):
                    def step(t, i, b, left):
                        pool.wait_ge(moments, t + 1)
                        pool.tensor_tensor(ve[:, b, :], mv[:, b, 1:2], eps[:, :], ALU.add).then_inc(rstd_step, 1)
                        pool.wait_ge(rstd_step, 2 * t + 1)
                        pool.tensor_tensor(rstd[:, b, :], ve[:, b, :], neg_half[:, :], ALU.pow).then_inc(rstd_step, 1)

                    by_tiles(pool, step)

                @block.scalar
                def _(act):
                    def copy_hT(t, b):
                        act.wait_ge(turned, t + 1)
                        act.activation(hT[:, b, :, :], psH[b], ACT.Copy).then_inc(hT_ready, 1)

                    def step(t, i, b, left):
                        if left:
                            copy_hT(t + 1, 1 - b)
                        act.wait_ge(product, t + 1)
                        wait_past(act, xp_out[b], 16 * i)
                        wait_past(act, terms_done, t)
                        act.activation(xp[:, b, :], psP[b], ACT.Copy).then_inc(xp_done, 1)

                    copy_hT(0, 0)
                    by_tiles(act, step)

                @block.tensor
                def _(pe):
                    def turn(t, b):
                        pe.wait_ge(normed, t + 1)
                        for k in range(HALVES):
                            mm = pe.transpose(psH[b][:, k, :], h[:, b, k * P:(k + 1) * P], ident[:, :])
                        mm.then_inc(turned, 1)

                    def step(t, i, b, left):
                        if left:
                            turn(t + 1, 1 - b)
                        pe.wait_ge(hT_ready, t + 1)
                        wait_past(pe, xp_done, t)
                        for k in range(HALVES):
                            mm = pe.matmul(psP[b], hT[:, b, k, :], wp[:, k, :], start=(k == 0), stop=(k == HALVES - 1))
                        mm.then_inc(product, 1)

                    pe.wait_ge(w_in, 32)
                    turn(0, 0)
                    by_tiles(pe, step)

                @block.vector
                def _(v):
                    def front(t, i, b):
                        v.wait_ge(y_in[b], 16 * i + 16)
                        v.wait_ge(sk_in[b], 16 * i + 16)
                        wait_past(v, x2_out[b], 16 * i)
                        v.scalar_tensor_tensor(out=x2[:, b, :], in0=yt[:, b, :], scalar=logits[:, ds(t, 1)], in1=sk[:, b, :],
                                               op0=ALU.mult, op1=ALU.add).then_inc(x2_done, 1)
                        v.wait_ge(x2_done, t + 1)
                        v.bn_stats(stat[:, b, :], x2[:, b, :]).then_inc(stats_done, 1)
                        v.wait_ge(stats_done, t + 1)
                        v.sem_inc(stats_seen, 1)
                        v.bn_aggr(mv[:, b, :], stat[:, b, :]).then_inc(moments, 1)
                        v.wait_ge(rstd_step, 2 * t + 2)
                        v.tensor_scalar(h[:, b, :], x2[:, b, :], mv[:, b, 0:1], rstd[:, b, :],
                                        ALU.subtract, ALU.mult).then_inc(normed, 1)

                    def step(t, i, b, left):
                        if left:
                            wait_past(v, turned, t)
                            front(t + 1, i + b, 1 - b)
                        v.wait_ge(xp_done, t + 1)
                        wait_past(v, logits_out[b], 16 * i)
                        v.tensor_tensor(terms[:, b, :, :], xp[:, b, :].unsqueeze(1).broadcast_to([P, 2, D]), att[:, :, :],
                                        ALU.mult).then_inc(terms_done, 1)
                        v.wait_ge(terms_done, t + 1)
                        v.tensor_reduce(head_logits[:, b, :], terms[:, b, :, :].rearrange("p s (h c) -> p (s h) c", h=HEADS),
                                        AX.X, ALU.add).then_inc(logits_done, 1)

                    v.wait_ge(w_in, 32)
                    front(0, 0, 0)
                    by_tiles(v, step)

        end_stage()

        chans = ExitStack()
        CHANS = 2 * HEADS + 1 + HEADS
        share = at(chans, "share", [P, CHUNKS, HEADS])
        chan = at(chans, "chan", [P, CHANS, ROW])
        SRC, DST, LOOP, TOP = 0, HEADS, 2 * HEADS, 2 * HEADS + 1
        source = at(chans, "s6_source", [P, ROW], I32)
        with ExitStack() as st:
            staged = at(st, "s6_staged", [P, U], I32)
            got = at(st, "s6_got", [P, U, 2 * HEADS])
            src_in = sem("s6_src_in")
            idx_taken, idx_ready, idx_seen, keep_go, kept = sem("s6_idx_taken"), sem("s6_idx_ready"), sem("s6_idx_seen"), sem("s6_keep_go"), sem("s6_kept")
            gathered = [sem(f"s6_gathered{s}") for s in range(U)]
            with nc.Block() as block:
                @block.sync
                def _(sp):
                    sp.dma_start(source[:, :], a["src_row"]).then_inc(src_in, 16)
                    sp.wait_ge(src_in, 16)

                @block.scalar
                def _(act):
                    act.wait_ge(src_in, 16)
                    for g in range(U // GRP):
                        act.activation(staged[:, g * GRP:(g + 1) * GRP], source[:, g * GRP:(g + 1) * GRP], ACT.Copy).then_inc(idx_ready, 1)

                    def keep(i, g):
                        for s in range(g * GRP, (g + 1) * GRP):
                            act.wait_ge(gathered[s], 16 * i + 16)
                        act.sem_inc(keep_go, 1)
                        act.activation(chan[:, SRC:SRC + 2 * HEADS, ds(i * U + g * GRP, GRP)].rearrange("p c s -> p s c"),
                                       got[:, g * GRP:(g + 1) * GRP, :], ACT.Copy).then_inc(kept, 1)

                    with act.Fori(0, ITER - 1) as i:
                        for g in range(U // GRP):
                            keep(i, g)
                            act.sem_inc(idx_taken, 1)
                            act.activation(staged[:, g * GRP:(g + 1) * GRP], source[:, ds(i * U + U + g * GRP, GRP)],
                                           ACT.Copy).then_inc(idx_ready, 1)
                    for g in range(U // GRP):
                        keep(ITER - 1, g)

                @block.gpsimd
                def _(pool):
                    def gathers(i, g, first_pass):
                        if not first_pass:
                            pool.wait_ge(kept, U // GRP * i - U // GRP + g + 1)
                        pool.wait_ge(idx_ready, U // GRP * i + g + 1)
                        pool.sem_inc(idx_seen, 1)
                        for s in range(g * GRP, (g + 1) * GRP):
                            pool.indirect_dma_start(
                                out=got[:, s, :], out_offset=None, in_=logit_table[:, :],
                                in_offset=bass.IndirectOffsetOnAxis(ap=staged[:, s:s + 1], axis=0),
                            ).then_inc(gathered[s], 16)

                    for g in range(U // GRP):
                        gathers(0, g, True)
                    with pool.Fori(1, ITER) as i:
                        for g in range(U // GRP):
                            gathers(i, g, False)

        end_stage()

        with ExitStack() as st:
            ends = at(st, "s7_ends", [P, ROW], I32)
            before = at(st, "s7_before", [P, ROW], I32)
            after = at(st, "s7_after", [P, ROW], I32)
            edge_i = at(st, "s7_edge_i", [P, ROW], I32)
            goes_on = at(st, "s7_goes_on", [P, ROW])
            more = at(st, "s7_more", [P, ROW])
            cut = at(st, "s7_cut", [P, ROW])
            last = at(st, "s7_last", [P, ROW])
            loop = at(st, "s7_loop", [P, ROW])
            spare = at(st, "s7_spare", [P, ROW])
            MAXES = HEADS + 1 + HEADS
            whole = at(st, "s7_whole", [P, 2])
            border = at(st, "s7_border", [P, 2, MAXES])
            rowwise = at(st, "s7_rowwise", [MAXES, 2, P])
            carry = at(st, "s7_carry", [MAXES, P + 1])
            start = at(st, "s7_start", [P, MAXES])
            psB = [bank(st, f"s7_psB{k}", P) for k in range(2)]
            psS = bank(st, "s7_psS", MAXES)
            psW = [bank(st, f"s7_psW{k}", P) for k in range(2)]
            ends_in, edge_made, share_out = sem("s7_ends_in"), sem("s7_edge_made"), sem("s7_share_out")
            step_done = sem("s7_step_done")
            border_ready, border_turned, carry_ready, carry_turned = sem("s7_border_ready"), sem("s7_border_turned"), sem("s7_carry_ready"), sem("s7_carry_turned")
            scores_ready, exp_done, shares_ready, share_turned, share_kept = sem("s7_scores_ready"), sem("s7_exp_done"), sem("s7_shares_ready"), sem("s7_share_turned"), sem("s7_share_kept")
            TURNS = (MAXES, MAXES, HEADS, HEADS)
            with nc.Block() as block:
                @block.sync
                def _(sp):
                    sp.dma_start(ends[:, :], a["dst_row"]).then_inc(ends_in, 16)
                    sp.dma_start(before[:, :], a["dst_before"]).then_inc(ends_in, 16)
                    sp.dma_start(after[:, :], a["dst_after"]).then_inc(ends_in, 16)
                    sp.wait_ge(share_kept, KR * HEADS)
                    sp.dma_start(share_rows, share[:, :, :]).then_inc(share_out, 16)
                    sp.wait_ge(share_out, 16)

                @block.gpsimd
                def _(pool):
                    pool.iota(edge_i[:, :], pattern=[[1, ROW]], base=0, channel_multiplier=ROW).then_inc(edge_made, 1)

                @block.scalar
                def _(act):
                    act.wait_ge(scores_ready, 1)
                    act.activation(chan[:, TOP:TOP + HEADS, :], chan[:, SRC:SRC + HEADS, :], ACT.Exp).then_inc(exp_done, 1)

                @block.tensor
                def _(pe):
                    for e, n in enumerate(TURNS):
                        pe.wait_ge(border_ready, e + 1)
                        for k in range(2):
                            mm = pe.transpose(psB[k][0:n, :], border[:, k, 0:n], ident[:, :])
                        mm.then_inc(border_turned, 1)
                        pe.wait_ge(carry_ready, e + 1)
                        shift = e % 2
                        pe.transpose(psS[:, 0:n], carry[0:n, shift:shift + P], ident[0:n, 0:n]).then_inc(carry_turned, 1)
                    pe.wait_ge(shares_ready, 1)
                    for j in range(KR * HEADS):
                        k, hd = j // HEADS, j % HEADS
                        if j >= 2:
                            pe.wait_ge(share_kept, j - 1)
                        pe.transpose(psW[j % 2], chan[:, TOP + hd, k * P:(k + 1) * P], ident[:, :]).then_inc(share_turned, 1)

                @block.vector
                def _(v):
                    count = [0]

                    def then(ins):
                        count[0] += 1
                        ins.then_inc(step_done, 1)
                        v.wait_ge(step_done, count[0])

                    def exchange(e, values, largest):
                        n, back = TURNS[e], e % 2
                        order = slice(None, None, -1 if back else 1)
                        then(v.tensor_copy(border[:, 1, 0:n], whole[:, back:back + 1].broadcast_to([P, n])))
                        v.tensor_copy(border[:, 0, 0:n], values).then_inc(border_ready, 1)
                        v.wait_ge(border_turned, e + 1)
                        then(v.tensor_copy(rowwise[0:n, 0, :], psB[0][0:n, :]))
                        if largest:
                            then(v.tensor_scalar(rowwise[0:n, 1, :], psB[1][0:n, :], 1.0, BIG, ALU.subtract, ALU.mult))
                        else:
                            then(v.tensor_copy(rowwise[0:n, 1, :], psB[1][0:n, :]))
                        none = -BIG if largest else 0.0
                        outside = slice(P, P + 1) if back else slice(0, 1)
                        inside = slice(0, P) if back else slice(1, P + 1)
                        then(v.memset(carry[0:n, outside], none))
                        v.tensor_tensor_scan(carry[0:n, inside][:, order], rowwise[0:n, 1, order], rowwise[0:n, 0, order], none,
                                             ALU.add if largest else ALU.mult, ALU.max if largest else ALU.add).then_inc(carry_ready, 1)
                        v.wait_ge(carry_turned, e + 1)
                        then(v.tensor_copy(start[:, 0:n], psS[:, 0:n]))

                    def to_all(e, c0, n):
                        each = chan[:, c0:c0 + n, :]
                        then(v.tensor_tensor(each, each, last[:, :].unsqueeze(1).broadcast_to([P, n, ROW]), ALU.mult))
                        for c in range(n):
                            then(v.tensor_tensor_scan(spare[:, ::-1], more[:, ::-1], chan[:, c0 + c, ::-1], 0.0, ALU.mult, ALU.add))
                            then(v.tensor_copy(border[:, 0, c:c + 1], spare[:, 0:1]))
                        exchange(e, border[:, 0, 0:n], False)
                        for c in range(n):
                            then(v.tensor_tensor_scan(chan[:, c0 + c, ::-1], more[:, ::-1], chan[:, c0 + c, ::-1], start[:, c:c + 1], ALU.mult, ALU.add))

                    v.wait_ge(ends_in, 48)
                    v.wait_ge(edge_made, 1)
                    then(v.tensor_tensor(goes_on[:, :], ends[:, :], before[:, :], ALU.is_equal))
                    then(v.tensor_tensor(more[:, :], ends[:, :], after[:, :], ALU.is_equal))
                    then(v.tensor_tensor(loop[:, :], source[:, :], ends[:, :], ALU.is_equal))
                    then(v.tensor_reduce(whole[:, 0:1], goes_on[:, :], AX.X, ALU.min))
                    then(v.tensor_reduce(whole[:, 1:2], more[:, :], AX.X, ALU.min))
                    then(v.tensor_scalar(cut[:, :], goes_on[:, :], 1.0, BIG, ALU.subtract, ALU.mult))
                    then(v.tensor_scalar(last[:, :], more[:, :], -1.0, 1.0, ALU.mult, ALU.add))

                    def loops(c0, n):
                        return loop[:, :].unsqueeze(1).broadcast_to([P, n, ROW])

                    then(v.tensor_scalar(spare[:, :], loop[:, :], 1.0, BIG, ALU.subtract, ALU.mult))
                    each = chan[:, DST:DST + HEADS, :]
                    then(v.tensor_tensor(each, each, loops(DST, HEADS), ALU.mult))
                    then(v.tensor_tensor(each, each, spare[:, :].unsqueeze(1).broadcast_to([P, HEADS, ROW]), ALU.add))

                    def loop_place(to):
                        then(v.tensor_tensor(to, edge_i[:, :], loop[:, :], ALU.mult))
                        then(v.tensor_tensor(to, spare[:, :], to, ALU.subtract))

                    loop_place(chan[:, LOOP, :])
                    for c in range(HEADS):
                        then(v.tensor_tensor_scan(chan[:, TOP + c, :], cut[:, :], chan[:, SRC + c, :], -BIG, ALU.add, ALU.max))
                    for c in range(HEADS + 1):
                        then(v.tensor_tensor_scan(chan[:, DST + c, :], cut[:, :], chan[:, DST + c, :], -BIG, ALU.add, ALU.max))
                    exchange(0, chan[:, DST:DST + MAXES, ROW - 1:ROW].rearrange("p c o -> p (c o)"), True)
                    for c in range(MAXES):
                        then(v.tensor_tensor_scan(chan[:, DST + c, :], cut[:, :], chan[:, DST + c, :], start[:, c:c + 1], ALU.add, ALU.max))
                    to_all(1, DST, MAXES)
                    scores, dst_logits, tops = (chan[:, c:c + HEADS, :] for c in (SRC, DST, TOP))
                    for each in (scores, tops):
                        then(v.tensor_tensor(each, each, dst_logits, ALU.add))
                        for c in range(HEADS):
                            one = each[:, c, :]
                            then(v.scalar_tensor_tensor(out=one, in0=one, scalar=0.2, in1=one, op0=ALU.mult, op1=ALU.max))
                    v.tensor_tensor(scores, scores, tops, ALU.subtract).then_inc(scores_ready, 1)
                    v.wait_ge(scores_ready, 1)
                    then(v.tensor_scalar(spare[:, :], loop[:, :], 1.0, BIG, ALU.subtract, ALU.mult))
                    loop_place(cut[:, :])
                    then(v.tensor_tensor(cut[:, :], cut[:, :], chan[:, LOOP, :], ALU.is_equal))
                    then(v.tensor_tensor(cut[:, :], cut[:, :], loop[:, :], ALU.mult))
                    then(v.tensor_scalar(cut[:, :], cut[:, :], 1.0, None, ALU.add))
                    v.wait_ge(exp_done, 1)
                    then(v.tensor_tensor(tops, tops, cut[:, :].unsqueeze(1).broadcast_to([P, HEADS, ROW]), ALU.mult))
                    for c in range(HEADS):
                        then(v.tensor_tensor_scan(chan[:, DST + c, :], goes_on[:, :], chan[:, TOP + c, :], 0.0, ALU.mult, ALU.add))
                    exchange(2, chan[:, DST:DST + HEADS, ROW - 1:ROW].rearrange("p c o -> p (c o)"), False)
                    for c in range(HEADS):
                        then(v.tensor_tensor_scan(chan[:, DST + c, :], goes_on[:, :], chan[:, TOP + c, :], start[:, c:c + 1], ALU.mult, ALU.add))
                    to_all(3, DST, HEADS)
                    then(v.reciprocal(dst_logits, dst_logits))
                    v.tensor_tensor(tops, tops, dst_logits, ALU.mult).then_inc(shares_ready, 1)
                    by_chunk = share[:, :, :].rearrange("q (p k) h -> q p k h", k=KR)
                    for j in range(KR * HEADS):
                        k, hd = j // HEADS, j % HEADS
                        v.wait_ge(share_turned, j + 1)
                        v.tensor_copy(by_chunk[:, :, k, hd], psW[j % 2]).then_inc(share_kept, 1)
        chans.close()
        end_stage()

        sums = at(ctx, "sums8", [P, HALVES, ACC])
        with ExitStack() as st:
            share = at(st, "s8_share", [P, CHUNKS, HEADS])
            first = at(st, "s8_first", [1, CHUNKS // 2 + 1], I32)
            alone = at(st, "s8_alone", [1, CHUNKS + 1], I32)
            first_all = at(st, "s8_first_all", [P, CHUNKS], I32)
            index = at(st, "s8_index", [P, CHUNKS], I32)
            local = at(st, "s8_local", [P, CHUNKS])
            ends = at(st, "s8_ends", [P, CHUNKS], I32)
            edges_in, edges_ready = sem("s8_edges_in"), sem("s8_edges_ready")
            with nc.Block() as block:
                @block.sync
                def _(sp):
                    sp.dma_start(alone[:, :], a["dst_first"]).then_inc(edges_in, 16)
                    sp.dma_start(first_all[:, :], a["dst_first"][0:1, 1:CHUNKS + 1].broadcast_to([P, CHUNKS])).then_inc(edges_in, 16)
                    sp.dma_start(index[:, :], a["src_chunk"]).then_inc(edges_in, 16)
                    sp.dma_start(ends[:, :], a["dst_chunk"]).then_inc(edges_in, 16)
                    sp.dma_start(share[:, :, :], share_rows).then_inc(edges_in, 16)
                    sp.wait_ge(edges_in, 16 * 5)

                @block.vector
                def _(v):
                    v.wait_ge(edges_in, 16 * 5)
                    pair_up(v, first, alone, edges_ready)
                    v.tensor_tensor(local[:, :], first_all[:, :], ends[:, :], ALU.subtract).then_inc(edges_ready, 1)
            aggregate("s8", xp_table, sums, index, local, first, share, True)
        end_stage()

        with ExitStack() as st:
            w1 = at(st, "s9_w1", [P, X * HALVES, H1])
            w2 = at(st, "s9_w2", [P, X, H1 // P * D])
            b1 = at(st, "s9_b1", [P, X, H1 // P])
            b2 = at(st, "s9_b2", [X, D])
            wg = at(st, "s9_wg", [P, HALVES, X])
            bg = at(st, "s9_bg", [P, X])
            bias = at(st, "s9_bias", [P, D])
            lower = at(st, "s9_lower", [P, X, X])
            lower_i = at(st, "s9_lower_i", [P, X, X], I32)
            x2 = at(st, "s9_x2", [P, 2, D])
            fixed = at(st, "s9_fixed", [P, 2, HALVES, P])
            z = at(st, "s9_z", [P, 2, D])
            below = at(st, "s9_below", [P, 2, D])
            x3 = at(st, "s9_x3", [P, 2, D])
            stat = at(st, "s9_stat", [P, 2, 6])
            mv = at(st, "s9_mv", [P, 2, 2])
            ve = at(st, "s9_ve", [P, 2, 1])
            rstd = at(st, "s9_rstd", [P, 2, 1])
            h = at(st, "s9_h", [P, 2, D])
            hT = at(st, "s9_hT", [P, 2, HALVES, P])
            gate = at(st, "s9_gate", [P, 2, X])
            wins = at(st, "s9_wins", [P, 2, X, X])
            ties = at(st, "s9_ties", [P, 2, X, X])
            rank = at(st, "s9_rank", [P, 2, X])
            mask = at(st, "s9_mask", [P, 2, X])
            maskT = at(st, "s9_maskT", [X, 2, P])
            hid = at(st, "s9_hid", [P, 2, H1 // P, P])
            total = at(st, "s9_total", [P, 2, D])
            psX = bank(st, "s9_psX", D)
            psH = bank(st, "s9_psH", HALVES, P)
            psR = bank(st, "s9_psR", X)
            psM = bank(st, "s9_psM", D + P)
            psG = [bank(st, f"s9_psG{k}", H1 // P, P) for k in range(2)]
            psY = [bank(st, f"s9_psY{k}", D) for k in range(2)]
            w_in, x_in, lower_made = sem("s9_w_in"), [sem(f"s9_x_in{b}") for b in range(2)], sem("s9_lower_made")
            held_go, held, unturned, z_done, below_done, exp_done = (sem(f"s9_{n}") for n in ("held_go", "held", "unturned", "z_done", "below_done", "exp_done"))
            part_done, x3_done, stats_done, stats_seen, moments, rstd_step = (sem(f"s9_{n}") for n in ("part_done", "x3_done", "stats", "stats_seen", "moments", "rstd_step"))
            normed, turned, hT_ready, scored, gated, compared = (sem(f"s9_{n}") for n in ("normed", "turned", "hT_ready", "scored", "gated", "compared"))
            masked, mask_turned, maskT_ready, biased, begun = (sem(f"s9_{n}") for n in ("masked", "mask_turned", "maskT_ready", "biased", "begun"))
            up_done, active, down_done, added = (sem(f"s9_{n}") for n in ("up_done", "active", "down_done", "added"))
            stored = [sem(f"s9_stored{b}") for b in range(2)]
            WEIGHTS = 16 * 7
            with nc.Block() as block:
                @block.sync
                def _(sp):
                    def load(t, b):
                        sp.dma_start(x2[:, b, :], x2_rows[ds(t * P, P), :]).then_inc(x_in[b], 16)

                    def step(t, i, b, left):
                        if left == 2:
                            sp.wait_ge(part_done, t + 1)
                            load(t + 2, b)
                        sp.wait_ge(added, X * t + X)
                        sp.dma_start(out[ds(t * P, P), :], total[:, b, :]).then_inc(stored[b], 16)

                    load(0, 0)
                    load(1, 1)
                    sp.dma_start(bias[:, :], a["att_bias"].broadcast_to([P, D])).then_inc(w_in, 16)
                    sp.dma_start(wg[:, :, :], a["gate_w"]).then_inc(w_in, 16)
                    sp.dma_start(bg[:, :], a["gate_b"].broadcast_to([P, X])).then_inc(w_in, 16)
                    sp.dma_start(b1[:, :, :], a["exp_b1"]).then_inc(w_in, 16)
                    sp.dma_start(b2[:, :], a["exp_b2"]).then_inc(w_in, 16)
                    sp.dma_start(w1[:, :, :], a["exp_w1"].rearrange("p x k n -> p (x k) n")).then_inc(w_in, 16)
                    sp.dma_start(w2[:, :, :], a["exp_w2"].rearrange("p x c n -> p x (c n)")).then_inc(w_in, 16)
                    by_tiles(sp, step)
                    for b in range(2):
                        sp.wait_ge(stored[b], 16 * PAIRS)

                @block.gpsimd
                def _(pool):
                    pool.iota(lower_i[:, :, :], pattern=[[1, X], [-1, X]], base=0, channel_multiplier=0).then_inc(lower_made, 1)

                    def step(t, i, b, left):
                        pool.wait_ge(moments, t + 1)
                        pool.tensor_tensor(ve[:, b, :], mv[:, b, 1:2], eps[:, :], ALU.add).then_inc(rstd_step, 1)
                        pool.wait_ge(rstd_step, 2 * t + 1)
                        pool.tensor_tensor(rstd[:, b, :], ve[:, b, :], neg_half[:, :], ALU.pow).then_inc(rstd_step, 1)

                    by_tiles(pool, step)

                @block.scalar
                def _(act):
                    def hold(t, b):
                        act.sem_inc(held_go, 1)
                        act.activation(fixed[:, b, :, :], sums[:, :, ds(t * P, P)], ACT.Copy).then_inc(held, 1)

                    def exp_below(t, b):
                        act.wait_ge(below_done, t + 1)
                        act.activation(below[:, b, :], below[:, b, :], ACT.Exp).then_inc(exp_done, 1)

                    def copy_hT(t, b):
                        act.wait_ge(turned, t + 1)
                        act.activation(hT[:, b, :, :], psH, ACT.Copy).then_inc(hT_ready, 1)

                    def copy_maskT(t, b):
                        act.wait_ge(mask_turned, t + 1)
                        act.activation(maskT[:, b, :], psM[0:X, D:D + P], ACT.Copy).then_inc(maskT_ready, 1)

                    def step(t, i, b, left):
                        if left == 2:
                            act.wait_ge(unturned, t + 1)
                            hold(t + 2, b)
                        for e in range(X):
                            act.wait_ge(up_done, X * t + e + 1)
                            for c in range(H1 // P):
                                g = act.activation(hid[:, e % 2, c, :], psG[e % 2][:, c, :], ACT.Gelu, bias=b1[:, e, c:c + 1])
                            g.then_inc(active, 1)
                            if left and e == 1:
                                exp_below(t + 1, 1 - b)
                            if left and e == 4:
                                copy_hT(t + 1, 1 - b)
                        if left:
                            copy_maskT(t + 1, 1 - b)

                    hold(0, 0)
                    hold(1, 1)
                    act.wait_ge(w_in, WEIGHTS)
                    exp_below(0, 0)
                    copy_hT(0, 0)
                    copy_maskT(0, 0)
                    by_tiles(act, step)

                @block.tensor
                def _(pe):
                    def unturn(t, b):
                        pe.wait_ge(held, t + 1)
                        for k in range(HALVES):
                            mm = pe.transpose(psX[:, k * P:(k + 1) * P], fixed[:, b, k, :], ident[:, :])
                        mm.then_inc(unturned, 1)

                    def turn(t, b):
                        pe.wait_ge(normed, t + 1)
                        for k in range(HALVES):
                            mm = pe.transpose(psH[:, k, :], h[:, b, k * P:(k + 1) * P], ident[:, :])
                        mm.then_inc(turned, 1)

                    def score(t, b):
                        pe.wait_ge(hT_ready, t + 1)
                        for k in range(HALVES):
                            mm = pe.matmul(psR, hT[:, b, k, :], wg[:, k, :], start=(k == 0), stop=(k == HALVES - 1))
                        mm.then_inc(scored, 1)

                    def turn_mask(t, b):
                        pe.wait_ge(masked, t + 1)
                        pe.transpose(psM[0:X, D:D + P], mask[:, b, :], ident[:, :]).then_inc(mask_turned, 1)

                    def bias_sum(t, b):
                        pe.wait_ge(maskT_ready, t + 1)
                        pe.matmul(psM[:, 0:D], maskT[:, b, :], b2[:, :], start=True, stop=True).then_inc(biased, 1)

                    def up(t, e, b):
                        for c in range(H1 // P):
                            for k in range(HALVES):
                                mm = pe.matmul(psG[e % 2][:, c, :], w1[:, e * HALVES + k, c * P:(c + 1) * P], hT[:, b, k, :],
                                               start=(k == 0), stop=(k == HALVES - 1))
                        mm.then_inc(up_done, 1)

                    def down(t, e, b):
                        pe.wait_ge(active, X * t + e + 1)
                        if e >= 2:
                            pe.wait_ge(added, X * t + e - 1)
                        for c in range(H1 // P):
                            mm = pe.matmul(psY[e % 2], hid[:, e % 2, c, :], w2[:, e, c * D:(c + 1) * D],
                                           start=(c == 0), stop=(c == H1 // P - 1))
                        mm.then_inc(down_done, 1)

                    def step(t, i, b, left):
                        if left:
                            pe.wait_ge(z_done, t + 1)
                            unturn(t + 1, 1 - b)
                        wait_past(pe, active, X * t)
                        up(t, 0, b)
                        bias_sum(t, b)
                        for e in range(X):
                            if e + 1 < X:
                                up(t, e + 1, b)
                            if e < 2:
                                wait_past(pe, added, X * t)
                            down(t, e, b)
                            if left and e == 3:
                                turn(t + 1, 1 - b)
                            if left and e == 5:
                                score(t + 1, 1 - b)
                        if left:
                            turn_mask(t + 1, 1 - b)

                    pe.wait_ge(w_in, WEIGHTS)
                    unturn(0, 0)
                    turn(0, 0)
                    score(0, 0)
                    turn_mask(0, 0)
                    by_tiles(pe, step)

                @block.vector
                def _(v):
                    def residual(t, i, b):
                        v.wait_ge(x_in[b], 16 * i + 16)
                        v.wait_ge(unturned, t + 1)
                        v.tensor_tensor(z[:, b, :], psX, bias[:, :], ALU.add).then_inc(z_done, 1)
                        v.wait_ge(z_done, t + 1)
                        v.tensor_scalar(below[:, b, :], z[:, b, :], 0.0, None, ALU.min).then_inc(below_done, 1)
                        v.scalar_tensor_tensor(out=z[:, b, :], in0=z[:, b, :], scalar=0.0, in1=x2[:, b, :],
                                               op0=ALU.max, op1=ALU.add).then_inc(part_done, 1)

                    def norm(t, b):
                        v.wait_ge(exp_done, t + 1)
                        v.wait_ge(part_done, t + 1)
                        v.scalar_tensor_tensor(out=x3[:, b, :], in0=below[:, b, :], scalar=-1.0, in1=z[:, b, :],
                                               op0=ALU.add, op1=ALU.add).then_inc(x3_done, 1)
                        v.wait_ge(x3_done, t + 1)
                        v.bn_stats(stat[:, b, :], x3[:, b, :]).then_inc(stats_done, 1)
                        v.wait_ge(stats_done, t + 1)
                        v.sem_inc(stats_seen, 1)
                        v.bn_aggr(mv[:, b, :], stat[:, b, :]).then_inc(moments, 1)
                        v.wait_ge(rstd_step, 2 * t + 2)
                        v.tensor_scalar(h[:, b, :], x3[:, b, :], mv[:, b, 0:1], rstd[:, b, :],
                                        ALU.subtract, ALU.mult).then_inc(normed, 1)

                    def choose(t, b):
                        v.wait_ge(scored, t + 1)
                        v.tensor_tensor(gate[:, b, :], psR, bg[:, :], ALU.add).then_inc(gated, 1)
                        v.wait_ge(gated, t + 1)
                        other = gate[:, b, :].unsqueeze(1).broadcast_to([P, X, X])
                        own = gate[:, b, :].unsqueeze(2).broadcast_to([P, X, X])
                        v.tensor_tensor(wins[:, b, :, :], other, own, ALU.is_gt).then_inc(compared, 1)
                        v.tensor_tensor(ties[:, b, :, :], other, own, ALU.is_equal).then_inc(compared, 1)
                        v.wait_ge(compared, 5 * t + 2)
                        v.tensor_tensor(ties[:, b, :, :], ties[:, b, :, :], lower[:, :, :], ALU.mult).then_inc(compared, 1)
                        v.wait_ge(compared, 5 * t + 3)
                        v.tensor_tensor(wins[:, b, :, :], wins[:, b, :, :], ties[:, b, :, :], ALU.add).then_inc(compared, 1)
                        v.wait_ge(compared, 5 * t + 4)
                        v.tensor_reduce(rank[:, b, :], wins[:, b, :, :], AX.X, ALU.add).then_inc(compared, 1)
                        v.wait_ge(compared, 5 * t + 5)
                        v.tensor_scalar(mask[:, b, :], rank[:, b, :], 2.0, None, ALU.is_lt).then_inc(masked, 1)

                    def step(t, i, b, left):
                        v.wait_ge(biased, t + 1)
                        wait_past(v, stored[b], 16 * i)
                        v.tensor_tensor(total[:, b, :], psM[:, 0:D], x3[:, b, :], ALU.add).then_inc(begun, 1)
                        v.wait_ge(begun, t + 1)
                        for e in range(X):
                            if left and e == 0:
                                residual(t + 1, i + b, 1 - b)
                            if left and e == 3:
                                norm(t + 1, 1 - b)
                            if left and e == 7:
                                choose(t + 1, 1 - b)
                            v.wait_ge(down_done, X * t + e + 1)
                            if e:
                                v.wait_ge(added, X * t + e)
                            v.scalar_tensor_tensor(out=total[:, b, :], in0=psY[e % 2], scalar=mask[:, b, e:e + 1],
                                                   in1=total[:, b, :], op0=ALU.mult, op1=ALU.add).then_inc(added, 1)

                    v.wait_ge(lower_made, 1)
                    v.tensor_scalar(lower[:, :, :], lower_i[:, :, :], 0.5, None, ALU.is_gt)
                    v.wait_ge(w_in, WEIGHTS)
                    residual(0, 0, 0)
                    norm(0, 0)
                    choose(0, 0)
                    by_tiles(v, step)




def lay_out(x, src, dst, edge_type_8, edge_weight, L0_gnn_weight, L0_ffn_wr, L0_ffn_br, L0_ffn_w1, L0_ffn_b1,
            L0_ffn_w2, L0_ffn_b2, L1_gnn_W, L1_gnn_att_src, L1_gnn_att_dst, L1_gnn_bias, L1_ffn_Wg, L1_ffn_bg,
            L1_ffn_W1, L1_ffn_b1, L1_ffn_W2, L1_ffn_b2, L0_ffn_attention_mask=None):
    import numpy as np

    def padded(v, value):
        return np.concatenate([v, np.full(P * ROW - E, value, v.dtype)])

    def by_row(v):
        return v.reshape(P, ROW)

    def by_chunk(v):
        return v.reshape(CHUNKS, P).T

    src, dst = padded(np.asarray(src), N), padded(np.asarray(dst), N)
    x = np.asarray(x)
    blocks = np.asarray(L0_gnn_weight).reshape(R, NB, SB, SB)
    rel_w = np.zeros((P, HALVES, R, P), np.float32)
    per = P // SB
    for k in range(HALVES):
        for j in range(per):
            o = slice(j * SB, (j + 1) * SB)
            rel_w[o, k, :, o] = blocks[:, k * per + j].transpose(1, 0, 2)
    edge = np.array([-1], np.int32)
    b = {
        "x": np.concatenate([x, np.zeros((NP - N, D), x.dtype)]),
        "rel_w": rel_w.reshape(P, HALVES, R * P),
        "src_row": by_row(src), "dst_row": by_row(dst),
        "dst_before": by_row(np.concatenate([edge, dst[:-1]])),
        "dst_after": by_row(np.concatenate([dst[1:], edge])),
        "src_chunk": by_chunk(src), "dst_chunk": by_chunk(dst),
        "dst_first": np.concatenate([dst[:1], dst[::P]]).reshape(1, CHUNKS + 1),
        "type_chunk": by_chunk(padded(np.asarray(edge_type_8), 0)),
        "weight_chunk": by_chunk(padded(np.asarray(edge_weight), 0)),
        "wr": np.asarray(L0_ffn_wr).reshape(1, D), "br": np.asarray(L0_ffn_br).reshape(1, 1),
        "ffn_w1": np.asarray(L0_ffn_w1).reshape(HALVES, P, H0).transpose(1, 0, 2),
        "ffn_b1": np.asarray(L0_ffn_b1).reshape(H0 // P, P).T,
        "ffn_w2": np.asarray(L0_ffn_w2).reshape(H0 // P, P, D).transpose(1, 0, 2),
        "ffn_b2": np.asarray(L0_ffn_b2).reshape(1, D),
        "att_w": np.asarray(L1_gnn_W).reshape(HALVES, P, D).transpose(1, 0, 2),
        "att": np.stack([np.asarray(L1_gnn_att_src).reshape(D), np.asarray(L1_gnn_att_dst).reshape(D)]).reshape(1, 2 * D),
        "att_bias": np.asarray(L1_gnn_bias).reshape(1, D),
        "gate_w": np.asarray(L1_ffn_Wg).reshape(HALVES, P, X).transpose(1, 0, 2),
        "gate_b": np.asarray(L1_ffn_bg).reshape(1, X),
        "exp_w1": np.asarray(L1_ffn_W1).reshape(X, HALVES, P, H1).transpose(2, 0, 1, 3),
        "exp_b1": np.asarray(L1_ffn_b1).reshape(X, H1 // P, P).transpose(2, 0, 1),
        "exp_w2": np.asarray(L1_ffn_W2).reshape(X, H1 // P, P, D).transpose(2, 0, 1, 3),
        "exp_b2": np.asarray(L1_ffn_b2),
    }
    return {f"in_{k}": np.ascontiguousarray(v) for k, v in b.items()}


def kernel(**inputs):
    import concourse.bacc as bacc
    from concourse.bass_utils import run_bass_kernel_spmd

    arrays = lay_out(**inputs)
    nc = bacc.Bacc("TRN2", target_bir_lowering=False, num_devices=1)
    aps = {n[3:]: nc.dram_tensor(n, v.shape, mybir.dt.from_np(v.dtype), kind="ExternalInput").ap() for n, v in arrays.items()}
    out = nc.dram_tensor("out", (NP, D), F32, kind="ExternalOutput").ap()
    gnn_kernel(nc, aps, out)
    r = run_bass_kernel_spmd(nc, [arrays], core_ids=[0])
    return r.results[0]["out"][:N]
```

```python
from contextlib import ExitStack

import concourse.bass as bass
from concourse import mybir

F32 = mybir.dt.float32
I32 = mybir.dt.int32
ALU = mybir.AluOpType
ACT = mybir.ActivationFunctionType
AX = mybir.AxisListType
ds = bass.ds

P = 128
N = 12500
E = 212500
D = 256
HALVES = D // P
R = 8
NB, SB = 8, 32
H0 = 1024
KEEP = 12500 // 2 - 1
HEADS, CH = 4, 64
X, H1 = 8, 512
NT = -(-N // P)
NP = NT * P
ROW = -(-(-(-E // P)) // P) * P
CHUNKS = ROW
SPAN = 2
WIDE = SPAN * P
SPANS = CHUNKS // SPAN
ACC = NP + WIDE
KR = ROW // P
EPS = 1e-5
BIG = 1e30
U = 16
GRP = 4
ITER = CHUNKS // U
SELS = 4
PICKS = 8
PAIRS = NT // 2
TILES = 2 * NT + X
RING = 7


def by_tiles(eng, step, pairs=PAIRS):
    step(0, 0, 0, 2)
    step(1, 0, 1, 2)
    with eng.Fori(1, pairs - 1) as i:
        step(2 * i, i, 0, 2)
        step(2 * i + 1, i, 1, 2)
    step(2 * pairs - 2, pairs - 1, 0, 1)
    step(2 * pairs - 1, pairs - 1, 1, 0)


def wait_past(eng, semaphore, n):
    if not isinstance(n, int) or n > 0:
        eng.wait_ge(semaphore, n)


def gnn_kernel(nc, a, out):
    ctx = ExitStack()

    def dram(name, shape, dt=F32):
        return nc.dram_tensor(name, shape, dt, kind="Internal").ap()

    rel_table = dram("rel_table", [R * NP, D])
    mid_rows = dram("mid_rows", [NP, 2 * D])
    x2_rows = dram("x2_rows", [NP, D])
    xp_table = dram("xp_table", [NP, D])
    x3_rows = dram("x3_rows", [NP, D])
    exp_rows = dram("exp_rows", [(TILES + 2 * X) * P, D])
    y_rows = dram("y_rows", [TILES * P, D])
    share_rows = dram("share_rows", [P, CHUNKS, HEADS])
    logit_table = dram("logit_table", [NP, 2 * HEADS])

    with ctx:
        in_use = []

        def sem(name):
            in_use.append(nc.alloc_semaphore(name=name))
            return in_use[-1]

        def end_stage():
            nc.clear_and_free_semaphores(in_use)
            in_use.clear()
            nc.all_engine_barrier()

        def at(stack, name, shape, dt=F32):
            return stack.enter_context(nc.sbuf_tensor(name, shape, dt))

        def bank(stack, name, *shape, banks=1):
            t = stack.enter_context(nc.psum_tensor(name, [P, 512 * banks], F32))
            size = 1
            for n in shape:
                size *= n
            view = t[:, 0:size]
            return view.rearrange("p (a b) -> p a b", a=shape[0]) if len(shape) == 2 else view

        ident = at(ctx, "ident", [P, P])
        iota_i = at(ctx, "iota_i", [P, WIDE], I32)
        window = at(ctx, "window", [P, WIDE])
        ones = at(ctx, "ones", [P, P])
        neg_half = at(ctx, "neg_half", [P, 1])
        eps = at(ctx, "eps", [P, 1])
        logits = at(ctx, "logits", [P, NT])
        made = sem("made")
        made_v = sem("made_v")

        with nc.Block() as block:
            @block.gpsimd
            def _(pool):
                pool.memset(ident[:, :], 0.0).then_inc(made, 1)
                pool.iota(iota_i[:, :], pattern=[[1, WIDE]], base=0, channel_multiplier=0).then_inc(made, 1)
                pool.memset(neg_half[:, :], -0.5).then_inc(made, 1)
                pool.memset(eps[:, :], EPS).then_inc(made, 1)
                pool.wait_ge(made, 4)
                pool.affine_select(out=ident[:, :], in_=ident[:, :], compare_op=ALU.not_equal, fill=1.0,
                                   base=0, pattern=[[-1, P]], channel_multiplier=1).then_inc(made, 1)

            @block.vector
            def _(v):
                v.memset(ones[:, :], 1.0).then_inc(made_v, 1)
                v.wait_ge(made, 5)
                v.tensor_copy(window[:, :], iota_i[:, :]).then_inc(made_v, 1)

        end_stage()

        with ExitStack() as st:
            rel_w = at(st, "rel_w", [P, HALVES, R * P])
            xt = at(st, "s1_x", [P, 2, D])
            stat = at(st, "s1_stat", [P, 2, 6])
            mv = at(st, "s1_mv", [P, 2, 2])
            ve = at(st, "s1_ve", [P, 2, 1])
            rstd = at(st, "s1_rstd", [P, 2, 1])
            h = at(st, "s1_h", [P, 2, D])
            hT = at(st, "s1_hT", [P, 2, HALVES, P])
            rows = at(st, "s1_rows", [P, 2, R, D])
            psT = [bank(st, f"s1_psT{b}", HALVES, P) for b in range(2)]
            psO = [bank(st, f"s1_psO{k}", R * P, banks=2) for k in range(HALVES)]
            w_in, x_in = sem("s1_w_in"), [sem(f"s1_x_in{b}") for b in range(2)]
            stats_done, stats_seen, moments, rstd_step, normed = sem("s1_stats"), sem("s1_stats_seen"), sem("s1_moments"), sem("s1_rstd_step"), sem("s1_normed")
            turned, hT_ready = sem("s1_turned"), sem("s1_hT_ready")
            product = [sem(f"s1_product{k}") for k in range(HALVES)]
            evicted = [sem(f"s1_evicted{k}") for k in range(HALVES)]
            stored = [sem(f"s1_stored{b}") for b in range(2)]
            x_tiles = a["x"]
            table_tiles = rel_table.rearrange("(r n) d -> n r d", r=R)

            with nc.Block() as block:
                @block.sync
                def _(sp):
                    sp.dma_start(rel_w[:, :, :], a["rel_w"]).then_inc(w_in, 16)

                    def load(t, i, b):
                        sp.dma_start(xt[:, b, :], x_tiles[ds(t * P, P), :]).then_inc(x_in[b], 16)

                    load(0, 0, 0)
                    load(1, 0, 1)
                    with sp.Fori(0, PAIRS - 1) as i:
                        for b in range(2):
                            sp.wait_ge(normed, 2 * i + b + 1)
                            load(2 * i + b + 2, i + 1, b)

                @block.gpsimd
                def _(pool):
                    def step(t, i, b, left):
                        pool.wait_ge(moments, t + 1)
                        pool.tensor_tensor(ve[:, b, :], mv[:, b, 1:2], eps[:, :], ALU.add).then_inc(rstd_step, 1)
                        pool.wait_ge(rstd_step, 2 * t + 1)
                        pool.tensor_tensor(rstd[:, b, :], ve[:, b, :], neg_half[:, :], ALU.pow).then_inc(rstd_step, 1)

                    by_tiles(pool, step)

                @block.vector
                def _(v):
                    def norm(t, i, b):
                        v.wait_ge(x_in[b], 16 * i + 16)
                        v.bn_stats(stat[:, b, :], xt[:, b, :]).then_inc(stats_done, 1)
                        v.wait_ge(stats_done, t + 1)
                        v.sem_inc(stats_seen, 1)
                        v.bn_aggr(mv[:, b, :], stat[:, b, :]).then_inc(moments, 1)
                        v.wait_ge(rstd_step, 2 * t + 2)
                        v.tensor_scalar(h[:, b, :], xt[:, b, :], mv[:, b, 0:1], rstd[:, b, :],
                                        ALU.subtract, ALU.mult).then_inc(normed, 1)

                    def evict(t, i, b):
                        v.wait_ge(product[0], t + 1)
                        wait_past(v, stored[b], 16 * i)
                        v.tensor_copy(rows[:, b, :, 0:P], psO[0][:, :].rearrange("p (r o) -> p r o", r=R)).then_inc(evicted[0], 1)

                    def step(t, i, b, left):
                        if left:
                            wait_past(v, turned, t)
                            norm(t + 1, i + b, 1 - b)
                        evict(t, i, b)

                    norm(0, 0, 0)
                    by_tiles(v, step)

                @block.scalar
                def _(act):
                    def copy_hT(t, b):
                        act.wait_ge(turned, t + 1)
                        act.activation(hT[:, b, :, :], psT[b][:, :, :], ACT.Copy).then_inc(hT_ready, 1)

                    def step(t, i, b, left):
                        if left:
                            wait_past(act, product[1], t)
                            copy_hT(t + 1, 1 - b)
                        act.wait_ge(product[1], t + 1)
                        wait_past(act, stored[b], 16 * i)
                        act.activation(rows[:, b, :, P:D], psO[1][:, :].rearrange("p (r o) -> p r o", r=R), ACT.Copy).then_inc(evicted[1], 1)
                        act.wait_ge(evicted[0], t + 1)
                        act.wait_ge(evicted[1], t + 1)
                        act.dma_start(table_tiles[ds(t * P, P), :, :], rows[:, b, :, :]).then_inc(stored[b], 16)

                    copy_hT(0, 0)
                    by_tiles(act, step)
                    for b in range(2):
                        act.wait_ge(stored[b], 16 * PAIRS)

                @block.tensor
                def _(pe):
                    def turn(t, b):
                        pe.wait_ge(normed, t + 1)
                        for k in range(HALVES):
                            mm = pe.transpose(psT[b][:, k, :], h[:, b, k * P:(k + 1) * P], ident[:, :])
                        mm.then_inc(turned, 1)

                    def step(t, i, b, left):
                        pe.wait_ge(hT_ready, t + 1)
                        for k in range(HALVES):
                            if left and k == 1:
                                turn(t + 1, 1 - b)
                            wait_past(pe, evicted[k], t)
                            for c in range(R * P // 512):
                                mm = pe.matmul(psO[k][:, c * 512:(c + 1) * 512], hT[:, b, k, :],
                                               rel_w[:, k, c * 512:(c + 1) * 512], start=True, stop=True)
                            mm.then_inc(product[k], 1)

                    pe.wait_ge(w_in, 16)
                    turn(0, 0)
                    by_tiles(pe, step)
        end_stage()

        def aggregate(name, table, sums, index, local, first, scale, per_head):
            with ExitStack() as st:
                rows = at(st, f"{name}_rows", [P, U, D])
                staged = at(st, f"{name}_staged", [P, U], I32)
                pick = at(st, f"{name}_pick", [P, PICKS, WIDE])
                apart = at(st, f"{name}_apart", [P, PICKS, WIDE]) if per_head else None
                scaled = at(st, f"{name}_scaled", [P, PICKS, D]) if per_head else None
                part = [bank(st, f"{name}_part{k}", HALVES, 512, banks=HALVES)[:, :, 0:WIDE] for k in range(SELS)]
                idx_taken, idx_ready, idx_seen = sem(f"{name}_idx_taken"), sem(f"{name}_idx_ready"), sem(f"{name}_idx_seen")
                gathered = [sem(f"{name}_gathered{s}") for s in range(U)]
                rows_scaled = sem(f"{name}_rows_scaled")
                picked, apart_go, apart_done = sem(f"{name}_picked"), sem(f"{name}_apart_go"), sem(f"{name}_apart_done")
                product, added, cleared = sem(f"{name}_product"), sem(f"{name}_added"), sem(f"{name}_cleared")
                rows_used, used_from = (rows_scaled, 0) if per_head else (product, 1)
                GROUPS = U // GRP

                with nc.Block() as block:
                    @block.scalar
                    def _(act):
                        def matrices(n, half, first_pass=False):
                            if not first_pass:
                                act.wait_ge(product, n * GRP - GRP + 1)
                            act.sem_inc(apart_go, 1)
                            for j in range(GRP):
                                act.activation(apart[:, half * GRP + j, :], window[:, :], ACT.Abs,
                                               bias=local[:, ds(n * GRP + j, 1)]).then_inc(apart_done, 1)
                            act.wait_ge(apart_done, n * GRP + GRP)
                            act.activation(pick[:, half * GRP:(half + 1) * GRP, :], apart[:, half * GRP:(half + 1) * GRP, :],
                                           ACT.Relu, bias=ones[:, 0:1], scale=-1.0).then_inc(picked, 1)

                        for g in range(GROUPS):
                            act.activation(staged[:, g * GRP:(g + 1) * GRP], index[:, g * GRP:(g + 1) * GRP],
                                           ACT.Copy).then_inc(idx_ready, 1)
                        if per_head:
                            matrices(0, 0, True)
                            matrices(1, 1, True)
                        with act.Fori(1, ITER) as i:
                            for g in range(GROUPS):
                                for s in range(g * GRP, (g + 1) * GRP):
                                    act.wait_ge(gathered[s], 16 * i)
                                act.sem_inc(idx_taken, 1)
                                act.activation(staged[:, g * GRP:(g + 1) * GRP], index[:, ds(i * U + g * GRP, GRP)],
                                               ACT.Copy).then_inc(idx_ready, 1)
                                if per_head:
                                    matrices(GROUPS * i - GROUPS + g + 2, g % 2)
                        if per_head:
                            for g in range(GROUPS):
                                if GROUPS * (ITER - 1) + g + 2 < GROUPS * ITER:
                                    matrices(GROUPS * (ITER - 1) + g + 2, g % 2)

                    @block.gpsimd
                    def _(pool):
                        def gathers(i, g, first_pass):
                            if not first_pass:
                                pool.wait_ge(rows_used, U * i - U + (g + 1) * GRP + used_from)
                            pool.wait_ge(idx_ready, GROUPS * i + g + 1)
                            pool.sem_inc(idx_seen, 1)
                            for s in range(g * GRP, (g + 1) * GRP):
                                pool.indirect_dma_start(
                                    out=rows[:, s, :], out_offset=None, in_=table[:, :],
                                    in_offset=bass.IndirectOffsetOnAxis(ap=staged[:, s:s + 1], axis=0),
                                ).then_inc(gathered[s], 16)

                        for g in range(GROUPS):
                            gathers(0, g, True)
                        with pool.Fori(1, ITER) as i:
                            for g in range(GROUPS):
                                gathers(i, g, False)

                    @block.tensor
                    def _(pe):
                        pe.sem_inc(product, 1)
                        with pe.Fori(0, ITER) as i:
                            for s in range(U):
                                c = i * U + s
                                if per_head:
                                    pe.wait_ge(rows_scaled, c + 1)
                                    pe.wait_ge(picked, i * GROUPS + s // GRP + 1)
                                else:
                                    pe.wait_ge(gathered[s], 16 * i + 16)
                                    pe.wait_ge(picked, c + 1)
                                if s % SPAN == 0:
                                    pe.wait_ge(added, i * (U // SPAN) + s // SPAN + 1)
                                for k in range(HALVES):
                                    left = scaled[:, s % PICKS, k * P:(k + 1) * P] if per_head else rows[:, s, k * P:(k + 1) * P]
                                    mm = pe.matmul(part[s // SPAN % SELS][:, k, :], left, pick[:, s % PICKS, :],
                                                   start=(s % SPAN == 0), stop=(s % SPAN == SPAN - 1))
                                mm.then_inc(product, 1)

                    @block.vector
                    def _(v):
                        def matrix(c, s):
                            v.tensor_scalar(pick[:, s % PICKS, :], window[:, :], local[:, ds(c, 1)], scale[:, ds(c, 1)],
                                            ALU.is_equal, ALU.mult).then_inc(picked, 1)

                        def scaling(i, s):
                            c = i * U + s
                            v.wait_ge(gathered[s], 16 * i + 16)
                            v.tensor_tensor(scaled[:, s % PICKS, :].rearrange("p (h c) -> p h c", h=HEADS),
                                            rows[:, s, :].rearrange("p (h c) -> p h c", h=HEADS),
                                            scale[:, ds(c, 1), :].rearrange("p o h -> p (o h)").unsqueeze(2).broadcast_to([P, HEADS, CH]),
                                            ALU.mult).then_inc(rows_scaled, 1)

                        def add(d, w, at_node):
                            v.wait_ge(product, d * SPAN + 1)
                            v.wait_ge(added, d + 3)
                            v.tensor_tensor(sums[:, :, ds(at_node, WIDE)], sums[:, :, ds(at_node, WIDE)],
                                            part[(w - 1) % SELS][:, :, :], ALU.add).then_inc(added, 1)

                        v.memset(sums[:, :, :], 0.0).then_inc(cleared, 1)
                        v.memset(part[SELS - 1][:, :, :], 0.0).then_inc(cleared, 1)
                        v.sem_inc(added, 3)
                        if not per_head:
                            matrix(0, 0)
                            matrix(1, 1)
                        v.wait_ge(cleared, 2)
                        with v.Fori(0, ITER) as i:
                            for s in range(0, U, 2 * SPAN):
                                d, w = i * (U // SPAN) + s // SPAN, s // SPAN
                                for j in range(2 * SPAN):
                                    if per_head:
                                        scaling(i, s + j)
                                    else:
                                        matrix(i * U + s + j + 2, (s + j + 2) % U)
                                both = v.value_load(first[0:1, ds(i * (U // SPAN // 2) + w // 2, 1)], min_val=0, max_val=2 ** 31 - 1)
                                for j, at_node in enumerate((both & 0xffff, both >> 16)):
                                    add(d + j, w + j, nc.s_assert_within(at_node, min_val=0, max_val=N,
                                                                         skip_runtime_bounds_check_because="a destination, at most N"))
                        at_node = v.value_load(first[0:1, SPANS // 2:SPANS // 2 + 1], min_val=0, max_val=N)
                        add(SPANS, 0, at_node)

        def pair_up(v, first, alone, done):
            lower, upper = alone[:, 0:SPANS:2], alone[:, 1:SPANS:2]
            v.tensor_scalar(first[:, 0:SPANS // 2], upper, 16, None, ALU.logical_shift_left).then_inc(done, 1)
            v.wait_ge(done, 1)
            v.tensor_tensor(first[:, 0:SPANS // 2], first[:, 0:SPANS // 2], lower, ALU.bitwise_or).then_inc(done, 1)
            v.tensor_copy(first[:, SPANS // 2:SPANS // 2 + 1], alone[:, SPANS:SPANS + 1]).then_inc(done, 1)

        sums_of = ExitStack()
        sums = at(sums_of, "sums", [P, HALVES, ACC])
        with ExitStack() as st:
            first = at(st, "s2_first", [1, SPANS // 2 + 1], I32)
            alone = at(st, "s2_alone", [1, SPANS + 1], I32)
            first_all = at(st, "s2_first_all", [P, SPANS], I32)
            index = at(st, "s2_index", [P, CHUNKS], I32)
            source = at(st, "s2_source", [P, CHUNKS], I32)
            local = at(st, "s2_local", [P, CHUNKS + 2])
            weight = at(st, "s2_weight", [P, CHUNKS + 2])
            ends = at(st, "s2_ends", [P, CHUNKS], I32)
            edges_in, edges_ready = sem("s2_edges_in"), sem("s2_edges_ready")
            with nc.Block() as block:
                @block.sync
                def _(sp):
                    sp.dma_start(alone[:, :], a["dst_first"]).then_inc(edges_in, 16)
                    sp.dma_start(first_all[:, :], a["dst_first"][0:1, 1:SPANS + 1].broadcast_to([P, SPANS])).then_inc(edges_in, 16)
                    sp.dma_start(index[:, :], a["type_chunk"]).then_inc(edges_in, 16)
                    sp.dma_start(source[:, :], a["src_chunk"]).then_inc(edges_in, 16)
                    sp.dma_start(ends[:, :], a["dst_chunk"]).then_inc(edges_in, 16)
                    sp.dma_start(weight[:, 0:CHUNKS], a["weight_chunk"]).then_inc(edges_in, 16)
                    sp.wait_ge(edges_in, 16 * 6)

                @block.vector
                def _(v):
                    v.memset(local[:, CHUNKS:CHUNKS + 2], 0.0)
                    v.memset(weight[:, CHUNKS:CHUNKS + 2], 0.0)
                    v.wait_ge(edges_in, 16 * 6)
                    pair_up(v, first, alone, edges_ready)
                    v.scalar_tensor_tensor(out=index[:, :], in0=index[:, :], scalar=float(NP), in1=source[:, :],
                                           op0=ALU.mult, op1=ALU.add).then_inc(edges_ready, 1)
                    v.tensor_tensor(local[:, 0:CHUNKS].rearrange("p (d j) -> p d j", j=SPAN), ends[:, :].rearrange("p (d j) -> p d j", j=SPAN),
                                    first_all[:, :].unsqueeze(2).broadcast_to([P, SPANS, SPAN]), ALU.subtract).then_inc(edges_ready, 1)
            aggregate("s2", rel_table, sums, index, local, first, weight, False)
        end_stage()

        with ExitStack() as st:
            w1 = at(st, "s3_w1", [P, HALVES, H0])
            w2 = at(st, "s3_w2", [P, H0 // P, D])
            b1 = at(st, "s3_b1", [P, H0 // P])
            b2 = at(st, "s3_b2", [P, D])
            wr = at(st, "s3_wr", [P, D])
            xt = at(st, "s3_x", [P, 2, D])
            fixed = at(st, "s3_fixed", [P, 2, HALVES, P])
            x1 = at(st, "s3_x1", [P, 2, D])
            stat = at(st, "s3_stat", [P, 2, 6])
            mv = at(st, "s3_mv", [P, 2, 2])
            ve = at(st, "s3_ve", [P, 2, 1])
            rstd = at(st, "s3_rstd", [P, 2, 1])
            h = at(st, "s3_h", [P, 2, D])
            skip = at(st, "s3_skip", [P, 2, D])
            y = at(st, "s3_y", [P, 2, D])
            routed = at(st, "s3_routed", [P, 2, D])
            logit = at(st, "s3_logit", [P, 2, 1])
            hT = at(st, "s3_hT", [P, 2, HALVES, P])
            hid = at(st, "s3_hid", [P, 2, H0 // P, P])
            psX = [bank(st, f"s3_psX{b}", D) for b in range(2)]
            psH = bank(st, "s3_psH", HALVES, P)
            psG = [bank(st, f"s3_psG{k}", 4, P) for k in range(2)]
            psY = bank(st, "s3_psY", D)
            w_in, x_in = sem("s3_w_in"), [sem(f"s3_x_in{b}") for b in range(2)]
            held, held_go, unturned, x1_done = sem("s3_held"), sem("s3_held_go"), sem("s3_unturned"), sem("s3_x1_done")
            stats_done, stats_seen, moments, rstd_step = sem("s3_stats"), sem("s3_stats_seen"), sem("s3_moments"), sem("s3_rstd_step")
            normed, skipped, logit_done, logit_go = sem("s3_normed"), sem("s3_skipped"), sem("s3_logit_done"), sem("s3_logit_go")
            turned, hT_ready = sem("s3_turned"), sem("s3_hT_ready")
            up_done, active = [sem(f"s3_up_done{k}") for k in range(2)], [sem(f"s3_active{k}") for k in range(2)]
            down_done, y_done = sem("s3_down_done"), sem("s3_y_done")
            skip_out, y_out = [sem(f"s3_skip_out{b}") for b in range(2)], [sem(f"s3_y_out{b}") for b in range(2)]
            with nc.Block() as block:
                @block.sync
                def _(sp):
                    def load(t, b):
                        sp.dma_start(xt[:, b, :], a["x"][ds(t * P, P), :]).then_inc(x_in[b], 16)

                    def step(t, i, b, left):
                        if left == 2:
                            sp.wait_ge(x1_done, t + 1)
                            load(t + 2, b)
                        sp.wait_ge(skipped, t + 1)
                        sp.dma_start(mid_rows[ds(t * P, P), 0:D], skip[:, b, :]).then_inc(skip_out[b], 16)
                        sp.wait_ge(y_done, t + 1)
                        sp.dma_start(mid_rows[ds(t * P, P), D:2 * D], y[:, b, :]).then_inc(y_out[b], 16)

                    load(0, 0)
                    load(1, 1)
                    sp.dma_start(wr[:, :], a["wr"].broadcast_to([P, D])).then_inc(w_in, 16)
                    sp.dma_start(w1[:, :, :], a["ffn_w1"]).then_inc(w_in, 16)
                    sp.dma_start(b1[:, :], a["ffn_b1"]).then_inc(w_in, 16)
                    sp.dma_start(w2[:, :, :], a["ffn_w2"]).then_inc(w_in, 16)
                    sp.dma_start(b2[:, :], a["ffn_b2"].broadcast_to([P, D])).then_inc(w_in, 16)
                    by_tiles(sp, step)
                    for b in range(2):
                        sp.wait_ge(skip_out[b], 16 * PAIRS)
                        sp.wait_ge(y_out[b], 16 * PAIRS)

                @block.gpsimd
                def _(pool):
                    def step(t, i, b, left):
                        pool.wait_ge(moments, t + 1)
                        pool.tensor_tensor(ve[:, b, :], mv[:, b, 1:2], eps[:, :], ALU.add).then_inc(rstd_step, 1)
                        pool.wait_ge(rstd_step, 2 * t + 1)
                        pool.tensor_tensor(rstd[:, b, :], ve[:, b, :], neg_half[:, :], ALU.pow).then_inc(rstd_step, 1)

                    by_tiles(pool, step)

                @block.scalar
                def _(act):
                    def hold(t, b):
                        act.sem_inc(held_go, 1)
                        act.activation(fixed[:, b, :, :], sums[:, :, ds(t * P, P)], ACT.Copy).then_inc(held, 1)

                    def copy_hT(t, b):
                        act.wait_ge(turned, t + 1)
                        act.activation(hT[:, b, :, :], psH, ACT.Copy).then_inc(hT_ready, 1)
                        act.wait_ge(logit_done, t + 1)
                        act.sem_inc(logit_go, 1)
                        act.activation(logits[:, ds(t, 1)], logit[:, b, :], ACT.Copy)

                    def step(t, i, b, left):
                        if left == 2:
                            act.wait_ge(unturned, t + 1)
                            hold(t + 2, b)
                        for k in range(2):
                            act.wait_ge(up_done[k], t + 1)
                            for c in range(4):
                                g = act.activation(hid[:, b, 4 * k + c, :], psG[k][:, c, :], ACT.Gelu_apprx_tanh,
                                                   bias=b1[:, 4 * k + c:4 * k + c + 1])
                            g.then_inc(active[k], 1)
                        if left:
                            copy_hT(t + 1, 1 - b)

                    hold(0, 0)
                    hold(1, 1)
                    act.wait_ge(w_in, 16 * 5)
                    copy_hT(0, 0)
                    by_tiles(act, step)

                @block.tensor
                def _(pe):
                    def unturn(t, b):
                        pe.wait_ge(held, t + 1)
                        for k in range(HALVES):
                            mm = pe.transpose(psX[b][:, k * P:(k + 1) * P], fixed[:, b, k, :], ident[:, :])
                        mm.then_inc(unturned, 1)

                    def turn(t, b):
                        pe.wait_ge(normed, t + 1)
                        for k in range(HALVES):
                            mm = pe.transpose(psH[:, k, :], h[:, b, k * P:(k + 1) * P], ident[:, :])
                        mm.then_inc(turned, 1)

                    def step(t, i, b, left):
                        if left == 2:
                            pe.wait_ge(x1_done, t + 1)
                            unturn(t + 2, b)
                        pe.wait_ge(hT_ready, t + 1)
                        for k in range(2):
                            wait_past(pe, active[k], t)
                            for c in range(4):
                                for half in range(HALVES):
                                    mm = pe.matmul(psG[k][:, c, :], w1[:, half, (4 * k + c) * P:(4 * k + c + 1) * P],
                                                   hT[:, b, half, :], start=(half == 0), stop=(half == HALVES - 1))
                            mm.then_inc(up_done[k], 1)
                        if left:
                            turn(t + 1, 1 - b)
                        wait_past(pe, y_done, t)
                        for k in range(2):
                            pe.wait_ge(active[k], t + 1)
                            for c in range(4 * k, 4 * k + 4):
                                mm = pe.matmul(psY, hid[:, b, c, :], w2[:, c, :], start=(c == 0), stop=(c == H0 // P - 1))
                        mm.then_inc(down_done, 1)

                    unturn(0, 0)
                    unturn(1, 1)
                    pe.wait_ge(w_in, 16 * 5)
                    turn(0, 0)
                    by_tiles(pe, step)

                @block.vector
                def _(v):
                    def front(t, i, b):
                        v.wait_ge(x_in[b], 16 * i + 16)
                        wait_past(v, skip_out[b], 16 * i)
                        v.wait_ge(unturned, t + 1)
                        v.tensor_tensor(x1[:, b, :], psX[b], xt[:, b, :], ALU.add).then_inc(x1_done, 1)
                        v.wait_ge(x1_done, t + 1)
                        v.bn_stats(stat[:, b, :], x1[:, b, :]).then_inc(stats_done, 1)
                        v.wait_ge(stats_done, t + 1)
                        v.sem_inc(stats_seen, 1)
                        v.bn_aggr(mv[:, b, :], stat[:, b, :]).then_inc(moments, 1)
                        v.wait_ge(rstd_step, 2 * t + 2)
                        v.tensor_scalar(h[:, b, :], x1[:, b, :], mv[:, b, 0:1], rstd[:, b, :],
                                        ALU.subtract, ALU.mult).then_inc(normed, 1)
                        v.wait_ge(normed, t + 1)
                        v.tensor_tensor(skip[:, b, :], x1[:, b, :], h[:, b, :], ALU.add).then_inc(skipped, 1)
                        v.tensor_tensor_reduce(routed[:, b, :], h[:, b, :], wr[:, :], 1.0, 0.0, ALU.mult, ALU.add,
                                               logit[:, b, :]).then_inc(logit_done, 1)

                    def step(t, i, b, left):
                        if left:
                            front(t + 1, i + b, 1 - b)
                        v.wait_ge(down_done, t + 1)
                        wait_past(v, y_out[b], 16 * i)
                        v.tensor_tensor(y[:, b, :], psY, b2[:, :], ALU.add).then_inc(y_done, 1)

                    v.wait_ge(w_in, 16 * 5)
                    front(0, 0, 0)
                    by_tiles(v, step)
        sums_of.close()
        end_stage()

        with ExitStack() as st:
            br = at(st, "s4_br", [P, 1])
            upto = at(st, "s4_upto", [P, P])
            prefix = at(st, "s4_prefix", [P, 1], I32)
            bit = at(st, "s4_bit", [P, 1], I32)
            cand = at(st, "s4_cand", [P, 1], I32)
            flip = at(st, "s4_flip", [P, 1], I32)
            value = at(st, "s4_value", [P, 1], I32)
            taken = at(st, "s4_taken", [P, 1], I32)
            over = at(st, "s4_over", [P, NT])
            same = at(st, "s4_same", [P, NT])
            count = at(st, "s4_count", [P, 1])
            left_over = at(st, "s4_left_over", [P, 1])
            before = at(st, "s4_before", [P, NT])
            rank = at(st, "s4_rank", [P, NT])
            zeros = at(st, "s4_zeros", [P, NT])
            psC = bank(st, "s4_psC", 1)
            psU = bank(st, "s4_psU", NT)
            psA = bank(st, "s4_psA", NT)
            br_in, tri, biased, padded = sem("s4_br_in"), sem("s4_tri"), sem("s4_biased"), sem("s4_padded")
            done, counted, total = sem("s4_done"), sem("s4_counted"), sem("s4_total")
            OPS = 9
            with nc.Block() as block:
                @block.sync
                def _(sp):
                    sp.dma_start(br[:, :], a["br"].broadcast_to([P, 1])).then_inc(br_in, 16)
                    sp.wait_ge(br_in, 16)

                @block.gpsimd
                def _(pool):
                    pool.affine_select(out=upto[:, :], in_=ones[:, :], compare_op=ALU.is_ge, fill=0.0,
                                       base=0, pattern=[[1, P]], channel_multiplier=-1).then_inc(tri, 1)
                    pool.wait_ge(biased, 1)
                    pool.affine_select(out=logits[:, :], in_=logits[:, :], compare_op=ALU.is_ge, fill=-3.4e38,
                                       base=N - 1, pattern=[[-P, NT]], channel_multiplier=-1).then_inc(padded, 1)

                @block.tensor
                def _(pe):
                    with pe.Fori(0, 33) as i:
                        pe.wait_ge(counted, i + 1)
                        pe.matmul(psC, ones[:, :], count[:, :], start=True, stop=True).then_inc(total, 1)
                    pe.wait_ge(counted, 34)
                    pe.wait_ge(tri, 1)
                    pe.matmul(psU, upto[:, :], same[:, :], start=True, stop=True)
                    pe.matmul(psA, ones[:, :], same[:, :], start=True, stop=True).then_inc(total, 1)

                @block.vector
                def _(v):
                    v.wait_ge(br_in, 16)
                    v.tensor_scalar(logits[:, :], logits[:, :], br[:, :], None, ALU.add).then_inc(biased, 1)
                    v.memset(zeros[:, :], 0.0)
                    v.memset(prefix[:, :], 0).then_inc(done, 1)
                    v.memset(bit[:, :], -2 ** 31).then_inc(done, 1)
                    v.wait_ge(padded, 1)

                    def as_value(k):
                        v.wait_ge(done, k)
                        v.tensor_scalar(flip[:, :], cand[:, :], 31, -1, ALU.arith_shift_right, ALU.bitwise_xor).then_inc(done, 1)
                        v.wait_ge(done, k + 1)
                        v.scalar_tensor_tensor(out=value[:, :], in0=flip[:, :], scalar=-2 ** 31, in1=cand[:, :],
                                               op0=ALU.bitwise_or, op1=ALU.bitwise_xor).then_inc(done, 1)

                    with v.Fori(0, 32) as i:
                        k = i * (OPS - 1) + 2
                        v.wait_ge(done, k)
                        v.tensor_tensor(cand[:, :], prefix[:, :], bit[:, :], ALU.bitwise_or).then_inc(done, 1)
                        as_value(k + 1)
                        v.wait_ge(done, k + 3)
                        v.tensor_scalar(over[:, :], logits[:, :], value[:, :].bitcast(F32), None, ALU.is_ge).then_inc(done, 1)
                        v.wait_ge(done, k + 4)
                        v.tensor_reduce(count[:, :], over[:, :], AX.X, ALU.add).then_inc(counted, 1)
                        v.wait_ge(total, i + 1)
                        v.tensor_scalar(taken[:, :], psC, float(KEEP), -1.0, ALU.is_ge, ALU.mult).then_inc(done, 1)
                        v.wait_ge(done, k + 5)
                        v.tensor_tensor(taken[:, :], taken[:, :], bit[:, :], ALU.bitwise_and).then_inc(done, 1)
                        v.wait_ge(done, k + 6)
                        v.tensor_tensor(prefix[:, :], prefix[:, :], taken[:, :], ALU.bitwise_or).then_inc(done, 1)
                        v.tensor_scalar(bit[:, :], bit[:, :], 1, None, ALU.logical_shift_right).then_inc(done, 1)
                    k = 32 * (OPS - 1) + 2
                    v.wait_ge(done, k)
                    v.tensor_copy(cand[:, :], prefix[:, :]).then_inc(done, 1)
                    as_value(k + 1)
                    v.wait_ge(done, k + 3)
                    threshold = value[:, :].bitcast(F32)
                    v.tensor_scalar(over[:, :], logits[:, :], threshold, None, ALU.is_gt).then_inc(done, 1)
                    v.wait_ge(done, k + 4)
                    v.tensor_reduce(count[:, :], over[:, :], AX.X, ALU.add).then_inc(counted, 1)
                    v.tensor_scalar(same[:, :], logits[:, :], threshold, None, ALU.is_equal).then_inc(counted, 1)
                    v.wait_ge(total, 33)
                    v.tensor_scalar(left_over[:, :], psC, -1.0, float(KEEP), ALU.mult, ALU.add).then_inc(done, 1)
                    v.wait_ge(total, 34)
                    v.tensor_tensor_scan(before[:, :], psA, zeros[:, :], 0.0, ALU.add, ALU.add).then_inc(done, 1)
                    v.wait_ge(done, k + 6)
                    v.tensor_tensor(rank[:, :], before[:, :], psA, ALU.subtract).then_inc(done, 1)
                    v.wait_ge(done, k + 7)
                    v.tensor_tensor(rank[:, :], rank[:, :], psU, ALU.add).then_inc(done, 1)
                    v.wait_ge(done, k + 8)
                    v.scalar_tensor_tensor(out=same[:, :], in0=rank[:, :], scalar=left_over[:, :], in1=same[:, :],
                                           op0=ALU.is_le, op1=ALU.mult).then_inc(done, 1)
                    v.wait_ge(done, k + 9)
                    v.tensor_tensor(over[:, :], over[:, :], same[:, :], ALU.add).then_inc(done, 1)
                    v.wait_ge(done, k + 10)
                    v.tensor_tensor(logits[:, :], logits[:, :], over[:, :], ALU.mult).then_inc(done, 1)
        end_stage()

        with ExitStack() as st:
            EXT = D + 2 * HEADS
            wp = at(st, "s5_wp", [P, HALVES, EXT])
            att = at(st, "s5_att", [P, 2, D])
            terms = at(st, "s5_terms", [P, HALVES, 2, D])
            mid = at(st, "s5_mid", [P, 2, 2 * D])
            x2 = at(st, "s5_x2", [P, 2, D])
            stat = at(st, "s5_stat", [P, 2, 6])
            mv = at(st, "s5_mv", [P, 2, 2])
            ve = at(st, "s5_ve", [P, 2, 1])
            rstd = at(st, "s5_rstd", [P, 2, 1])
            h = at(st, "s5_h", [P, 2, D])
            hT = at(st, "s5_hT", [P, 2, HALVES, P])
            xp = at(st, "s5_xp", [P, 2, D])
            head_logits = at(st, "s5_head_logits", [P, NT, 2 * HEADS])
            psH = [bank(st, f"s5_psH{b}", HALVES, P) for b in range(2)]
            psP = [bank(st, f"s5_psP{b}", EXT) for b in range(2)]
            w_in, w_done, mid_in = sem("s5_w_in"), sem("s5_w_done"), [sem(f"s5_mid_in{b}") for b in range(2)]
            x2_done, stats_done, stats_seen, moments, rstd_step = sem("s5_x2_done"), sem("s5_stats"), sem("s5_stats_seen"), sem("s5_moments"), sem("s5_rstd_step")
            normed, turned, hT_ready, product = sem("s5_normed"), sem("s5_turned"), sem("s5_hT_ready"), sem("s5_product")
            xp_done, logits_go, logits_done, logits_out = sem("s5_xp_done"), sem("s5_logits_go"), sem("s5_logits_done"), sem("s5_logits_out")
            x2_out, xp_out = ([sem(f"s5_{n}_out{b}") for b in range(2)] for n in ("x2", "xp"))
            with nc.Block() as block:
                @block.sync
                def _(sp):
                    def load(t, b):
                        sp.dma_start(mid[:, b, :], mid_rows[ds(t * P, P), :]).then_inc(mid_in[b], 16)

                    def step(t, i, b, left):
                        sp.wait_ge(x2_done, t + 1)
                        if left == 2:
                            load(t + 2, b)
                        sp.dma_start(x2_rows[ds(t * P, P), :], x2[:, b, :]).then_inc(x2_out[b], 16)

                    load(0, 0)
                    load(1, 1)
                    sp.dma_start(wp[:, :, 0:D], a["att_w"]).then_inc(w_in, 16)
                    sp.dma_start(att[:, :, :], a["att"].broadcast_to([P, 2 * D]).rearrange("p (s c) -> p s c", s=2)).then_inc(w_in, 16)
                    by_tiles(sp, step)
                    sp.wait_ge(logits_done, NT)
                    sp.dma_start(logit_table.rearrange("(p t) c -> p t c", p=P), head_logits[:, :, :]).then_inc(logits_out, 16)
                    sp.wait_ge(logits_out, 16)
                    for b in range(2):
                        sp.wait_ge(x2_out[b], 16 * PAIRS)

                @block.gpsimd
                def _(pool):
                    def step(t, i, b, left):
                        pool.wait_ge(moments, t + 1)
                        pool.tensor_tensor(ve[:, b, :], mv[:, b, 1:2], eps[:, :], ALU.add).then_inc(rstd_step, 1)
                        pool.wait_ge(rstd_step, 2 * t + 1)
                        pool.tensor_tensor(rstd[:, b, :], ve[:, b, :], neg_half[:, :], ALU.pow).then_inc(rstd_step, 1)

                    by_tiles(pool, step)

                @block.scalar
                def _(act):
                    def copy_hT(t, b):
                        act.wait_ge(turned, t + 1)
                        act.activation(hT[:, b, :, :], psH[b], ACT.Copy).then_inc(hT_ready, 1)

                    def step(t, i, b, left):
                        if left:
                            copy_hT(t + 1, 1 - b)
                        act.wait_ge(product, t + 1)
                        wait_past(act, xp_out[b], 16 * i)
                        act.activation(xp[:, b, :], psP[b][:, 0:D], ACT.Copy).then_inc(xp_done, 1)
                        act.sem_inc(logits_go, 1)
                        act.activation(head_logits[:, ds(t, 1), :].rearrange("p o c -> p (o c)"), psP[b][:, D:EXT], ACT.Copy).then_inc(logits_done, 1)
                        act.wait_ge(xp_done, t + 1)
                        act.dma_start(xp_table[ds(t * P, P), :], xp[:, b, :]).then_inc(xp_out[b], 16)

                    copy_hT(0, 0)
                    by_tiles(act, step)
                    for b in range(2):
                        act.wait_ge(xp_out[b], 16 * PAIRS)

                @block.tensor
                def _(pe):
                    def turn(t, b):
                        pe.wait_ge(normed, t + 1)
                        for k in range(HALVES):
                            mm = pe.transpose(psH[b][:, k, :], h[:, b, k * P:(k + 1) * P], ident[:, :])
                        mm.then_inc(turned, 1)

                    def step(t, i, b, left):
                        if left:
                            turn(t + 1, 1 - b)
                        pe.wait_ge(hT_ready, t + 1)
                        wait_past(pe, logits_done, t)
                        for k in range(HALVES):
                            mm = pe.matmul(psP[b], hT[:, b, k, :], wp[:, k, :], start=(k == 0), stop=(k == HALVES - 1))
                        mm.then_inc(product, 1)

                    pe.wait_ge(w_done, 2)
                    turn(0, 0)
                    by_tiles(pe, step)

                @block.vector
                def _(v):
                    def mix(t, i, b):
                        v.wait_ge(mid_in[b], 16 * i + 16)
                        wait_past(v, x2_out[b], 16 * i)
                        v.scalar_tensor_tensor(out=x2[:, b, :], in0=mid[:, b, D:2 * D], scalar=logits[:, ds(t, 1)], in1=mid[:, b, 0:D],
                                               op0=ALU.mult, op1=ALU.add).then_inc(x2_done, 1)

                    def moment(t, b):
                        v.wait_ge(x2_done, t + 1)
                        v.bn_stats(stat[:, b, :], x2[:, b, :]).then_inc(stats_done, 1)
                        v.wait_ge(stats_done, t + 1)
                        v.sem_inc(stats_seen, 1)
                        v.bn_aggr(mv[:, b, :], stat[:, b, :]).then_inc(moments, 1)

                    def step(t, i, b, left):
                        if left:
                            mix(t + 1, i + b, 1 - b)
                        v.wait_ge(rstd_step, 2 * t + 2)
                        wait_past(v, turned, t - 1)
                        v.tensor_scalar(h[:, b, :], x2[:, b, :], mv[:, b, 0:1], rstd[:, b, :],
                                        ALU.subtract, ALU.mult).then_inc(normed, 1)
                        if left:
                            moment(t + 1, 1 - b)

                    mix(0, 0, 0)
                    moment(0, 0)
                    v.wait_ge(w_in, 32)
                    v.tensor_tensor(terms[:, :, :, :], wp[:, :, 0:D].unsqueeze(2).broadcast_to([P, HALVES, 2, D]),
                                    att[:, :, :].unsqueeze(1).broadcast_to([P, HALVES, 2, D]), ALU.mult).then_inc(w_done, 1)
                    v.wait_ge(w_done, 1)
                    v.tensor_reduce(wp[:, :, D:EXT], terms[:, :, :, :].rearrange("p k s (h c) -> p k (s h) c", h=HEADS),
                                    AX.X, ALU.add).then_inc(w_done, 1)
                    by_tiles(v, step)

        end_stage()

        chans = ExitStack()
        CHANS = 2 * HEADS + 1 + HEADS
        share = at(chans, "share", [P, CHUNKS, HEADS])
        chan = at(chans, "chan", [P, CHANS, ROW])
        SRC, DST, LOOP, TOP = 0, HEADS, 2 * HEADS, 2 * HEADS + 1
        source = at(chans, "s6_source", [P, ROW], I32)
        with ExitStack() as st:
            staged = at(st, "s6_staged", [P, U], I32)
            place = at(st, "s6_place", [P, ROW], I32)
            tile = at(st, "s6_tile", [P, ROW], I32)
            got = at(st, "s6_got", [P, U, 2 * HEADS])
            src_in, place_step = sem("s6_src_in"), sem("s6_place_step")
            idx_taken, idx_ready, idx_seen, keep_go, kept = sem("s6_idx_taken"), sem("s6_idx_ready"), sem("s6_idx_seen"), sem("s6_keep_go"), sem("s6_kept")
            gathered = [sem(f"s6_gathered{s}") for s in range(U)]
            with nc.Block() as block:
                @block.sync
                def _(sp):
                    sp.dma_start(source[:, :], a["src_row"]).then_inc(src_in, 16)
                    sp.wait_ge(src_in, 16)

                @block.vector
                def _(v):
                    v.wait_ge(src_in, 16)
                    v.tensor_scalar(tile[:, :], source[:, :], P.bit_length() - 1, None, ALU.logical_shift_right).then_inc(place_step, 1)
                    v.tensor_scalar(place[:, :], source[:, :], P - 1, None, ALU.bitwise_and).then_inc(place_step, 1)
                    v.wait_ge(place_step, 2)
                    v.scalar_tensor_tensor(out=place[:, :], in0=place[:, :], scalar=float(NT), in1=tile[:, :],
                                           op0=ALU.mult, op1=ALU.add).then_inc(place_step, 1)

                @block.scalar
                def _(act):
                    act.wait_ge(place_step, 3)
                    for g in range(U // GRP):
                        act.activation(staged[:, g * GRP:(g + 1) * GRP], place[:, g * GRP:(g + 1) * GRP], ACT.Copy).then_inc(idx_ready, 1)

                    def keep(i, g):
                        for s in range(g * GRP, (g + 1) * GRP):
                            act.wait_ge(gathered[s], 16 * i + 16)
                        act.sem_inc(keep_go, 1)
                        act.activation(chan[:, SRC:SRC + 2 * HEADS, ds(i * U + g * GRP, GRP)].rearrange("p c s -> p s c"),
                                       got[:, g * GRP:(g + 1) * GRP, :], ACT.Copy).then_inc(kept, 1)

                    with act.Fori(0, ITER - 1) as i:
                        for g in range(U // GRP):
                            keep(i, g)
                            act.sem_inc(idx_taken, 1)
                            act.activation(staged[:, g * GRP:(g + 1) * GRP], place[:, ds(i * U + U + g * GRP, GRP)],
                                           ACT.Copy).then_inc(idx_ready, 1)
                    for g in range(U // GRP):
                        keep(ITER - 1, g)

                @block.gpsimd
                def _(pool):
                    def gathers(i, g, first_pass):
                        if not first_pass:
                            pool.wait_ge(kept, U // GRP * i - U // GRP + g + 1)
                        pool.wait_ge(idx_ready, U // GRP * i + g + 1)
                        pool.sem_inc(idx_seen, 1)
                        for s in range(g * GRP, (g + 1) * GRP):
                            pool.indirect_dma_start(
                                out=got[:, s, :], out_offset=None, in_=logit_table[:, :],
                                in_offset=bass.IndirectOffsetOnAxis(ap=staged[:, s:s + 1], axis=0),
                            ).then_inc(gathered[s], 16)

                    for g in range(U // GRP):
                        gathers(0, g, True)
                    with pool.Fori(1, ITER) as i:
                        for g in range(U // GRP):
                            gathers(i, g, False)

        end_stage()

        with ExitStack() as st:
            ends = at(st, "s7_ends", [P, ROW], I32)
            before = at(st, "s7_before", [P, ROW], I32)
            after = at(st, "s7_after", [P, ROW], I32)
            edge_i = at(st, "s7_edge_i", [P, ROW], I32)
            goes_on = at(st, "s7_goes_on", [P, ROW])
            more = at(st, "s7_more", [P, ROW])
            cut = at(st, "s7_cut", [P, ROW])
            last = at(st, "s7_last", [P, ROW])
            loop = at(st, "s7_loop", [P, ROW])
            spare = at(st, "s7_spare", [P, ROW])
            MAXES = HEADS + 1 + HEADS
            whole = at(st, "s7_whole", [P, 2])
            border = at(st, "s7_border", [P, 2, MAXES])
            rowwise = at(st, "s7_rowwise", [MAXES, 2, P])
            carry = at(st, "s7_carry", [MAXES, P + 1])
            start = at(st, "s7_start", [P, MAXES])
            psB = [bank(st, f"s7_psB{k}", P) for k in range(2)]
            psS = bank(st, "s7_psS", MAXES)
            psW = [bank(st, f"s7_psW{k}", P) for k in range(2)]
            ends_in, edge_made, share_out = sem("s7_ends_in"), sem("s7_edge_made"), sem("s7_share_out")
            step_done = sem("s7_step_done")
            border_ready, border_turned, carry_ready, carry_turned = sem("s7_border_ready"), sem("s7_border_turned"), sem("s7_carry_ready"), sem("s7_carry_turned")
            scores_ready, exp_done, shares_ready, share_turned, share_kept = sem("s7_scores_ready"), sem("s7_exp_done"), sem("s7_shares_ready"), sem("s7_share_turned"), sem("s7_share_kept")
            TURNS = (MAXES, MAXES, HEADS, HEADS)
            with nc.Block() as block:
                @block.sync
                def _(sp):
                    sp.dma_start(ends[:, :], a["dst_row"]).then_inc(ends_in, 16)
                    sp.dma_start(before[:, :], a["dst_before"]).then_inc(ends_in, 16)
                    sp.dma_start(after[:, :], a["dst_after"]).then_inc(ends_in, 16)
                    sp.wait_ge(share_kept, KR * HEADS)
                    sp.dma_start(share_rows, share[:, :, :]).then_inc(share_out, 16)
                    sp.wait_ge(share_out, 16)

                @block.gpsimd
                def _(pool):
                    pool.iota(edge_i[:, :], pattern=[[1, ROW]], base=0, channel_multiplier=ROW).then_inc(edge_made, 1)

                @block.scalar
                def _(act):
                    act.wait_ge(scores_ready, 1)
                    act.activation(chan[:, TOP:TOP + HEADS, :], chan[:, SRC:SRC + HEADS, :], ACT.Exp).then_inc(exp_done, 1)

                @block.tensor
                def _(pe):
                    for e, n in enumerate(TURNS):
                        pe.wait_ge(border_ready, e + 1)
                        for k in range(2):
                            mm = pe.transpose(psB[k][0:n, :], border[:, k, 0:n], ident[:, :])
                        mm.then_inc(border_turned, 1)
                        pe.wait_ge(carry_ready, e + 1)
                        shift = e % 2
                        pe.transpose(psS[:, 0:n], carry[0:n, shift:shift + P], ident[0:n, 0:n]).then_inc(carry_turned, 1)
                    pe.wait_ge(shares_ready, 1)
                    for j in range(KR * HEADS):
                        k, hd = j // HEADS, j % HEADS
                        if j >= 2:
                            pe.wait_ge(share_kept, j - 1)
                        pe.transpose(psW[j % 2], chan[:, TOP + hd, k * P:(k + 1) * P], ident[:, :]).then_inc(share_turned, 1)

                @block.vector
                def _(v):
                    count = [0]

                    def then(ins):
                        count[0] += 1
                        ins.then_inc(step_done, 1)
                        v.wait_ge(step_done, count[0])

                    def exchange(e, values, largest):
                        n, back = TURNS[e], e % 2
                        order = slice(None, None, -1 if back else 1)
                        then(v.tensor_copy(border[:, 1, 0:n], whole[:, back:back + 1].broadcast_to([P, n])))
                        v.tensor_copy(border[:, 0, 0:n], values).then_inc(border_ready, 1)
                        v.wait_ge(border_turned, e + 1)
                        then(v.tensor_copy(rowwise[0:n, 0, :], psB[0][0:n, :]))
                        if largest:
                            then(v.tensor_scalar(rowwise[0:n, 1, :], psB[1][0:n, :], 1.0, BIG, ALU.subtract, ALU.mult))
                        else:
                            then(v.tensor_copy(rowwise[0:n, 1, :], psB[1][0:n, :]))
                        none = -BIG if largest else 0.0
                        outside = slice(P, P + 1) if back else slice(0, 1)
                        inside = slice(0, P) if back else slice(1, P + 1)
                        then(v.memset(carry[0:n, outside], none))
                        v.tensor_tensor_scan(carry[0:n, inside][:, order], rowwise[0:n, 1, order], rowwise[0:n, 0, order], none,
                                             ALU.add if largest else ALU.mult, ALU.max if largest else ALU.add).then_inc(carry_ready, 1)
                        v.wait_ge(carry_turned, e + 1)
                        then(v.tensor_copy(start[:, 0:n], psS[:, 0:n]))

                    def to_all(e, c0, n):
                        each = chan[:, c0:c0 + n, :]
                        then(v.tensor_tensor(each, each, last[:, :].unsqueeze(1).broadcast_to([P, n, ROW]), ALU.mult))
                        for c in range(n):
                            then(v.tensor_tensor_scan(spare[:, ::-1], more[:, ::-1], chan[:, c0 + c, ::-1], 0.0, ALU.mult, ALU.add))
                            then(v.tensor_copy(border[:, 0, c:c + 1], spare[:, 0:1]))
                        exchange(e, border[:, 0, 0:n], False)
                        for c in range(n):
                            then(v.tensor_tensor_scan(chan[:, c0 + c, ::-1], more[:, ::-1], chan[:, c0 + c, ::-1], start[:, c:c + 1], ALU.mult, ALU.add))

                    v.wait_ge(ends_in, 48)
                    v.wait_ge(edge_made, 1)
                    then(v.tensor_tensor(goes_on[:, :], ends[:, :], before[:, :], ALU.is_equal))
                    then(v.tensor_tensor(more[:, :], ends[:, :], after[:, :], ALU.is_equal))
                    then(v.tensor_tensor(loop[:, :], source[:, :], ends[:, :], ALU.is_equal))
                    then(v.tensor_reduce(whole[:, 0:1], goes_on[:, :], AX.X, ALU.min))
                    then(v.tensor_reduce(whole[:, 1:2], more[:, :], AX.X, ALU.min))
                    then(v.tensor_scalar(cut[:, :], goes_on[:, :], 1.0, BIG, ALU.subtract, ALU.mult))
                    then(v.tensor_scalar(last[:, :], more[:, :], -1.0, 1.0, ALU.mult, ALU.add))

                    def loops(c0, n):
                        return loop[:, :].unsqueeze(1).broadcast_to([P, n, ROW])

                    then(v.tensor_scalar(spare[:, :], loop[:, :], 1.0, BIG, ALU.subtract, ALU.mult))
                    each = chan[:, DST:DST + HEADS, :]
                    then(v.tensor_tensor(each, each, loops(DST, HEADS), ALU.mult))
                    then(v.tensor_tensor(each, each, spare[:, :].unsqueeze(1).broadcast_to([P, HEADS, ROW]), ALU.add))

                    def loop_place(to):
                        then(v.tensor_tensor(to, edge_i[:, :], loop[:, :], ALU.mult))
                        then(v.tensor_tensor(to, spare[:, :], to, ALU.subtract))

                    loop_place(chan[:, LOOP, :])
                    for c in range(HEADS):
                        then(v.tensor_tensor_scan(chan[:, TOP + c, :], cut[:, :], chan[:, SRC + c, :], -BIG, ALU.add, ALU.max))
                    for c in range(HEADS + 1):
                        then(v.tensor_tensor_scan(chan[:, DST + c, :], cut[:, :], chan[:, DST + c, :], -BIG, ALU.add, ALU.max))
                    exchange(0, chan[:, DST:DST + MAXES, ROW - 1:ROW].rearrange("p c o -> p (c o)"), True)
                    for c in range(MAXES):
                        then(v.tensor_tensor_scan(chan[:, DST + c, :], cut[:, :], chan[:, DST + c, :], start[:, c:c + 1], ALU.add, ALU.max))
                    to_all(1, DST, MAXES)
                    scores, dst_logits, tops = (chan[:, c:c + HEADS, :] for c in (SRC, DST, TOP))
                    for each in (scores, tops):
                        then(v.tensor_tensor(each, each, dst_logits, ALU.add))
                        for c in range(HEADS):
                            one = each[:, c, :]
                            then(v.scalar_tensor_tensor(out=one, in0=one, scalar=0.2, in1=one, op0=ALU.mult, op1=ALU.max))
                    v.tensor_tensor(scores, scores, tops, ALU.subtract).then_inc(scores_ready, 1)
                    v.wait_ge(scores_ready, 1)
                    then(v.tensor_scalar(spare[:, :], loop[:, :], 1.0, BIG, ALU.subtract, ALU.mult))
                    loop_place(cut[:, :])
                    then(v.tensor_tensor(cut[:, :], cut[:, :], chan[:, LOOP, :], ALU.is_equal))
                    then(v.tensor_tensor(cut[:, :], cut[:, :], loop[:, :], ALU.mult))
                    then(v.tensor_scalar(cut[:, :], cut[:, :], 1.0, None, ALU.add))
                    v.wait_ge(exp_done, 1)
                    then(v.tensor_tensor(tops, tops, cut[:, :].unsqueeze(1).broadcast_to([P, HEADS, ROW]), ALU.mult))
                    for c in range(HEADS):
                        then(v.tensor_tensor_scan(chan[:, DST + c, :], goes_on[:, :], chan[:, TOP + c, :], 0.0, ALU.mult, ALU.add))
                    exchange(2, chan[:, DST:DST + HEADS, ROW - 1:ROW].rearrange("p c o -> p (c o)"), False)
                    for c in range(HEADS):
                        then(v.tensor_tensor_scan(chan[:, DST + c, :], goes_on[:, :], chan[:, TOP + c, :], start[:, c:c + 1], ALU.mult, ALU.add))
                    to_all(3, DST, HEADS)
                    then(v.reciprocal(dst_logits, dst_logits))
                    v.tensor_tensor(tops, tops, dst_logits, ALU.mult).then_inc(shares_ready, 1)
                    by_chunk = share[:, :, :].rearrange("q (p k) h -> q p k h", k=KR)
                    for j in range(KR * HEADS):
                        k, hd = j // HEADS, j % HEADS
                        v.wait_ge(share_turned, j + 1)
                        v.tensor_copy(by_chunk[:, :, k, hd], psW[j % 2]).then_inc(share_kept, 1)
        chans.close()
        end_stage()

        sums = at(ctx, "sums8", [P, HALVES, ACC])
        with ExitStack() as st:
            share = at(st, "s8_share", [P, CHUNKS, HEADS])
            first = at(st, "s8_first", [1, SPANS // 2 + 1], I32)
            alone = at(st, "s8_alone", [1, SPANS + 1], I32)
            first_all = at(st, "s8_first_all", [P, SPANS], I32)
            index = at(st, "s8_index", [P, CHUNKS], I32)
            local = at(st, "s8_local", [P, CHUNKS])
            ends = at(st, "s8_ends", [P, CHUNKS], I32)
            edges_in, edges_ready = sem("s8_edges_in"), sem("s8_edges_ready")
            with nc.Block() as block:
                @block.sync
                def _(sp):
                    sp.dma_start(alone[:, :], a["dst_first"]).then_inc(edges_in, 16)
                    sp.dma_start(first_all[:, :], a["dst_first"][0:1, 1:SPANS + 1].broadcast_to([P, SPANS])).then_inc(edges_in, 16)
                    sp.dma_start(index[:, :], a["src_chunk"]).then_inc(edges_in, 16)
                    sp.dma_start(ends[:, :], a["dst_chunk"]).then_inc(edges_in, 16)
                    sp.dma_start(share[:, :, :], share_rows).then_inc(edges_in, 16)
                    sp.wait_ge(edges_in, 16 * 5)

                @block.vector
                def _(v):
                    v.wait_ge(edges_in, 16 * 5)
                    pair_up(v, first, alone, edges_ready)
                    v.tensor_tensor(local[:, :].rearrange("p (d j) -> p d j", j=SPAN),
                                    first_all[:, :].unsqueeze(2).broadcast_to([P, SPANS, SPAN]),
                                    ends[:, :].rearrange("p (d j) -> p d j", j=SPAN), ALU.subtract).then_inc(edges_ready, 1)
            aggregate("s8", xp_table, sums, index, local, first, share, True)
        end_stage()

        w1_b1 = at(ctx, "exp_w1_b1", [P, X, HALVES * H1 + H1 // P])
        w2 = at(ctx, "exp_w2", [P, X, H1 // P * D])
        b2 = at(ctx, "exp_b2", [P, X, D])
        slots = at(ctx, "slots", [P, NT, 2], I32)
        fill = at(ctx, "fill", [P, 2 * X], I32)
        tile_exp = at(ctx, "tile_exp", [1, TILES], I32)
        scores_of = ExitStack()
        gates = at(scores_of, "gates", [P, NT, X])
        exp_in = sem("exp_in")
        with ExitStack() as st:
            wg = at(st, "s9_wg", [P, HALVES, X])
            bg = at(st, "s9_bg", [P, X])
            bias = at(st, "s9_bias", [P, D])
            x2 = at(st, "s9_x2", [P, 2, D])
            fixed = at(st, "s9_fixed", [P, 2, HALVES, P])
            z = at(st, "s9_z", [P, 2, D])
            below = at(st, "s9_below", [P, 2, D])
            x3 = at(st, "s9_x3", [P, 2, D])
            stat = at(st, "s9_stat", [P, 2, 6])
            mv = at(st, "s9_mv", [P, 2, 2])
            ve = at(st, "s9_ve", [P, 2, 1])
            rstd = at(st, "s9_rstd", [P, 2, 1])
            h = at(st, "s9_h", [P, 2, D])
            hT = at(st, "s9_hT", [P, 2, HALVES, P])
            psX = [bank(st, f"s9_psX{b}", D) for b in range(2)]
            psH = [bank(st, f"s9_psH{b}", HALVES, P) for b in range(2)]
            psR = [bank(st, f"s9_psR{b}", X) for b in range(2)]
            w_in, x_in, x3_out = sem("s9_w_in"), [sem(f"s9_x_in{b}") for b in range(2)], [sem(f"s9_x3_out{b}") for b in range(2)]
            held_go, held, unturned, z_done, below_done, exp_done = (sem(f"s9_{n}") for n in ("held_go", "held", "unturned", "z_done", "below_done", "exp_done"))
            part_done, x3_done, stats_done, stats_seen, moments, rstd_step = (sem(f"s9_{n}") for n in ("part_done", "x3_done", "stats", "stats_seen", "moments", "rstd_step"))
            normed, turned, hT_ready, scored, gated = (sem(f"s9_{n}") for n in ("normed", "turned", "hT_ready", "scored", "gated"))
            kept, kept_go = sem("s9_kept"), sem("s9_kept_go")
            with nc.Block() as block:
                @block.sync
                def _(sp):
                    def load(t, b):
                        sp.dma_start(x2[:, b, :], x2_rows[ds(t * P, P), :]).then_inc(x_in[b], 16)

                    def step(t, i, b, left):
                        if left == 2:
                            sp.wait_ge(part_done, t + 1)
                            load(t + 2, b)
                        sp.wait_ge(x3_done, t + 1)
                        sp.dma_start(x3_rows[ds(t * P, P), :], x3[:, b, :]).then_inc(x3_out[b], 16)

                    load(0, 0)
                    load(1, 1)
                    sp.dma_start(bias[:, :], a["att_bias"].broadcast_to([P, D])).then_inc(w_in, 16)
                    sp.dma_start(wg[:, :, :], a["gate_w"]).then_inc(w_in, 16)
                    sp.dma_start(bg[:, :], a["gate_b"].broadcast_to([P, X])).then_inc(w_in, 16)
                    sp.dma_start(w1_b1[:, :, :], a["exp_w1_b1"]).then_inc(exp_in, 16)
                    sp.dma_start(w2[:, :, :], a["exp_w2"]).then_inc(exp_in, 16)
                    sp.dma_start(b2[:, :, :].rearrange("p x d -> p (x d)"), a["exp_b2"].broadcast_to([P, X * D])).then_inc(exp_in, 16)
                    by_tiles(sp, step)
                    for b in range(2):
                        sp.wait_ge(x3_out[b], 16 * PAIRS)

                @block.gpsimd
                def _(pool):
                    def step(t, i, b, left):
                        pool.wait_ge(moments, t + 1)
                        pool.tensor_tensor(ve[:, b, :], mv[:, b, 1:2], eps[:, :], ALU.add).then_inc(rstd_step, 1)
                        pool.wait_ge(rstd_step, 2 * t + 1)
                        pool.tensor_tensor(rstd[:, b, :], ve[:, b, :], neg_half[:, :], ALU.pow).then_inc(rstd_step, 1)

                    by_tiles(pool, step)

                @block.scalar
                def _(act):
                    def hold(t, b):
                        act.sem_inc(held_go, 1)
                        act.activation(fixed[:, b, :, :], sums[:, :, ds(t * P, P)], ACT.Copy).then_inc(held, 1)

                    def exp_below(t, b):
                        act.wait_ge(below_done, t + 1)
                        act.activation(below[:, b, :], below[:, b, :], ACT.Exp).then_inc(exp_done, 1)

                    def step(t, i, b, left):
                        if left == 2:
                            act.wait_ge(unturned, t + 1)
                            hold(t + 2, b)
                        if left:
                            exp_below(t + 1, 1 - b)
                        act.wait_ge(turned, t + 1)
                        wait_past(act, scored, t - 1)
                        act.activation(hT[:, b, :, :], psH[b], ACT.Copy).then_inc(hT_ready, 1)
                        act.wait_ge(normed, t + 1)
                        act.wait_ge(held, t + 1)
                        act.sem_inc(kept_go, 1)
                        act.activation(sums[:, :, ds(t * P, P)], h[:, b, :].rearrange("p (k c) -> p k c", k=HALVES), ACT.Copy).then_inc(kept, 1)

                    hold(0, 0)
                    hold(1, 1)
                    exp_below(0, 0)
                    by_tiles(act, step)

                @block.tensor
                def _(pe):
                    def unturn(t, b):
                        pe.wait_ge(held, t + 1)
                        for k in range(HALVES):
                            mm = pe.transpose(psX[b][:, k * P:(k + 1) * P], fixed[:, b, k, :], ident[:, :])
                        mm.then_inc(unturned, 1)

                    def step(t, i, b, left):
                        if left == 2:
                            pe.wait_ge(z_done, t + 1)
                            unturn(t + 2, b)
                        pe.wait_ge(normed, t + 1)
                        wait_past(pe, hT_ready, t - 1)
                        for k in range(HALVES):
                            mm = pe.transpose(psH[b][:, k, :], h[:, b, k * P:(k + 1) * P], ident[:, :])
                        mm.then_inc(turned, 1)
                        pe.wait_ge(hT_ready, t + 1)
                        wait_past(pe, gated, t - 1)
                        for k in range(HALVES):
                            mm = pe.matmul(psR[b], hT[:, b, k, :], wg[:, k, :], start=(k == 0), stop=(k == HALVES - 1))
                        mm.then_inc(scored, 1)

                    unturn(0, 0)
                    unturn(1, 1)
                    pe.wait_ge(w_in, 48)
                    by_tiles(pe, step)

                @block.vector
                def _(v):
                    def residual(t, i, b):
                        v.wait_ge(x_in[b], 16 * i + 16)
                        v.wait_ge(unturned, t + 1)
                        v.tensor_tensor(z[:, b, :], psX[b], bias[:, :], ALU.add).then_inc(z_done, 1)
                        v.wait_ge(z_done, t + 1)
                        v.tensor_scalar(below[:, b, :], z[:, b, :], 0.0, None, ALU.min).then_inc(below_done, 1)
                        v.scalar_tensor_tensor(out=z[:, b, :], in0=z[:, b, :], scalar=0.0, in1=x2[:, b, :],
                                               op0=ALU.max, op1=ALU.add).then_inc(part_done, 1)

                    def moment(t, i, b):
                        v.wait_ge(exp_done, t + 1)
                        v.wait_ge(part_done, t + 1)
                        wait_past(v, x3_out[b], 16 * i)
                        v.scalar_tensor_tensor(out=x3[:, b, :], in0=below[:, b, :], scalar=-1.0, in1=z[:, b, :],
                                               op0=ALU.add, op1=ALU.add).then_inc(x3_done, 1)
                        v.wait_ge(x3_done, t + 1)
                        v.bn_stats(stat[:, b, :], x3[:, b, :]).then_inc(stats_done, 1)
                        v.wait_ge(stats_done, t + 1)
                        v.sem_inc(stats_seen, 1)
                        v.bn_aggr(mv[:, b, :], stat[:, b, :]).then_inc(moments, 1)

                    def score(t, b):
                        v.wait_ge(scored, t + 1)
                        v.tensor_tensor(gates[:, ds(t, 1), :].rearrange("p o x -> p (o x)"), psR[b], bg[:, :], ALU.add).then_inc(gated, 1)

                    def step(t, i, b, left):
                        if left:
                            residual(t + 1, i + b, 1 - b)
                        v.wait_ge(rstd_step, 2 * t + 2)
                        wait_past(v, turned, t - 1)
                        wait_past(v, kept, t - 1)
                        v.tensor_scalar(h[:, b, :], x3[:, b, :], mv[:, b, 0:1], rstd[:, b, :],
                                        ALU.subtract, ALU.mult).then_inc(normed, 1)
                        if left:
                            moment(t + 1, i + b, 1 - b)
                        if not isinstance(t, int) or t > 0:
                            score(t - 1, 1 - b)

                    v.wait_ge(w_in, 48)
                    residual(0, 0, 0)
                    moment(0, 0, 0)
                    by_tiles(v, step)
                    score(NT - 1, (NT - 1) % 2)

        HALF, PART = NT // 2, NT // RING
        with ExitStack() as st:
            wins = at(st, "s10_wins", [P, PART, X, X])
            ties = at(st, "s10_ties", [P, PART, X, X])
            lower_i = at(st, "s10_lower_i", [P, X, X], I32)
            lower = at(st, "s10_lower", [P, X, X])
            upto = at(st, "s10_upto", [P, P])
            step_i = at(st, "s10_step_i", [P, X], I32)
            steps = at(st, "s10_steps", [P, X])
            region = at(st, "s10_region", [P, X])
            spare = at(st, "s10_spare", [P, X])
            own_row = at(st, "s10_own_row", [P, X])
            line_i = at(st, "s10_line_i", [P, 1], I32)
            line = at(st, "s10_line", [P, 1])
            tile_i = at(st, "s10_tile_i", [1, TILES], I32)
            behind = at(st, "s10_behind", [P, X])
            mask = at(st, "s10_mask", [P, NT, X])
            upon = at(st, "s10_upon", [P, NT, X])
            place = at(st, "s10_place", [P, NT, X])
            both = at(st, "s10_both", [P, NT])
            second = at(st, "s10_second", [P, NT])
            many_i = at(st, "s10_many_i", [P, X], I32)
            many = at(st, "s10_many", [P, X])
            end = at(st, "s10_end", [P, X])
            end_row = at(st, "s10_end_row", [P, 1])
            over = at(st, "s10_over", [1, TILES, X])
            exp_f = at(st, "s10_exp_f", [1, TILES])
            psB = [bank(st, f"s10_psB{k}", HALF * X) for k in range(2)]
            psU = [bank(st, f"s10_psU{k}", HALF * X) for k in range(2)]
            made10, step_done, counted, masked10 = sem("s10_made"), sem("s10_step_done"), sem("s10_counted"), sem("s10_masked")
            with nc.Block() as block:
                @block.gpsimd
                def _(pool):
                    pool.iota(lower_i[:, :, :], pattern=[[1, X], [-1, X]], base=0, channel_multiplier=0).then_inc(made10, 1)
                    pool.iota(step_i[:, :], pattern=[[P, X]], base=0, channel_multiplier=0).then_inc(made10, 1)
                    pool.iota(line_i[:, :], pattern=[[0, 1]], base=0, channel_multiplier=1).then_inc(made10, 1)
                    pool.iota(tile_i[:, :], pattern=[[1, TILES]], base=0, channel_multiplier=0).then_inc(made10, 1)
                    pool.affine_select(out=upto[:, :], in_=ones[:, :], compare_op=ALU.is_gt, fill=0.0,
                                       base=0, pattern=[[1, P]], channel_multiplier=-1).then_inc(made10, 1)

                @block.tensor
                def _(pe):
                    pe.wait_ge(masked10, 1)
                    pe.wait_ge(made10, 5)
                    for k in range(2):
                        half = mask[:, k * HALF:(k + 1) * HALF, :].rearrange("p t x -> p (t x)")
                        pe.matmul(psB[k], upto[:, :], half, start=True, stop=True).then_inc(counted, 1)
                        pe.matmul(psU[k], ones[:, :], half, start=True, stop=True).then_inc(counted, 1)

                @block.vector
                def _(v):
                    count = [0]

                    def then(ins):
                        count[0] += 1
                        ins.then_inc(step_done, 1)
                        v.wait_ge(step_done, count[0])

                    v.wait_ge(made10, 5)
                    then(v.tensor_scalar(lower[:, :, :], lower_i[:, :, :], 0.5, None, ALU.is_gt))
                    then(v.tensor_copy(steps[:, :], step_i[:, :]))
                    then(v.tensor_copy(line[:, :], line_i[:, :]))
                    for k in range(RING):
                        tiles = slice(k * PART, (k + 1) * PART)
                        other = gates[:, tiles, :].unsqueeze(2).broadcast_to([P, PART, X, X])
                        own = gates[:, tiles, :].unsqueeze(3).broadcast_to([P, PART, X, X])
                        then(v.tensor_tensor(wins[:, :, :, :], other, own, ALU.is_gt))
                        then(v.tensor_tensor(ties[:, :, :, :], other, own, ALU.is_equal))
                        then(v.tensor_tensor(ties[:, :, :, :], ties[:, :, :, :], lower[:, :, :].unsqueeze(1).broadcast_to([P, PART, X, X]), ALU.mult))
                        then(v.tensor_tensor(wins[:, :, :, :], wins[:, :, :, :], ties[:, :, :, :], ALU.add))
                        then(v.tensor_reduce(place[:, tiles, :], wins[:, :, :, :], AX.X, ALU.add))
                    v.tensor_scalar(mask[:, :, :], place[:, :, :], 2.0, None, ALU.is_lt).then_inc(masked10, 1)
                    v.wait_ge(counted, 4)
                    for k in range(2):
                        then(v.tensor_copy(upon[:, k * HALF:(k + 1) * HALF, :].rearrange("p t x -> p (t x)"), psU[k]))
                    for e in range(X):
                        then(v.tensor_tensor_scan(place[:, :, e], ones[:, 0:NT], upon[:, :, e], 0.0, ALU.mult, ALU.add))
                    last = place[:, NT - 1, :]
                    then(v.tensor_scalar(many_i[:, :], last, float(P - 1), None, ALU.add))
                    then(v.tensor_scalar(many_i[:, :], many_i[:, :], P.bit_length() - 1, None, ALU.logical_shift_right))
                    then(v.tensor_copy(many[:, :], many_i[:, :]))
                    then(v.tensor_tensor_scan(end[:, :], ones[:, 0:X], many[:, :], 0.0, ALU.mult, ALU.add))
                    then(v.tensor_tensor(region[:, :], end[:, :], many[:, :], ALU.subtract))
                    then(v.tensor_scalar(region[:, :], region[:, :], float(P), None, ALU.mult))
                    then(v.tensor_tensor(behind[:, :], last, region[:, :], ALU.add))
                    then(v.tensor_scalar(behind[:, :], behind[:, :], line[:, :], None, ALU.add))
                    then(v.tensor_scalar(spare[:, :], steps[:, :], line[:, :], float((TILES + X) * P), ALU.add, ALU.add))
                    then(v.scalar_tensor_tensor(out=own_row[:, :], in0=end[:, :], scalar=float(P), in1=behind[:, :], op0=ALU.mult, op1=ALU.is_gt))
                    then(v.tensor_tensor(behind[:, :], behind[:, :], spare[:, :], ALU.subtract))
                    then(v.tensor_tensor(behind[:, :], behind[:, :], own_row[:, :], ALU.mult))
                    then(v.tensor_tensor(fill[:, 0:X], behind[:, :], spare[:, :], ALU.add))
                    then(v.tensor_scalar(end_row[:, :], end[:, X - 1:X], float(P), None, ALU.mult))
                    then(v.tensor_scalar(fill[:, X:2 * X], steps[:, :], end_row[:, :], line[:, :], ALU.add, ALU.add))
                    then(v.tensor_tensor(place[:, :, :], place[:, :, :], upon[:, :, :], ALU.subtract))
                    for k in range(2):
                        half = place[:, k * HALF:(k + 1) * HALF, :].rearrange("p t x -> p (t x)")
                        then(v.tensor_tensor(half, half, psB[k], ALU.add))
                    then(v.tensor_tensor(place[:, :, :], place[:, :, :], region[:, :].unsqueeze(1).broadcast_to([P, NT, X]), ALU.add))
                    then(v.tensor_tensor(place[:, :, :], place[:, :, :], mask[:, :, :], ALU.mult))
                    then(v.tensor_reduce(both[:, :], place[:, :, :], AX.X, ALU.add))
                    then(v.tensor_reduce(second[:, :], place[:, :, :], AX.X, ALU.max))
                    then(v.tensor_tensor(slots[:, :, 0], both[:, :], second[:, :], ALU.subtract))
                    then(v.tensor_copy(slots[:, :, 1], second[:, :]))
                    tile_of = tile_i[:, :].unsqueeze(2).broadcast_to([1, TILES, X])
                    then(v.tensor_tensor(over[:, :, :], tile_of, end[0:1, :].unsqueeze(1).broadcast_to([1, TILES, X]), ALU.is_ge))
                    then(v.tensor_reduce(exp_f[:, :], over[:, :, :], AX.X, ALU.add))
                    then(v.tensor_scalar(tile_exp[:, :], exp_f[:, :], float(X - 1), None, ALU.min))

        scores_of.close()

        with ExitStack() as st:
            zeros = at(st, "s11_zeros", [P, D])
            moved = at(st, "s11_moved", [P, RING, D])
            staged = at(st, "s11_staged", [P, RING, 2], I32)
            zero_made, zeros_out = sem("s11_zero_made"), sem("s11_zeros_out")
            moved_go, moved_done = sem("s11_moved_go"), sem("s11_moved_done")
            scattered = [sem(f"s11_scattered{s}") for s in range(RING)]
            with nc.Block() as block:
                @block.vector
                def _(v):
                    v.memset(zeros[:, :], 0.0).then_inc(zero_made, 1)

                @block.scalar
                def _(act):
                    def move(t, s):
                        act.sem_inc(moved_go, 1)
                        act.activation(staged[:, s, :], slots[:, ds(t, 1), :].rearrange("p o j -> p (o j)"), ACT.Copy).then_inc(moved_done, 1)
                        act.activation(moved[:, s, :].rearrange("p (k c) -> p k c", k=HALVES), sums[:, :, ds(t * P, P)], ACT.Copy).then_inc(moved_done, 1)

                    for s in range(RING):
                        move(s, s)
                    with act.Fori(1, NT // RING) as i:
                        for s in range(RING):
                            act.wait_ge(scattered[s], 32 * i)
                            move(i * RING + s, s)

                @block.gpsimd
                def _(pool):
                    pool.wait_ge(zero_made, 1)
                    for e in range(2 * X):
                        pool.indirect_dma_start(out=exp_rows[:, :], in_=zeros[:, :], in_offset=None,
                                                out_offset=bass.IndirectOffsetOnAxis(ap=fill[:, e:e + 1], axis=0)).then_inc(zeros_out, 16)

                    def scatter(t, s):
                        pool.wait_ge(moved_done, 2 * t + 2)
                        pool.sem_inc(moved_go, 1)
                        for j in range(2):
                            pool.indirect_dma_start(out=exp_rows[:, :], in_=moved[:, s, :], in_offset=None,
                                                    out_offset=bass.IndirectOffsetOnAxis(ap=staged[:, s, j:j + 1], axis=0)).then_inc(scattered[s], 16)

                    with pool.Fori(0, NT // RING) as i:
                        for s in range(RING):
                            scatter(i * RING + s, s)
                    for s in range(RING):
                        pool.wait_ge(scattered[s], 32 * (NT // RING))
                    pool.wait_ge(zeros_out, 16 * 2 * X)

        with ExitStack() as st:
            rows = at(st, "s12_rows", [P, 2, D])
            hT = at(st, "s12_hT", [P, 2, HALVES, P])
            w1_now = at(st, "s12_w1_now", [P, 2, HALVES * H1 + H1 // P])
            w2_now = at(st, "s12_w2_now", [P, 2, H1 // P * D])
            b2_now = at(st, "s12_b2_now", [P, 2, D])
            hid = at(st, "s12_hid", [P, 2, H1 // P, P])
            y = at(st, "s12_y", [P, 2, D])
            psH = [bank(st, f"s12_psH{b}", HALVES, P) for b in range(2)]
            psG = [bank(st, f"s12_psG{b}", H1 // P, P) for b in range(2)]
            psY = [bank(st, f"s12_psY{b}", D) for b in range(2)]
            rows_in, y_out = [sem(f"s12_rows_in{b}") for b in range(2)], [sem(f"s12_y_out{b}") for b in range(2)]
            w1_go, w1_ready, w2_go, w2_ready, b2_ready = (sem(f"s12_{n}") for n in ("w1_go", "w1_ready", "w2_go", "w2_ready", "b2_ready"))
            turned, hT_ready, up_done, active, down_done, y_done = (sem(f"s12_{n}") for n in ("turned", "hT_ready", "up_done", "active", "down_done", "y_done"))

            def expert(eng, t):
                return eng.value_load(tile_exp[0:1, ds(t, 1)], min_val=0, max_val=X - 1)

            with nc.Block() as block:
                @block.sync
                def _(sp):
                    def load(t, b):
                        sp.dma_start(rows[:, b, :], exp_rows[ds(t * P, P), :]).then_inc(rows_in[b], 16)

                    def store(t, b):
                        sp.wait_ge(y_done, t + 1)
                        sp.dma_start(y_rows[ds(t * P, P), :], y[:, b, :]).then_inc(y_out[b], 16)

                    def step(t, i, b, left):
                        if left == 2:
                            sp.wait_ge(turned, t + 1)
                            load(t + 2, b)
                        if not isinstance(t, int) or t > 0:
                            store(t - 1, 1 - b)

                    load(0, 0)
                    load(1, 1)
                    by_tiles(sp, step, TILES // 2)
                    store(TILES - 1, (TILES - 1) % 2)
                    for b in range(2):
                        sp.wait_ge(y_out[b], 16 * (TILES // 2))

                @block.scalar
                def _(act):
                    def copy_hT(t, b):
                        act.wait_ge(turned, t + 1)
                        wait_past(act, up_done, t - 1)
                        act.activation(hT[:, b, :, :], psH[b], ACT.Copy).then_inc(hT_ready, 1)

                    def second_weights(t, b):
                        e = expert(act, t)
                        wait_past(act, down_done, t - 1)
                        act.sem_inc(w2_go, 1)
                        act.activation(w2_now[:, b, :], w2[:, ds(e, 1), :].rearrange("p o n -> p (o n)"), ACT.Copy).then_inc(w2_ready, 1)

                    def gelu(t, b):
                        act.wait_ge(up_done, t + 1)
                        wait_past(act, down_done, t - 1)
                        for c in range(H1 // P):
                            g = act.activation(hid[:, b, c, :], psG[b][:, c, :], ACT.Gelu,
                                               bias=w1_now[:, b, HALVES * H1 + c:HALVES * H1 + c + 1])
                        g.then_inc(active, 1)

                    def step(t, i, b, left):
                        if left:
                            second_weights(t + 1, 1 - b)
                            gelu(t + 1, 1 - b)
                        if left == 2:
                            copy_hT(t + 2, b)

                    act.wait_ge(exp_in, 48)
                    copy_hT(0, 0)
                    copy_hT(1, 1)
                    second_weights(0, 0)
                    gelu(0, 0)
                    by_tiles(act, step, TILES // 2)

                @block.tensor
                def _(pe):
                    def turn(t, i, b):
                        pe.wait_ge(rows_in[b], 16 * i + 16)
                        wait_past(pe, hT_ready, t - 1)
                        for k in range(HALVES):
                            mm = pe.transpose(psH[b][:, k, :], rows[:, b, k * P:(k + 1) * P], ident[:, :])
                        mm.then_inc(turned, 1)

                    def up(t, b):
                        pe.wait_ge(hT_ready, t + 1)
                        pe.wait_ge(w1_ready, t + 1)
                        wait_past(pe, active, t - 1)
                        for c in range(H1 // P):
                            for k in range(HALVES):
                                at_w = k * H1 + c * P
                                mm = pe.matmul(psG[b][:, c, :], w1_now[:, b, at_w:at_w + P], hT[:, b, k, :],
                                               start=(k == 0), stop=(k == HALVES - 1))
                        mm.then_inc(up_done, 1)

                    def down(t, b):
                        pe.wait_ge(active, t + 1)
                        pe.wait_ge(w2_ready, t + 1)
                        wait_past(pe, y_done, t - 1)
                        for c in range(H1 // P):
                            mm = pe.matmul(psY[b], hid[:, b, c, :], w2_now[:, b, c * D:(c + 1) * D],
                                           start=(c == 0), stop=(c == H1 // P - 1))
                        mm.then_inc(down_done, 1)

                    def step(t, i, b, left):
                        if left:
                            up(t + 1, 1 - b)
                        if left == 2:
                            turn(t + 2, i + 1, b)
                        down(t, b)

                    turn(0, 0, 0)
                    turn(1, 0, 1)
                    up(0, 0)
                    by_tiles(pe, step, TILES // 2)

                @block.vector
                def _(v):
                    def first_weights(t, b):
                        e = expert(v, t)
                        wait_past(v, up_done, t - 1)
                        wait_past(v, active, t - 1)
                        v.sem_inc(w1_go, 1)
                        v.tensor_copy(w1_now[:, b, :], w1_b1[:, ds(e, 1), :].rearrange("p o n -> p (o n)")).then_inc(w1_ready, 1)
                        return e

                    def last_bias(e, b):
                        v.tensor_copy(b2_now[:, b, :], b2[:, ds(e, 1), :].rearrange("p o n -> p (o n)")).then_inc(b2_ready, 1)

                    def step(t, i, b, left):
                        if left == 2:
                            e = first_weights(t + 2, b)
                        v.wait_ge(down_done, t + 1)
                        v.wait_ge(b2_ready, t + 1)
                        wait_past(v, y_out[b], 16 * i)
                        v.tensor_tensor(y[:, b, :], psY[b], b2_now[:, b, :], ALU.add).then_inc(y_done, 1)
                        if left == 2:
                            v.wait_ge(y_done, t + 1)
                            last_bias(e, b)

                    v.wait_ge(exp_in, 48)
                    for b in range(2):
                        last_bias(first_weights(b, b), b)
                    by_tiles(v, step, TILES // 2)

        with ExitStack() as st:
            x3 = at(st, "s13_x3", [P, RING, D])
            got = at(st, "s13_got", [P, RING, 2, D])
            staged = at(st, "s13_staged", [P, RING, 2], I32)
            total = at(st, "s13_total", [P, RING, D])
            staged_go, staged_done, pair_done, total_done = sem("s13_staged_go"), sem("s13_staged_done"), sem("s13_pair_done"), sem("s13_total_done")
            x3_in = [sem(f"s13_x3_in{s}") for s in range(RING)]
            gathered = [sem(f"s13_gathered{s}") for s in range(RING)]
            stored = [sem(f"s13_stored{s}") for s in range(RING)]
            ROUNDS = NT // RING

            def by_round(eng, step):
                for s in range(RING):
                    step(0, s)
                with eng.Fori(1, ROUNDS) as i:
                    for s in range(RING):
                        step(i, s)

            with nc.Block() as block:
                @block.sync
                def _(sp):
                    def step(i, s):
                        wait_past(sp, total_done, (i - 1) * RING + s + 1)
                        sp.dma_start(x3[:, s, :], x3_rows[ds((i * RING + s) * P, P), :]).then_inc(x3_in[s], 16)

                    for s in range(RING):
                        sp.dma_start(x3[:, s, :], x3_rows[s * P:(s + 1) * P, :]).then_inc(x3_in[s], 16)
                    with sp.Fori(1, ROUNDS) as i:
                        for s in range(RING):
                            step(i, s)

                @block.scalar
                def _(act):
                    def stage(i, s):
                        act.sem_inc(staged_go, 1)
                        act.activation(staged[:, s, :], slots[:, ds(i * RING + s, 1), :].rearrange("p o j -> p (o j)"), ACT.Copy).then_inc(staged_done, 1)

                    def store(i, s):
                        act.wait_ge(total_done, i * RING + s + 1)
                        act.dma_start(out[ds((i * RING + s) * P, P), :], total[:, s, :]).then_inc(stored[s], 16)

                    for s in range(RING):
                        stage(0, s)
                    with act.Fori(0, ROUNDS - 1) as i:
                        for s in range(RING):
                            act.wait_ge(gathered[s], 32 * i + 32)
                            stage(i + 1, s)
                            store(i, s)
                    for s in range(RING):
                        store(ROUNDS - 1, s)
                    for s in range(RING):
                        act.wait_ge(stored[s], 16 * ROUNDS)

                @block.gpsimd
                def _(pool):
                    def step(i, s):
                        if not isinstance(i, int):
                            pool.wait_ge(total_done, i * RING - RING + s + 1)
                        pool.wait_ge(staged_done, i * RING + s + 1)
                        pool.sem_inc(staged_go, 1)
                        for j in range(2):
                            pool.indirect_dma_start(out=got[:, s, j, :], out_offset=None, in_=y_rows[:, :],
                                                    in_offset=bass.IndirectOffsetOnAxis(ap=staged[:, s, j:j + 1], axis=0)).then_inc(gathered[s], 16)

                    by_round(pool, step)

                @block.vector
                def _(v):
                    def step(i, s):
                        v.wait_ge(gathered[s], 32 * i + 32)
                        v.tensor_tensor(got[:, s, 0, :], got[:, s, 0, :], got[:, s, 1, :], ALU.add).then_inc(pair_done, 1)
                        v.wait_ge(pair_done, i * RING + s + 1)
                        v.wait_ge(x3_in[s], 16 * i + 16)
                        wait_past(v, stored[s], 16 * i)
                        v.tensor_tensor(total[:, s, :], got[:, s, 0, :], x3[:, s, :], ALU.add).then_inc(total_done, 1)

                    by_round(v, step)




def lay_out(x, src, dst, edge_type_8, edge_weight, L0_gnn_weight, L0_ffn_wr, L0_ffn_br, L0_ffn_w1, L0_ffn_b1,
            L0_ffn_w2, L0_ffn_b2, L1_gnn_W, L1_gnn_att_src, L1_gnn_att_dst, L1_gnn_bias, L1_ffn_Wg, L1_ffn_bg,
            L1_ffn_W1, L1_ffn_b1, L1_ffn_W2, L1_ffn_b2, L0_ffn_attention_mask=None):
    import numpy as np

    def padded(v, value):
        return np.concatenate([v, np.full(P * ROW - E, value, v.dtype)])

    def by_row(v):
        return v.reshape(P, ROW)

    def by_chunk(v):
        return v.reshape(CHUNKS, P).T

    src, dst = padded(np.asarray(src), N), padded(np.asarray(dst), N)
    x = np.asarray(x)
    blocks = np.asarray(L0_gnn_weight).reshape(R, NB, SB, SB)
    rel_w = np.zeros((P, HALVES, R, P), np.float32)
    per = P // SB
    for k in range(HALVES):
        for j in range(per):
            o = slice(j * SB, (j + 1) * SB)
            rel_w[o, k, :, o] = blocks[:, k * per + j].transpose(1, 0, 2)
    edge = np.array([-1], np.int32)
    b = {
        "x": np.concatenate([x, np.zeros((NP - N, D), x.dtype)]),
        "rel_w": rel_w.reshape(P, HALVES, R * P),
        "src_row": by_row(src), "dst_row": by_row(dst),
        "dst_before": by_row(np.concatenate([edge, dst[:-1]])),
        "dst_after": by_row(np.concatenate([dst[1:], edge])),
        "src_chunk": by_chunk(src), "dst_chunk": by_chunk(dst),
        "dst_first": np.concatenate([dst[:1], dst[::WIDE]]).reshape(1, SPANS + 1),
        "type_chunk": by_chunk(padded(np.asarray(edge_type_8), 0)),
        "weight_chunk": by_chunk(padded(np.asarray(edge_weight), 0)),
        "wr": np.asarray(L0_ffn_wr).reshape(1, D), "br": np.asarray(L0_ffn_br).reshape(1, 1),
        "ffn_w1": np.asarray(L0_ffn_w1).reshape(HALVES, P, H0).transpose(1, 0, 2),
        "ffn_b1": np.asarray(L0_ffn_b1).reshape(H0 // P, P).T,
        "ffn_w2": np.asarray(L0_ffn_w2).reshape(H0 // P, P, D).transpose(1, 0, 2),
        "ffn_b2": np.asarray(L0_ffn_b2).reshape(1, D),
        "att_w": np.asarray(L1_gnn_W).reshape(HALVES, P, D).transpose(1, 0, 2),
        "att": np.stack([np.asarray(L1_gnn_att_src).reshape(D), np.asarray(L1_gnn_att_dst).reshape(D)]).reshape(1, 2 * D),
        "att_bias": np.asarray(L1_gnn_bias).reshape(1, D),
        "gate_w": np.asarray(L1_ffn_Wg).reshape(HALVES, P, X).transpose(1, 0, 2),
        "gate_b": np.asarray(L1_ffn_bg).reshape(1, X),
        "exp_w1_b1": np.concatenate([
            np.asarray(L1_ffn_W1).reshape(X, HALVES, P, H1).transpose(2, 0, 1, 3).reshape(P, X, HALVES * H1),
            np.asarray(L1_ffn_b1).reshape(X, H1 // P, P).transpose(2, 0, 1)], axis=2),
        "exp_w2": np.asarray(L1_ffn_W2).reshape(X, H1 // P, P, D).transpose(2, 0, 1, 3).reshape(P, X, H1 // P * D),
        "exp_b2": np.asarray(L1_ffn_b2).reshape(1, X * D),
    }
    return {f"in_{k}": np.ascontiguousarray(v) for k, v in b.items()}


def kernel(**inputs):
    import concourse.bacc as bacc
    from concourse.bass_utils import run_bass_kernel_spmd

    arrays = lay_out(**inputs)
    nc = bacc.Bacc("TRN2", target_bir_lowering=False, num_devices=1)
    aps = {n[3:]: nc.dram_tensor(n, v.shape, mybir.dt.from_np(v.dtype), kind="ExternalInput").ap() for n, v in arrays.items()}
    out = nc.dram_tensor("out", (NP, D), F32, kind="ExternalOutput").ap()
    gnn_kernel(nc, aps, out)
    r = run_bass_kernel_spmd(nc, [arrays], core_ids=[0])
    return r.results[0]["out"][:N]
```

```python
from contextlib import ExitStack

import concourse.bass as bass
from concourse import mybir

F32 = mybir.dt.float32
I32 = mybir.dt.int32
ALU = mybir.AluOpType
ACT = mybir.ActivationFunctionType
AX = mybir.AxisListType
ds = bass.ds

P = 128
N = 12500
E = 212500
D = 256
HALVES = D // P
R = 8
NB, SB = 8, 32
H0 = 1024
KEEP = 12500 // 2 - 1
HEADS, CH = 4, 64
X, H1 = 8, 512
NT = -(-N // P)
NP = NT * P
ROW = -(-(-(-E // P)) // P) * P
CHUNKS = ROW
SPAN = 2
WIDE = SPAN * P
SPANS = CHUNKS // SPAN
ACC = NP + WIDE
KR = ROW // P
EPS = 1e-5
BIG = 1e30
U = 16
GRP = 4
ITER = CHUNKS // U
SELS = 4
PICKS = 8
PAIRS = NT // 2
CAP = NP + P
TILES = 2 * NT + X
RING = 7


def by_tiles(eng, step, pairs=PAIRS, peel=1):
    for i in range(peel):
        step(2 * i, i, 0, 2)
        step(2 * i + 1, i, 1, 2)
    with eng.Fori(peel, pairs - 1) as i:
        step(2 * i, i, 0, 2)
        step(2 * i + 1, i, 1, 2)
    step(2 * pairs - 2, pairs - 1, 0, 1)
    step(2 * pairs - 1, pairs - 1, 1, 0)


def wait_past(eng, semaphore, n):
    if not isinstance(n, int) or n > 0:
        eng.wait_ge(semaphore, n)


def gnn_kernel(nc, a, out):
    ctx = ExitStack()

    def dram(name, shape, dt=F32):
        return nc.dram_tensor(name, shape, dt, kind="Internal").ap()

    rel_table = dram("rel_table", [R * NP, D])
    mid_rows = dram("mid_rows", [NP, 2 * D])
    x2_rows = dram("x2_rows", [NP, D])
    xp_table = dram("xp_table", [NP, D])
    x3_rows = dram("x3_rows", [NP, D])
    exp_rows = dram("exp_rows", [X * CAP + X * P, D])
    y_rows = dram("y_rows", [TILES * P, D])
    share_rows = dram("share_rows", [P, CHUNKS, HEADS])
    logit_table = dram("logit_table", [NP, 2 * HEADS])

    with ctx:
        in_use = []

        def sem(name):
            in_use.append(nc.alloc_semaphore(name=name))
            return in_use[-1]

        def end_stage():
            nc.clear_and_free_semaphores(in_use)
            in_use.clear()
            nc.all_engine_barrier()

        def at(stack, name, shape, dt=F32):
            return stack.enter_context(nc.sbuf_tensor(name, shape, dt))

        def bank(stack, name, *shape, banks=1):
            t = stack.enter_context(nc.psum_tensor(name, [P, 512 * banks], F32))
            size = 1
            for n in shape:
                size *= n
            view = t[:, 0:size]
            return view.rearrange("p (a b) -> p a b", a=shape[0]) if len(shape) == 2 else view

        ident = at(ctx, "ident", [P, P])
        iota_i = at(ctx, "iota_i", [P, WIDE], I32)
        window = at(ctx, "window", [P, WIDE])
        ones = at(ctx, "ones", [P, P])
        neg_half = at(ctx, "neg_half", [P, 1])
        eps = at(ctx, "eps", [P, 1])
        logits = at(ctx, "logits", [P, NT])
        made = sem("made")
        made_v = sem("made_v")

        with nc.Block() as block:
            @block.gpsimd
            def _(pool):
                pool.memset(ident[:, :], 0.0).then_inc(made, 1)
                pool.iota(iota_i[:, :], pattern=[[1, WIDE]], base=0, channel_multiplier=0).then_inc(made, 1)
                pool.memset(neg_half[:, :], -0.5).then_inc(made, 1)
                pool.memset(eps[:, :], EPS).then_inc(made, 1)
                pool.wait_ge(made, 4)
                pool.affine_select(out=ident[:, :], in_=ident[:, :], compare_op=ALU.not_equal, fill=1.0,
                                   base=0, pattern=[[-1, P]], channel_multiplier=1).then_inc(made, 1)

            @block.vector
            def _(v):
                v.memset(ones[:, :], 1.0).then_inc(made_v, 1)
                v.wait_ge(made, 5)
                v.tensor_copy(window[:, :], iota_i[:, :]).then_inc(made_v, 1)

        end_stage()

        with ExitStack() as st:
            rel_w = at(st, "rel_w", [P, HALVES, R * P])
            xt = at(st, "s1_x", [P, 2, D])
            stat = at(st, "s1_stat", [P, 2, 6])
            mv = at(st, "s1_mv", [P, 2, 2])
            ve = at(st, "s1_ve", [P, 2, 1])
            rstd = at(st, "s1_rstd", [P, 2, 1])
            h = at(st, "s1_h", [P, 2, D])
            hT = at(st, "s1_hT", [P, 2, HALVES, P])
            rows = at(st, "s1_rows", [P, 2, R, D])
            psT = [bank(st, f"s1_psT{b}", HALVES, P) for b in range(2)]
            psO = [bank(st, f"s1_psO{k}", R * P, banks=2) for k in range(HALVES)]
            w_in, x_in = sem("s1_w_in"), [sem(f"s1_x_in{b}") for b in range(2)]
            stats_done, stats_seen, moments, rstd_step, normed = sem("s1_stats"), sem("s1_stats_seen"), sem("s1_moments"), sem("s1_rstd_step"), sem("s1_normed")
            turned, hT_ready = sem("s1_turned"), sem("s1_hT_ready")
            product = [sem(f"s1_product{k}") for k in range(HALVES)]
            evicted = [sem(f"s1_evicted{k}") for k in range(HALVES)]
            stored = [sem(f"s1_stored{b}") for b in range(2)]
            x_tiles = a["x"]
            table_tiles = rel_table.rearrange("(r n) d -> n r d", r=R)

            with nc.Block() as block:
                @block.sync
                def _(sp):
                    sp.dma_start(rel_w[:, :, :], a["rel_w"]).then_inc(w_in, 16)

                    def load(t, i, b):
                        sp.dma_start(xt[:, b, :], x_tiles[ds(t * P, P), :]).then_inc(x_in[b], 16)

                    load(0, 0, 0)
                    load(1, 0, 1)
                    with sp.Fori(0, PAIRS - 1) as i:
                        for b in range(2):
                            sp.wait_ge(normed, 2 * i + b + 1)
                            load(2 * i + b + 2, i + 1, b)

                @block.gpsimd
                def _(pool):
                    def step(t, i, b, left):
                        pool.wait_ge(moments, t + 1)
                        pool.tensor_tensor(ve[:, b, :], mv[:, b, 1:2], eps[:, :], ALU.add).then_inc(rstd_step, 1)
                        pool.wait_ge(rstd_step, 2 * t + 1)
                        pool.tensor_tensor(rstd[:, b, :], ve[:, b, :], neg_half[:, :], ALU.pow).then_inc(rstd_step, 1)

                    by_tiles(pool, step)

                @block.vector
                def _(v):
                    def norm(t, i, b):
                        v.wait_ge(x_in[b], 16 * i + 16)
                        v.bn_stats(stat[:, b, :], xt[:, b, :]).then_inc(stats_done, 1)
                        v.wait_ge(stats_done, t + 1)
                        v.sem_inc(stats_seen, 1)
                        v.bn_aggr(mv[:, b, :], stat[:, b, :]).then_inc(moments, 1)
                        v.wait_ge(rstd_step, 2 * t + 2)
                        v.tensor_scalar(h[:, b, :], xt[:, b, :], mv[:, b, 0:1], rstd[:, b, :],
                                        ALU.subtract, ALU.mult).then_inc(normed, 1)

                    def evict(t, i, b):
                        v.wait_ge(product[0], t + 1)
                        wait_past(v, stored[b], 16 * i)
                        v.tensor_copy(rows[:, b, :, 0:P], psO[0][:, :].rearrange("p (r o) -> p r o", r=R)).then_inc(evicted[0], 1)

                    def step(t, i, b, left):
                        if left:
                            wait_past(v, turned, t)
                            norm(t + 1, i + b, 1 - b)
                        evict(t, i, b)

                    norm(0, 0, 0)
                    by_tiles(v, step)

                @block.scalar
                def _(act):
                    def copy_hT(t, b):
                        act.wait_ge(turned, t + 1)
                        act.activation(hT[:, b, :, :], psT[b][:, :, :], ACT.Copy).then_inc(hT_ready, 1)

                    def step(t, i, b, left):
                        if left:
                            wait_past(act, product[1], t)
                            copy_hT(t + 1, 1 - b)
                        act.wait_ge(product[1], t + 1)
                        wait_past(act, stored[b], 16 * i)
                        act.activation(rows[:, b, :, P:D], psO[1][:, :].rearrange("p (r o) -> p r o", r=R), ACT.Copy).then_inc(evicted[1], 1)
                        act.wait_ge(evicted[0], t + 1)
                        act.wait_ge(evicted[1], t + 1)
                        act.dma_start(table_tiles[ds(t * P, P), :, :], rows[:, b, :, :]).then_inc(stored[b], 16)

                    copy_hT(0, 0)
                    by_tiles(act, step)
                    for b in range(2):
                        act.wait_ge(stored[b], 16 * PAIRS)

                @block.tensor
                def _(pe):
                    def turn(t, b):
                        pe.wait_ge(normed, t + 1)
                        for k in range(HALVES):
                            mm = pe.transpose(psT[b][:, k, :], h[:, b, k * P:(k + 1) * P], ident[:, :])
                        mm.then_inc(turned, 1)

                    def step(t, i, b, left):
                        pe.wait_ge(hT_ready, t + 1)
                        for k in range(HALVES):
                            if left and k == 1:
                                turn(t + 1, 1 - b)
                            wait_past(pe, evicted[k], t)
                            for c in range(R * P // 512):
                                mm = pe.matmul(psO[k][:, c * 512:(c + 1) * 512], hT[:, b, k, :],
                                               rel_w[:, k, c * 512:(c + 1) * 512], start=True, stop=True)
                            mm.then_inc(product[k], 1)

                    pe.wait_ge(w_in, 16)
                    turn(0, 0)
                    by_tiles(pe, step)
        end_stage()

        def aggregate(name, table, sums, index, local, first, scale, per_head):
            with ExitStack() as st:
                rows = at(st, f"{name}_rows", [P, U, D])
                staged = at(st, f"{name}_staged", [P, U], I32)
                pick = at(st, f"{name}_pick", [P, PICKS, WIDE])
                apart = at(st, f"{name}_apart", [P, PICKS, WIDE]) if per_head else None
                scaled = at(st, f"{name}_scaled", [P, PICKS, D]) if per_head else None
                part = [bank(st, f"{name}_part{k}", HALVES, 512, banks=HALVES)[:, :, 0:WIDE] for k in range(SELS)]
                idx_taken, idx_ready, idx_seen = sem(f"{name}_idx_taken"), sem(f"{name}_idx_ready"), sem(f"{name}_idx_seen")
                gathered = [sem(f"{name}_gathered{s}") for s in range(U)]
                rows_scaled = sem(f"{name}_rows_scaled")
                picked, apart_go, apart_done = sem(f"{name}_picked"), sem(f"{name}_apart_go"), sem(f"{name}_apart_done")
                product, added, cleared = sem(f"{name}_product"), sem(f"{name}_added"), sem(f"{name}_cleared")
                rows_used, used_from = (rows_scaled, 0) if per_head else (product, 1)
                GROUPS = U // GRP

                with nc.Block() as block:
                    @block.scalar
                    def _(act):
                        def matrices(n, half, first_pass=False):
                            if not first_pass:
                                act.wait_ge(product, n * GRP - GRP + 1)
                            act.sem_inc(apart_go, 1)
                            for j in range(GRP):
                                act.activation(apart[:, half * GRP + j, :], window[:, :], ACT.Abs,
                                               bias=local[:, ds(n * GRP + j, 1)]).then_inc(apart_done, 1)
                            act.wait_ge(apart_done, n * GRP + GRP)
                            act.activation(pick[:, half * GRP:(half + 1) * GRP, :], apart[:, half * GRP:(half + 1) * GRP, :],
                                           ACT.Relu, bias=ones[:, 0:1], scale=-1.0).then_inc(picked, 1)

                        for g in range(GROUPS):
                            act.activation(staged[:, g * GRP:(g + 1) * GRP], index[:, g * GRP:(g + 1) * GRP],
                                           ACT.Copy).then_inc(idx_ready, 1)
                        if per_head:
                            matrices(0, 0, True)
                            matrices(1, 1, True)
                        with act.Fori(1, ITER) as i:
                            for g in range(GROUPS):
                                for s in range(g * GRP, (g + 1) * GRP):
                                    act.wait_ge(gathered[s], 16 * i)
                                act.sem_inc(idx_taken, 1)
                                act.activation(staged[:, g * GRP:(g + 1) * GRP], index[:, ds(i * U + g * GRP, GRP)],
                                               ACT.Copy).then_inc(idx_ready, 1)
                                if per_head:
                                    matrices(GROUPS * i - GROUPS + g + 2, g % 2)
                        if per_head:
                            for g in range(GROUPS):
                                if GROUPS * (ITER - 1) + g + 2 < GROUPS * ITER:
                                    matrices(GROUPS * (ITER - 1) + g + 2, g % 2)

                    @block.gpsimd
                    def _(pool):
                        def gathers(i, g, first_pass):
                            if not first_pass:
                                pool.wait_ge(rows_used, U * i - U + (g + 1) * GRP + used_from)
                            pool.wait_ge(idx_ready, GROUPS * i + g + 1)
                            pool.sem_inc(idx_seen, 1)
                            for s in range(g * GRP, (g + 1) * GRP):
                                pool.indirect_dma_start(
                                    out=rows[:, s, :], out_offset=None, in_=table[:, :],
                                    in_offset=bass.IndirectOffsetOnAxis(ap=staged[:, s:s + 1], axis=0),
                                ).then_inc(gathered[s], 16)

                        for g in range(GROUPS):
                            gathers(0, g, True)
                        with pool.Fori(1, ITER) as i:
                            for g in range(GROUPS):
                                gathers(i, g, False)

                    @block.tensor
                    def _(pe):
                        pe.sem_inc(product, 1)
                        with pe.Fori(0, ITER) as i:
                            for s in range(U):
                                c = i * U + s
                                if per_head:
                                    pe.wait_ge(rows_scaled, c + 1)
                                    pe.wait_ge(picked, i * GROUPS + s // GRP + 1)
                                else:
                                    pe.wait_ge(gathered[s], 16 * i + 16)
                                    pe.wait_ge(picked, c + 1)
                                if s % SPAN == 0:
                                    pe.wait_ge(added, i * (U // SPAN) + s // SPAN + 1)
                                for k in range(HALVES):
                                    left = scaled[:, s % PICKS, k * P:(k + 1) * P] if per_head else rows[:, s, k * P:(k + 1) * P]
                                    mm = pe.matmul(part[s // SPAN % SELS][:, k, :], left, pick[:, s % PICKS, :],
                                                   start=(s % SPAN == 0), stop=(s % SPAN == SPAN - 1))
                                mm.then_inc(product, 1)

                    @block.vector
                    def _(v):
                        def matrix(c, s):
                            v.tensor_scalar(pick[:, s % PICKS, :], window[:, :], local[:, ds(c, 1)], scale[:, ds(c, 1)],
                                            ALU.is_equal, ALU.mult).then_inc(picked, 1)

                        def scaling(i, s):
                            c = i * U + s
                            v.wait_ge(gathered[s], 16 * i + 16)
                            v.tensor_tensor(scaled[:, s % PICKS, :].rearrange("p (h c) -> p h c", h=HEADS),
                                            rows[:, s, :].rearrange("p (h c) -> p h c", h=HEADS),
                                            scale[:, ds(c, 1), :].rearrange("p o h -> p (o h)").unsqueeze(2).broadcast_to([P, HEADS, CH]),
                                            ALU.mult).then_inc(rows_scaled, 1)

                        def add(d, w, at_node):
                            v.wait_ge(product, d * SPAN + 1)
                            v.wait_ge(added, d + 3)
                            v.tensor_tensor(sums[:, :, ds(at_node, WIDE)], sums[:, :, ds(at_node, WIDE)],
                                            part[(w - 1) % SELS][:, :, :], ALU.add).then_inc(added, 1)

                        v.memset(sums[:, :, :], 0.0).then_inc(cleared, 1)
                        v.memset(part[SELS - 1][:, :, :], 0.0).then_inc(cleared, 1)
                        v.sem_inc(added, 3)
                        if not per_head:
                            matrix(0, 0)
                            matrix(1, 1)
                        v.wait_ge(cleared, 2)
                        with v.Fori(0, ITER) as i:
                            for s in range(0, U, 2 * SPAN):
                                d, w = i * (U // SPAN) + s // SPAN, s // SPAN
                                for j in range(2 * SPAN):
                                    if per_head:
                                        scaling(i, s + j)
                                    else:
                                        matrix(i * U + s + j + 2, (s + j + 2) % U)
                                both = v.value_load(first[0:1, ds(i * (U // SPAN // 2) + w // 2, 1)], min_val=0, max_val=2 ** 31 - 1)
                                for j, at_node in enumerate((both & 0xffff, both >> 16)):
                                    add(d + j, w + j, nc.s_assert_within(at_node, min_val=0, max_val=N,
                                                                         skip_runtime_bounds_check_because="a destination, at most N"))
                        at_node = v.value_load(first[0:1, SPANS // 2:SPANS // 2 + 1], min_val=0, max_val=N)
                        add(SPANS, 0, at_node)

        def pair_up(v, first, alone, done):
            lower, upper = alone[:, 0:SPANS:2], alone[:, 1:SPANS:2]
            v.tensor_scalar(first[:, 0:SPANS // 2], upper, 16, None, ALU.logical_shift_left).then_inc(done, 1)
            v.wait_ge(done, 1)
            v.tensor_tensor(first[:, 0:SPANS // 2], first[:, 0:SPANS // 2], lower, ALU.bitwise_or).then_inc(done, 1)
            v.tensor_copy(first[:, SPANS // 2:SPANS // 2 + 1], alone[:, SPANS:SPANS + 1]).then_inc(done, 1)

        sums_of = ExitStack()
        sums = at(sums_of, "sums", [P, HALVES, ACC])
        with ExitStack() as st:
            first = at(st, "s2_first", [1, SPANS // 2 + 1], I32)
            alone = at(st, "s2_alone", [1, SPANS + 1], I32)
            first_all = at(st, "s2_first_all", [P, SPANS], I32)
            index = at(st, "s2_index", [P, CHUNKS], I32)
            source = at(st, "s2_source", [P, CHUNKS], I32)
            local = at(st, "s2_local", [P, CHUNKS + 2])
            weight = at(st, "s2_weight", [P, CHUNKS + 2])
            ends = at(st, "s2_ends", [P, CHUNKS], I32)
            edges_in, edges_ready = sem("s2_edges_in"), sem("s2_edges_ready")
            with nc.Block() as block:
                @block.sync
                def _(sp):
                    sp.dma_start(alone[:, :], a["dst_first"]).then_inc(edges_in, 16)
                    sp.dma_start(first_all[:, :], a["dst_first"][0:1, 1:SPANS + 1].broadcast_to([P, SPANS])).then_inc(edges_in, 16)
                    sp.dma_start(index[:, :], a["type_chunk"]).then_inc(edges_in, 16)
                    sp.dma_start(source[:, :], a["src_chunk"]).then_inc(edges_in, 16)
                    sp.dma_start(ends[:, :], a["dst_chunk"]).then_inc(edges_in, 16)
                    sp.dma_start(weight[:, 0:CHUNKS], a["weight_chunk"]).then_inc(edges_in, 16)
                    sp.wait_ge(edges_in, 16 * 6)

                @block.vector
                def _(v):
                    v.memset(local[:, CHUNKS:CHUNKS + 2], 0.0)
                    v.memset(weight[:, CHUNKS:CHUNKS + 2], 0.0)
                    v.wait_ge(edges_in, 16 * 6)
                    pair_up(v, first, alone, edges_ready)
                    v.scalar_tensor_tensor(out=index[:, :], in0=index[:, :], scalar=float(NP), in1=source[:, :],
                                           op0=ALU.mult, op1=ALU.add).then_inc(edges_ready, 1)
                    v.tensor_tensor(local[:, 0:CHUNKS].rearrange("p (d j) -> p d j", j=SPAN), ends[:, :].rearrange("p (d j) -> p d j", j=SPAN),
                                    first_all[:, :].unsqueeze(2).broadcast_to([P, SPANS, SPAN]), ALU.subtract).then_inc(edges_ready, 1)
            aggregate("s2", rel_table, sums, index, local, first, weight, False)
        end_stage()

        with ExitStack() as st:
            w1 = at(st, "s3_w1", [P, HALVES, H0])
            w2 = at(st, "s3_w2", [P, H0 // P, D])
            b1 = at(st, "s3_b1", [P, H0 // P])
            b2 = at(st, "s3_b2", [P, D])
            wr = at(st, "s3_wr", [P, D])
            xt = at(st, "s3_x", [P, 2, D])
            fixed = at(st, "s3_fixed", [P, 2, HALVES, P])
            x1 = at(st, "s3_x1", [P, 2, D])
            stat = at(st, "s3_stat", [P, 2, 6])
            mv = at(st, "s3_mv", [P, 2, 2])
            ve = at(st, "s3_ve", [P, 2, 1])
            rstd = at(st, "s3_rstd", [P, 2, 1])
            h = at(st, "s3_h", [P, 2, D])
            skip = at(st, "s3_skip", [P, 2, D])
            y = at(st, "s3_y", [P, 2, D])
            routed = at(st, "s3_routed", [P, 2, D])
            logit = at(st, "s3_logit", [P, 2, 1])
            hT = at(st, "s3_hT", [P, 2, HALVES, P])
            hid = at(st, "s3_hid", [P, 2, H0 // P, P])
            psX = [bank(st, f"s3_psX{b}", D) for b in range(2)]
            psH = bank(st, "s3_psH", HALVES, P)
            psG = [bank(st, f"s3_psG{k}", 4, P) for k in range(2)]
            psY = bank(st, "s3_psY", D)
            w_in, x_in = sem("s3_w_in"), [sem(f"s3_x_in{b}") for b in range(2)]
            held, held_go, unturned, x1_done = sem("s3_held"), sem("s3_held_go"), sem("s3_unturned"), sem("s3_x1_done")
            stats_done, stats_seen, moments, rstd_step = sem("s3_stats"), sem("s3_stats_seen"), sem("s3_moments"), sem("s3_rstd_step")
            normed, skipped, logit_done, logit_go = sem("s3_normed"), sem("s3_skipped"), sem("s3_logit_done"), sem("s3_logit_go")
            turned, hT_ready = sem("s3_turned"), sem("s3_hT_ready")
            up_done, active = [sem(f"s3_up_done{k}") for k in range(2)], [sem(f"s3_active{k}") for k in range(2)]
            down_done, y_done = sem("s3_down_done"), sem("s3_y_done")
            skip_out, y_out = [sem(f"s3_skip_out{b}") for b in range(2)], [sem(f"s3_y_out{b}") for b in range(2)]
            with nc.Block() as block:
                @block.sync
                def _(sp):
                    def load(t, b):
                        sp.dma_start(xt[:, b, :], a["x"][ds(t * P, P), :]).then_inc(x_in[b], 16)

                    def step(t, i, b, left):
                        if left == 2:
                            sp.wait_ge(x1_done, t + 1)
                            load(t + 2, b)
                        sp.wait_ge(skipped, t + 1)
                        sp.dma_start(mid_rows[ds(t * P, P), 0:D], skip[:, b, :]).then_inc(skip_out[b], 16)
                        sp.wait_ge(y_done, t + 1)
                        sp.dma_start(mid_rows[ds(t * P, P), D:2 * D], y[:, b, :]).then_inc(y_out[b], 16)

                    load(0, 0)
                    load(1, 1)
                    sp.dma_start(wr[:, :], a["wr"].broadcast_to([P, D])).then_inc(w_in, 16)
                    sp.dma_start(w1[:, :, :], a["ffn_w1"]).then_inc(w_in, 16)
                    sp.dma_start(b1[:, :], a["ffn_b1"]).then_inc(w_in, 16)
                    sp.dma_start(w2[:, :, :], a["ffn_w2"]).then_inc(w_in, 16)
                    sp.dma_start(b2[:, :], a["ffn_b2"].broadcast_to([P, D])).then_inc(w_in, 16)
                    by_tiles(sp, step)
                    for b in range(2):
                        sp.wait_ge(skip_out[b], 16 * PAIRS)
                        sp.wait_ge(y_out[b], 16 * PAIRS)

                @block.gpsimd
                def _(pool):
                    def step(t, i, b, left):
                        pool.wait_ge(moments, t + 1)
                        pool.tensor_tensor(ve[:, b, :], mv[:, b, 1:2], eps[:, :], ALU.add).then_inc(rstd_step, 1)
                        pool.wait_ge(rstd_step, 2 * t + 1)
                        pool.tensor_tensor(rstd[:, b, :], ve[:, b, :], neg_half[:, :], ALU.pow).then_inc(rstd_step, 1)

                    by_tiles(pool, step)

                @block.scalar
                def _(act):
                    def hold(t, b):
                        act.sem_inc(held_go, 1)
                        act.activation(fixed[:, b, :, :], sums[:, :, ds(t * P, P)], ACT.Copy).then_inc(held, 1)

                    def copy_hT(t, b):
                        act.wait_ge(turned, t + 1)
                        act.activation(hT[:, b, :, :], psH, ACT.Copy).then_inc(hT_ready, 1)
                        act.wait_ge(logit_done, t + 1)
                        act.sem_inc(logit_go, 1)
                        act.activation(logits[:, ds(t, 1)], logit[:, b, :], ACT.Copy)

                    def step(t, i, b, left):
                        if left == 2:
                            act.wait_ge(unturned, t + 1)
                            hold(t + 2, b)
                        for k in range(2):
                            act.wait_ge(up_done[k], t + 1)
                            for c in range(4):
                                g = act.activation(hid[:, b, 4 * k + c, :], psG[k][:, c, :], ACT.Gelu_apprx_tanh,
                                                   bias=b1[:, 4 * k + c:4 * k + c + 1])
                            g.then_inc(active[k], 1)
                        if left:
                            copy_hT(t + 1, 1 - b)

                    hold(0, 0)
                    hold(1, 1)
                    act.wait_ge(w_in, 16 * 5)
                    copy_hT(0, 0)
                    by_tiles(act, step)

                @block.tensor
                def _(pe):
                    def unturn(t, b):
                        pe.wait_ge(held, t + 1)
                        for k in range(HALVES):
                            mm = pe.transpose(psX[b][:, k * P:(k + 1) * P], fixed[:, b, k, :], ident[:, :])
                        mm.then_inc(unturned, 1)

                    def turn(t, b):
                        pe.wait_ge(normed, t + 1)
                        for k in range(HALVES):
                            mm = pe.transpose(psH[:, k, :], h[:, b, k * P:(k + 1) * P], ident[:, :])
                        mm.then_inc(turned, 1)

                    def step(t, i, b, left):
                        if left == 2:
                            pe.wait_ge(x1_done, t + 1)
                            unturn(t + 2, b)
                        pe.wait_ge(hT_ready, t + 1)
                        for k in range(2):
                            wait_past(pe, active[k], t)
                            for c in range(4):
                                for half in range(HALVES):
                                    mm = pe.matmul(psG[k][:, c, :], w1[:, half, (4 * k + c) * P:(4 * k + c + 1) * P],
                                                   hT[:, b, half, :], start=(half == 0), stop=(half == HALVES - 1))
                            mm.then_inc(up_done[k], 1)
                        if left:
                            turn(t + 1, 1 - b)
                        wait_past(pe, y_done, t)
                        for k in range(2):
                            pe.wait_ge(active[k], t + 1)
                            for c in range(4 * k, 4 * k + 4):
                                mm = pe.matmul(psY, hid[:, b, c, :], w2[:, c, :], start=(c == 0), stop=(c == H0 // P - 1))
                        mm.then_inc(down_done, 1)

                    unturn(0, 0)
                    unturn(1, 1)
                    pe.wait_ge(w_in, 16 * 5)
                    turn(0, 0)
                    by_tiles(pe, step)

                @block.vector
                def _(v):
                    def front(t, i, b):
                        v.wait_ge(x_in[b], 16 * i + 16)
                        wait_past(v, skip_out[b], 16 * i)
                        v.wait_ge(unturned, t + 1)
                        v.tensor_tensor(x1[:, b, :], psX[b], xt[:, b, :], ALU.add).then_inc(x1_done, 1)
                        v.wait_ge(x1_done, t + 1)
                        v.bn_stats(stat[:, b, :], x1[:, b, :]).then_inc(stats_done, 1)
                        v.wait_ge(stats_done, t + 1)
                        v.sem_inc(stats_seen, 1)
                        v.bn_aggr(mv[:, b, :], stat[:, b, :]).then_inc(moments, 1)
                        v.wait_ge(rstd_step, 2 * t + 2)
                        v.tensor_scalar(h[:, b, :], x1[:, b, :], mv[:, b, 0:1], rstd[:, b, :],
                                        ALU.subtract, ALU.mult).then_inc(normed, 1)
                        v.wait_ge(normed, t + 1)
                        v.tensor_tensor(skip[:, b, :], x1[:, b, :], h[:, b, :], ALU.add).then_inc(skipped, 1)
                        v.tensor_tensor_reduce(routed[:, b, :], h[:, b, :], wr[:, :], 1.0, 0.0, ALU.mult, ALU.add,
                                               logit[:, b, :]).then_inc(logit_done, 1)

                    def step(t, i, b, left):
                        if left:
                            front(t + 1, i + b, 1 - b)
                        v.wait_ge(down_done, t + 1)
                        wait_past(v, y_out[b], 16 * i)
                        v.tensor_tensor(y[:, b, :], psY, b2[:, :], ALU.add).then_inc(y_done, 1)

                    v.wait_ge(w_in, 16 * 5)
                    front(0, 0, 0)
                    by_tiles(v, step)
        sums_of.close()
        end_stage()

        with ExitStack() as st:
            br = at(st, "s4_br", [P, 1])
            upto = at(st, "s4_upto", [P, P])
            prefix = at(st, "s4_prefix", [P, 1], I32)
            bit = at(st, "s4_bit", [P, 1], I32)
            cand = at(st, "s4_cand", [P, 1], I32)
            flip = at(st, "s4_flip", [P, 1], I32)
            value = at(st, "s4_value", [P, 1], I32)
            taken = at(st, "s4_taken", [P, 1], I32)
            over = at(st, "s4_over", [P, NT])
            same = at(st, "s4_same", [P, NT])
            count = at(st, "s4_count", [P, 1])
            left_over = at(st, "s4_left_over", [P, 1])
            before = at(st, "s4_before", [P, NT])
            rank = at(st, "s4_rank", [P, NT])
            zeros = at(st, "s4_zeros", [P, NT])
            psC = bank(st, "s4_psC", 1)
            psU = bank(st, "s4_psU", NT)
            psA = bank(st, "s4_psA", NT)
            br_in, tri, biased, padded = sem("s4_br_in"), sem("s4_tri"), sem("s4_biased"), sem("s4_padded")
            done, counted, total = sem("s4_done"), sem("s4_counted"), sem("s4_total")
            OPS = 9
            with nc.Block() as block:
                @block.sync
                def _(sp):
                    sp.dma_start(br[:, :], a["br"].broadcast_to([P, 1])).then_inc(br_in, 16)
                    sp.wait_ge(br_in, 16)

                @block.gpsimd
                def _(pool):
                    pool.affine_select(out=upto[:, :], in_=ones[:, :], compare_op=ALU.is_ge, fill=0.0,
                                       base=0, pattern=[[1, P]], channel_multiplier=-1).then_inc(tri, 1)
                    pool.wait_ge(biased, 1)
                    pool.affine_select(out=logits[:, :], in_=logits[:, :], compare_op=ALU.is_ge, fill=-3.4e38,
                                       base=N - 1, pattern=[[-P, NT]], channel_multiplier=-1).then_inc(padded, 1)

                @block.tensor
                def _(pe):
                    with pe.Fori(0, 33) as i:
                        pe.wait_ge(counted, i + 1)
                        pe.matmul(psC, ones[:, :], count[:, :], start=True, stop=True).then_inc(total, 1)
                    pe.wait_ge(counted, 34)
                    pe.wait_ge(tri, 1)
                    pe.matmul(psU, upto[:, :], same[:, :], start=True, stop=True)
                    pe.matmul(psA, ones[:, :], same[:, :], start=True, stop=True).then_inc(total, 1)

                @block.vector
                def _(v):
                    v.wait_ge(br_in, 16)
                    v.tensor_scalar(logits[:, :], logits[:, :], br[:, :], None, ALU.add).then_inc(biased, 1)
                    v.memset(zeros[:, :], 0.0)
                    v.memset(prefix[:, :], 0).then_inc(done, 1)
                    v.memset(bit[:, :], -2 ** 31).then_inc(done, 1)
                    v.wait_ge(padded, 1)

                    def as_value(k):
                        v.wait_ge(done, k)
                        v.tensor_scalar(flip[:, :], cand[:, :], 31, -1, ALU.arith_shift_right, ALU.bitwise_xor).then_inc(done, 1)
                        v.wait_ge(done, k + 1)
                        v.scalar_tensor_tensor(out=value[:, :], in0=flip[:, :], scalar=-2 ** 31, in1=cand[:, :],
                                               op0=ALU.bitwise_or, op1=ALU.bitwise_xor).then_inc(done, 1)

                    with v.Fori(0, 32) as i:
                        k = i * (OPS - 1) + 2
                        v.wait_ge(done, k)
                        v.tensor_tensor(cand[:, :], prefix[:, :], bit[:, :], ALU.bitwise_or).then_inc(done, 1)
                        as_value(k + 1)
                        v.wait_ge(done, k + 3)
                        v.tensor_scalar(over[:, :], logits[:, :], value[:, :].bitcast(F32), None, ALU.is_ge).then_inc(done, 1)
                        v.wait_ge(done, k + 4)
                        v.tensor_reduce(count[:, :], over[:, :], AX.X, ALU.add).then_inc(counted, 1)
                        v.wait_ge(total, i + 1)
                        v.tensor_scalar(taken[:, :], psC, float(KEEP), -1.0, ALU.is_ge, ALU.mult).then_inc(done, 1)
                        v.wait_ge(done, k + 5)
                        v.tensor_tensor(taken[:, :], taken[:, :], bit[:, :], ALU.bitwise_and).then_inc(done, 1)
                        v.wait_ge(done, k + 6)
                        v.tensor_tensor(prefix[:, :], prefix[:, :], taken[:, :], ALU.bitwise_or).then_inc(done, 1)
                        v.tensor_scalar(bit[:, :], bit[:, :], 1, None, ALU.logical_shift_right).then_inc(done, 1)
                    k = 32 * (OPS - 1) + 2
                    v.wait_ge(done, k)
                    v.tensor_copy(cand[:, :], prefix[:, :]).then_inc(done, 1)
                    as_value(k + 1)
                    v.wait_ge(done, k + 3)
                    threshold = value[:, :].bitcast(F32)
                    v.tensor_scalar(over[:, :], logits[:, :], threshold, None, ALU.is_gt).then_inc(done, 1)
                    v.wait_ge(done, k + 4)
                    v.tensor_reduce(count[:, :], over[:, :], AX.X, ALU.add).then_inc(counted, 1)
                    v.tensor_scalar(same[:, :], logits[:, :], threshold, None, ALU.is_equal).then_inc(counted, 1)
                    v.wait_ge(total, 33)
                    v.tensor_scalar(left_over[:, :], psC, -1.0, float(KEEP), ALU.mult, ALU.add).then_inc(done, 1)
                    v.wait_ge(total, 34)
                    v.tensor_tensor_scan(before[:, :], psA, zeros[:, :], 0.0, ALU.add, ALU.add).then_inc(done, 1)
                    v.wait_ge(done, k + 6)
                    v.tensor_tensor(rank[:, :], before[:, :], psA, ALU.subtract).then_inc(done, 1)
                    v.wait_ge(done, k + 7)
                    v.tensor_tensor(rank[:, :], rank[:, :], psU, ALU.add).then_inc(done, 1)
                    v.wait_ge(done, k + 8)
                    v.scalar_tensor_tensor(out=same[:, :], in0=rank[:, :], scalar=left_over[:, :], in1=same[:, :],
                                           op0=ALU.is_le, op1=ALU.mult).then_inc(done, 1)
                    v.wait_ge(done, k + 9)
                    v.tensor_tensor(over[:, :], over[:, :], same[:, :], ALU.add).then_inc(done, 1)
                    v.wait_ge(done, k + 10)
                    v.tensor_tensor(logits[:, :], logits[:, :], over[:, :], ALU.mult).then_inc(done, 1)
        end_stage()

        with ExitStack() as st:
            EXT = D + 2 * HEADS
            wp = at(st, "s5_wp", [P, HALVES, EXT])
            att = at(st, "s5_att", [P, 2, D])
            terms = at(st, "s5_terms", [P, HALVES, 2, D])
            mid = at(st, "s5_mid", [P, 2, 2 * D])
            x2 = at(st, "s5_x2", [P, 2, D])
            stat = at(st, "s5_stat", [P, 2, 6])
            mv = at(st, "s5_mv", [P, 2, 2])
            ve = at(st, "s5_ve", [P, 2, 1])
            rstd = at(st, "s5_rstd", [P, 2, 1])
            h = at(st, "s5_h", [P, 2, D])
            hT = at(st, "s5_hT", [P, 2, HALVES, P])
            xp = at(st, "s5_xp", [P, 2, D])
            head_logits = at(st, "s5_head_logits", [P, NT, 2 * HEADS])
            psH = [bank(st, f"s5_psH{b}", HALVES, P) for b in range(2)]
            psP = [bank(st, f"s5_psP{b}", EXT) for b in range(2)]
            w_in, w_done, mid_in = sem("s5_w_in"), sem("s5_w_done"), [sem(f"s5_mid_in{b}") for b in range(2)]
            x2_done, stats_done, stats_seen, moments, rstd_step = sem("s5_x2_done"), sem("s5_stats"), sem("s5_stats_seen"), sem("s5_moments"), sem("s5_rstd_step")
            normed, turned, hT_ready, product = sem("s5_normed"), sem("s5_turned"), sem("s5_hT_ready"), sem("s5_product")
            xp_done, logits_go, logits_done, logits_out = sem("s5_xp_done"), sem("s5_logits_go"), sem("s5_logits_done"), sem("s5_logits_out")
            x2_out, xp_out = ([sem(f"s5_{n}_out{b}") for b in range(2)] for n in ("x2", "xp"))
            with nc.Block() as block:
                @block.sync
                def _(sp):
                    def load(t, b):
                        sp.dma_start(mid[:, b, :], mid_rows[ds(t * P, P), :]).then_inc(mid_in[b], 16)

                    def step(t, i, b, left):
                        sp.wait_ge(x2_done, t + 1)
                        if left == 2:
                            load(t + 2, b)
                        sp.dma_start(x2_rows[ds(t * P, P), :], x2[:, b, :]).then_inc(x2_out[b], 16)

                    load(0, 0)
                    load(1, 1)
                    sp.dma_start(wp[:, :, 0:D], a["att_w"]).then_inc(w_in, 16)
                    sp.dma_start(att[:, :, :], a["att"].broadcast_to([P, 2 * D]).rearrange("p (s c) -> p s c", s=2)).then_inc(w_in, 16)
                    by_tiles(sp, step)
                    sp.wait_ge(logits_done, NT)
                    sp.dma_start(logit_table.rearrange("(p t) c -> p t c", p=P), head_logits[:, :, :]).then_inc(logits_out, 16)
                    sp.wait_ge(logits_out, 16)
                    for b in range(2):
                        sp.wait_ge(x2_out[b], 16 * PAIRS)

                @block.gpsimd
                def _(pool):
                    def step(t, i, b, left):
                        pool.wait_ge(moments, t + 1)
                        pool.tensor_tensor(ve[:, b, :], mv[:, b, 1:2], eps[:, :], ALU.add).then_inc(rstd_step, 1)
                        pool.wait_ge(rstd_step, 2 * t + 1)
                        pool.tensor_tensor(rstd[:, b, :], ve[:, b, :], neg_half[:, :], ALU.pow).then_inc(rstd_step, 1)

                    by_tiles(pool, step)

                @block.scalar
                def _(act):
                    def copy_hT(t, b):
                        act.wait_ge(turned, t + 1)
                        act.activation(hT[:, b, :, :], psH[b], ACT.Copy).then_inc(hT_ready, 1)

                    def step(t, i, b, left):
                        if left:
                            copy_hT(t + 1, 1 - b)
                        act.wait_ge(product, t + 1)
                        wait_past(act, xp_out[b], 16 * i)
                        act.activation(xp[:, b, :], psP[b][:, 0:D], ACT.Copy).then_inc(xp_done, 1)
                        act.sem_inc(logits_go, 1)
                        act.activation(head_logits[:, ds(t, 1), :].rearrange("p o c -> p (o c)"), psP[b][:, D:EXT], ACT.Copy).then_inc(logits_done, 1)
                        act.wait_ge(xp_done, t + 1)
                        act.dma_start(xp_table[ds(t * P, P), :], xp[:, b, :]).then_inc(xp_out[b], 16)

                    copy_hT(0, 0)
                    by_tiles(act, step)
                    for b in range(2):
                        act.wait_ge(xp_out[b], 16 * PAIRS)

                @block.tensor
                def _(pe):
                    def turn(t, b):
                        pe.wait_ge(normed, t + 1)
                        for k in range(HALVES):
                            mm = pe.transpose(psH[b][:, k, :], h[:, b, k * P:(k + 1) * P], ident[:, :])
                        mm.then_inc(turned, 1)

                    def step(t, i, b, left):
                        if left:
                            turn(t + 1, 1 - b)
                        pe.wait_ge(hT_ready, t + 1)
                        wait_past(pe, logits_done, t)
                        for k in range(HALVES):
                            mm = pe.matmul(psP[b], hT[:, b, k, :], wp[:, k, :], start=(k == 0), stop=(k == HALVES - 1))
                        mm.then_inc(product, 1)

                    pe.wait_ge(w_done, 2)
                    turn(0, 0)
                    by_tiles(pe, step)

                @block.vector
                def _(v):
                    def mix(t, i, b):
                        v.wait_ge(mid_in[b], 16 * i + 16)
                        wait_past(v, x2_out[b], 16 * i)
                        v.scalar_tensor_tensor(out=x2[:, b, :], in0=mid[:, b, D:2 * D], scalar=logits[:, ds(t, 1)], in1=mid[:, b, 0:D],
                                               op0=ALU.mult, op1=ALU.add).then_inc(x2_done, 1)

                    def moment(t, b):
                        v.wait_ge(x2_done, t + 1)
                        v.bn_stats(stat[:, b, :], x2[:, b, :]).then_inc(stats_done, 1)
                        v.wait_ge(stats_done, t + 1)
                        v.sem_inc(stats_seen, 1)
                        v.bn_aggr(mv[:, b, :], stat[:, b, :]).then_inc(moments, 1)

                    def step(t, i, b, left):
                        if left:
                            mix(t + 1, i + b, 1 - b)
                        v.wait_ge(rstd_step, 2 * t + 2)
                        wait_past(v, turned, t - 1)
                        v.tensor_scalar(h[:, b, :], x2[:, b, :], mv[:, b, 0:1], rstd[:, b, :],
                                        ALU.subtract, ALU.mult).then_inc(normed, 1)
                        if left:
                            moment(t + 1, 1 - b)

                    mix(0, 0, 0)
                    moment(0, 0)
                    v.wait_ge(w_in, 32)
                    v.tensor_tensor(terms[:, :, :, :], wp[:, :, 0:D].unsqueeze(2).broadcast_to([P, HALVES, 2, D]),
                                    att[:, :, :].unsqueeze(1).broadcast_to([P, HALVES, 2, D]), ALU.mult).then_inc(w_done, 1)
                    v.wait_ge(w_done, 1)
                    v.tensor_reduce(wp[:, :, D:EXT], terms[:, :, :, :].rearrange("p k s (h c) -> p k (s h) c", h=HEADS),
                                    AX.X, ALU.add).then_inc(w_done, 1)
                    by_tiles(v, step)

        end_stage()

        chans = ExitStack()
        CHANS = 2 * HEADS + 1 + HEADS
        share = at(chans, "share", [P, CHUNKS, HEADS])
        chan = at(chans, "chan", [P, CHANS, ROW])
        SRC, DST, LOOP, TOP = 0, HEADS, 2 * HEADS, 2 * HEADS + 1
        source = at(chans, "s6_source", [P, ROW], I32)
        with ExitStack() as st:
            staged = at(st, "s6_staged", [P, U], I32)
            place = at(st, "s6_place", [P, ROW], I32)
            tile = at(st, "s6_tile", [P, ROW], I32)
            got = at(st, "s6_got", [P, U, 2 * HEADS])
            src_in, place_step = sem("s6_src_in"), sem("s6_place_step")
            idx_taken, idx_ready, idx_seen, keep_go, kept = sem("s6_idx_taken"), sem("s6_idx_ready"), sem("s6_idx_seen"), sem("s6_keep_go"), sem("s6_kept")
            gathered = [sem(f"s6_gathered{s}") for s in range(U)]
            with nc.Block() as block:
                @block.sync
                def _(sp):
                    sp.dma_start(source[:, :], a["src_row"]).then_inc(src_in, 16)
                    sp.wait_ge(src_in, 16)

                @block.vector
                def _(v):
                    v.wait_ge(src_in, 16)
                    v.tensor_scalar(tile[:, :], source[:, :], P.bit_length() - 1, None, ALU.logical_shift_right).then_inc(place_step, 1)
                    v.tensor_scalar(place[:, :], source[:, :], P - 1, None, ALU.bitwise_and).then_inc(place_step, 1)
                    v.wait_ge(place_step, 2)
                    v.scalar_tensor_tensor(out=place[:, :], in0=place[:, :], scalar=float(NT), in1=tile[:, :],
                                           op0=ALU.mult, op1=ALU.add).then_inc(place_step, 1)

                @block.scalar
                def _(act):
                    act.wait_ge(place_step, 3)
                    for g in range(U // GRP):
                        act.activation(staged[:, g * GRP:(g + 1) * GRP], place[:, g * GRP:(g + 1) * GRP], ACT.Copy).then_inc(idx_ready, 1)

                    def keep(i, g):
                        for s in range(g * GRP, (g + 1) * GRP):
                            act.wait_ge(gathered[s], 16 * i + 16)
                        act.sem_inc(keep_go, 1)
                        act.activation(chan[:, SRC:SRC + 2 * HEADS, ds(i * U + g * GRP, GRP)].rearrange("p c s -> p s c"),
                                       got[:, g * GRP:(g + 1) * GRP, :], ACT.Copy).then_inc(kept, 1)

                    with act.Fori(0, ITER - 1) as i:
                        for g in range(U // GRP):
                            keep(i, g)
                            act.sem_inc(idx_taken, 1)
                            act.activation(staged[:, g * GRP:(g + 1) * GRP], place[:, ds(i * U + U + g * GRP, GRP)],
                                           ACT.Copy).then_inc(idx_ready, 1)
                    for g in range(U // GRP):
                        keep(ITER - 1, g)

                @block.gpsimd
                def _(pool):
                    def gathers(i, g, first_pass):
                        if not first_pass:
                            pool.wait_ge(kept, U // GRP * i - U // GRP + g + 1)
                        pool.wait_ge(idx_ready, U // GRP * i + g + 1)
                        pool.sem_inc(idx_seen, 1)
                        for s in range(g * GRP, (g + 1) * GRP):
                            pool.indirect_dma_start(
                                out=got[:, s, :], out_offset=None, in_=logit_table[:, :],
                                in_offset=bass.IndirectOffsetOnAxis(ap=staged[:, s:s + 1], axis=0),
                            ).then_inc(gathered[s], 16)

                    for g in range(U // GRP):
                        gathers(0, g, True)
                    with pool.Fori(1, ITER) as i:
                        for g in range(U // GRP):
                            gathers(i, g, False)

        end_stage()

        with ExitStack() as st:
            ends = at(st, "s7_ends", [P, ROW], I32)
            before = at(st, "s7_before", [P, ROW], I32)
            after = at(st, "s7_after", [P, ROW], I32)
            edge_i = at(st, "s7_edge_i", [P, ROW], I32)
            goes_on = at(st, "s7_goes_on", [P, ROW])
            more = at(st, "s7_more", [P, ROW])
            cut = at(st, "s7_cut", [P, ROW])
            last = at(st, "s7_last", [P, ROW])
            loop = at(st, "s7_loop", [P, ROW])
            spare = at(st, "s7_spare", [P, ROW])
            MAXES = HEADS + 1 + HEADS
            whole = at(st, "s7_whole", [P, 2])
            border = at(st, "s7_border", [P, 2, MAXES])
            rowwise = at(st, "s7_rowwise", [MAXES, 2, P])
            carry = at(st, "s7_carry", [MAXES, P + 1])
            start = at(st, "s7_start", [P, MAXES])
            psB = [bank(st, f"s7_psB{k}", P) for k in range(2)]
            psS = bank(st, "s7_psS", MAXES)
            psW = [bank(st, f"s7_psW{k}", P) for k in range(2)]
            ends_in, edge_made, share_out = sem("s7_ends_in"), sem("s7_edge_made"), sem("s7_share_out")
            step_done = sem("s7_step_done")
            border_ready, border_turned, carry_ready, carry_turned = sem("s7_border_ready"), sem("s7_border_turned"), sem("s7_carry_ready"), sem("s7_carry_turned")
            scores_ready, exp_done, shares_ready, share_turned, share_kept = sem("s7_scores_ready"), sem("s7_exp_done"), sem("s7_shares_ready"), sem("s7_share_turned"), sem("s7_share_kept")
            TURNS = (MAXES, MAXES, HEADS, HEADS)
            with nc.Block() as block:
                @block.sync
                def _(sp):
                    sp.dma_start(ends[:, :], a["dst_row"]).then_inc(ends_in, 16)
                    sp.dma_start(before[:, :], a["dst_before"]).then_inc(ends_in, 16)
                    sp.dma_start(after[:, :], a["dst_after"]).then_inc(ends_in, 16)
                    sp.wait_ge(share_kept, KR * HEADS)
                    sp.dma_start(share_rows, share[:, :, :]).then_inc(share_out, 16)
                    sp.wait_ge(share_out, 16)

                @block.gpsimd
                def _(pool):
                    pool.iota(edge_i[:, :], pattern=[[1, ROW]], base=0, channel_multiplier=ROW).then_inc(edge_made, 1)

                @block.scalar
                def _(act):
                    act.wait_ge(scores_ready, 1)
                    act.activation(chan[:, TOP:TOP + HEADS, :], chan[:, SRC:SRC + HEADS, :], ACT.Exp).then_inc(exp_done, 1)

                @block.tensor
                def _(pe):
                    for e, n in enumerate(TURNS):
                        pe.wait_ge(border_ready, e + 1)
                        for k in range(2):
                            mm = pe.transpose(psB[k][0:n, :], border[:, k, 0:n], ident[:, :])
                        mm.then_inc(border_turned, 1)
                        pe.wait_ge(carry_ready, e + 1)
                        shift = e % 2
                        pe.transpose(psS[:, 0:n], carry[0:n, shift:shift + P], ident[0:n, 0:n]).then_inc(carry_turned, 1)
                    pe.wait_ge(shares_ready, 1)
                    for j in range(KR * HEADS):
                        k, hd = j // HEADS, j % HEADS
                        if j >= 2:
                            pe.wait_ge(share_kept, j - 1)
                        pe.transpose(psW[j % 2], chan[:, TOP + hd, k * P:(k + 1) * P], ident[:, :]).then_inc(share_turned, 1)

                @block.vector
                def _(v):
                    count = [0]

                    def then(ins):
                        count[0] += 1
                        ins.then_inc(step_done, 1)
                        v.wait_ge(step_done, count[0])

                    def exchange(e, values, largest):
                        n, back = TURNS[e], e % 2
                        order = slice(None, None, -1 if back else 1)
                        then(v.tensor_copy(border[:, 1, 0:n], whole[:, back:back + 1].broadcast_to([P, n])))
                        v.tensor_copy(border[:, 0, 0:n], values).then_inc(border_ready, 1)
                        v.wait_ge(border_turned, e + 1)
                        then(v.tensor_copy(rowwise[0:n, 0, :], psB[0][0:n, :]))
                        if largest:
                            then(v.tensor_scalar(rowwise[0:n, 1, :], psB[1][0:n, :], 1.0, BIG, ALU.subtract, ALU.mult))
                        else:
                            then(v.tensor_copy(rowwise[0:n, 1, :], psB[1][0:n, :]))
                        none = -BIG if largest else 0.0
                        outside = slice(P, P + 1) if back else slice(0, 1)
                        inside = slice(0, P) if back else slice(1, P + 1)
                        then(v.memset(carry[0:n, outside], none))
                        v.tensor_tensor_scan(carry[0:n, inside][:, order], rowwise[0:n, 1, order], rowwise[0:n, 0, order], none,
                                             ALU.add if largest else ALU.mult, ALU.max if largest else ALU.add).then_inc(carry_ready, 1)
                        v.wait_ge(carry_turned, e + 1)
                        then(v.tensor_copy(start[:, 0:n], psS[:, 0:n]))

                    def to_all(e, c0, n):
                        each = chan[:, c0:c0 + n, :]
                        then(v.tensor_tensor(each, each, last[:, :].unsqueeze(1).broadcast_to([P, n, ROW]), ALU.mult))
                        for c in range(n):
                            then(v.tensor_tensor_scan(spare[:, ::-1], more[:, ::-1], chan[:, c0 + c, ::-1], 0.0, ALU.mult, ALU.add))
                            then(v.tensor_copy(border[:, 0, c:c + 1], spare[:, 0:1]))
                        exchange(e, border[:, 0, 0:n], False)
                        for c in range(n):
                            then(v.tensor_tensor_scan(chan[:, c0 + c, ::-1], more[:, ::-1], chan[:, c0 + c, ::-1], start[:, c:c + 1], ALU.mult, ALU.add))

                    v.wait_ge(ends_in, 48)
                    v.wait_ge(edge_made, 1)
                    then(v.tensor_tensor(goes_on[:, :], ends[:, :], before[:, :], ALU.is_equal))
                    then(v.tensor_tensor(more[:, :], ends[:, :], after[:, :], ALU.is_equal))
                    then(v.tensor_tensor(loop[:, :], source[:, :], ends[:, :], ALU.is_equal))
                    then(v.tensor_reduce(whole[:, 0:1], goes_on[:, :], AX.X, ALU.min))
                    then(v.tensor_reduce(whole[:, 1:2], more[:, :], AX.X, ALU.min))
                    then(v.tensor_scalar(cut[:, :], goes_on[:, :], 1.0, BIG, ALU.subtract, ALU.mult))
                    then(v.tensor_scalar(last[:, :], more[:, :], -1.0, 1.0, ALU.mult, ALU.add))

                    def loops(c0, n):
                        return loop[:, :].unsqueeze(1).broadcast_to([P, n, ROW])

                    then(v.tensor_scalar(spare[:, :], loop[:, :], 1.0, BIG, ALU.subtract, ALU.mult))
                    each = chan[:, DST:DST + HEADS, :]
                    then(v.tensor_tensor(each, each, loops(DST, HEADS), ALU.mult))
                    then(v.tensor_tensor(each, each, spare[:, :].unsqueeze(1).broadcast_to([P, HEADS, ROW]), ALU.add))

                    def loop_place(to):
                        then(v.tensor_tensor(to, edge_i[:, :], loop[:, :], ALU.mult))
                        then(v.tensor_tensor(to, spare[:, :], to, ALU.subtract))

                    loop_place(chan[:, LOOP, :])
                    for c in range(HEADS):
                        then(v.tensor_tensor_scan(chan[:, TOP + c, :], cut[:, :], chan[:, SRC + c, :], -BIG, ALU.add, ALU.max))
                    for c in range(HEADS + 1):
                        then(v.tensor_tensor_scan(chan[:, DST + c, :], cut[:, :], chan[:, DST + c, :], -BIG, ALU.add, ALU.max))
                    exchange(0, chan[:, DST:DST + MAXES, ROW - 1:ROW].rearrange("p c o -> p (c o)"), True)
                    for c in range(MAXES):
                        then(v.tensor_tensor_scan(chan[:, DST + c, :], cut[:, :], chan[:, DST + c, :], start[:, c:c + 1], ALU.add, ALU.max))
                    to_all(1, DST, MAXES)
                    scores, dst_logits, tops = (chan[:, c:c + HEADS, :] for c in (SRC, DST, TOP))
                    for each in (scores, tops):
                        then(v.tensor_tensor(each, each, dst_logits, ALU.add))
                        for c in range(HEADS):
                            one = each[:, c, :]
                            then(v.scalar_tensor_tensor(out=one, in0=one, scalar=0.2, in1=one, op0=ALU.mult, op1=ALU.max))
                    v.tensor_tensor(scores, scores, tops, ALU.subtract).then_inc(scores_ready, 1)
                    v.wait_ge(scores_ready, 1)
                    then(v.tensor_scalar(spare[:, :], loop[:, :], 1.0, BIG, ALU.subtract, ALU.mult))
                    loop_place(cut[:, :])
                    then(v.tensor_tensor(cut[:, :], cut[:, :], chan[:, LOOP, :], ALU.is_equal))
                    then(v.tensor_tensor(cut[:, :], cut[:, :], loop[:, :], ALU.mult))
                    then(v.tensor_scalar(cut[:, :], cut[:, :], 1.0, None, ALU.add))
                    v.wait_ge(exp_done, 1)
                    then(v.tensor_tensor(tops, tops, cut[:, :].unsqueeze(1).broadcast_to([P, HEADS, ROW]), ALU.mult))
                    for c in range(HEADS):
                        then(v.tensor_tensor_scan(chan[:, DST + c, :], goes_on[:, :], chan[:, TOP + c, :], 0.0, ALU.mult, ALU.add))
                    exchange(2, chan[:, DST:DST + HEADS, ROW - 1:ROW].rearrange("p c o -> p (c o)"), False)
                    for c in range(HEADS):
                        then(v.tensor_tensor_scan(chan[:, DST + c, :], goes_on[:, :], chan[:, TOP + c, :], start[:, c:c + 1], ALU.mult, ALU.add))
                    to_all(3, DST, HEADS)
                    then(v.reciprocal(dst_logits, dst_logits))
                    v.tensor_tensor(tops, tops, dst_logits, ALU.mult).then_inc(shares_ready, 1)
                    by_chunk = share[:, :, :].rearrange("q (p k) h -> q p k h", k=KR)
                    for j in range(KR * HEADS):
                        k, hd = j // HEADS, j % HEADS
                        v.wait_ge(share_turned, j + 1)
                        v.tensor_copy(by_chunk[:, :, k, hd], psW[j % 2]).then_inc(share_kept, 1)
        chans.close()
        end_stage()

        sums = at(ctx, "sums8", [P, HALVES, ACC])
        with ExitStack() as st:
            share = at(st, "s8_share", [P, CHUNKS, HEADS])
            first = at(st, "s8_first", [1, SPANS // 2 + 1], I32)
            alone = at(st, "s8_alone", [1, SPANS + 1], I32)
            first_all = at(st, "s8_first_all", [P, SPANS], I32)
            index = at(st, "s8_index", [P, CHUNKS], I32)
            local = at(st, "s8_local", [P, CHUNKS])
            ends = at(st, "s8_ends", [P, CHUNKS], I32)
            edges_in, edges_ready = sem("s8_edges_in"), sem("s8_edges_ready")
            with nc.Block() as block:
                @block.sync
                def _(sp):
                    sp.dma_start(alone[:, :], a["dst_first"]).then_inc(edges_in, 16)
                    sp.dma_start(first_all[:, :], a["dst_first"][0:1, 1:SPANS + 1].broadcast_to([P, SPANS])).then_inc(edges_in, 16)
                    sp.dma_start(index[:, :], a["src_chunk"]).then_inc(edges_in, 16)
                    sp.dma_start(ends[:, :], a["dst_chunk"]).then_inc(edges_in, 16)
                    sp.dma_start(share[:, :, :], share_rows).then_inc(edges_in, 16)
                    sp.wait_ge(edges_in, 16 * 5)

                @block.vector
                def _(v):
                    v.wait_ge(edges_in, 16 * 5)
                    pair_up(v, first, alone, edges_ready)
                    v.tensor_tensor(local[:, :].rearrange("p (d j) -> p d j", j=SPAN),
                                    first_all[:, :].unsqueeze(2).broadcast_to([P, SPANS, SPAN]),
                                    ends[:, :].rearrange("p (d j) -> p d j", j=SPAN), ALU.subtract).then_inc(edges_ready, 1)
            aggregate("s8", xp_table, sums, index, local, first, share, True)
        end_stage()

        w1_b1 = at(ctx, "exp_w1_b1", [P, X, HALVES * H1 + H1 // P])
        w2 = at(ctx, "exp_w2", [P, X, H1 // P * D])
        b2 = at(ctx, "exp_b2", [P, X, D])
        slots = at(ctx, "slots", [P, NT, 2], I32)
        tile_row = at(ctx, "tile_row", [1, TILES], I32)
        tile_exp = at(ctx, "tile_exp", [1, TILES], I32)
        scores_of = ExitStack()
        base = at(scores_of, "base", [P, X])
        count = at(scores_of, "count", [P, X])
        mask_all = at(scores_of, "mask_all", [P, NT, X])
        place_all = at(scores_of, "place_all", [P, NT, X])
        exp_in = sem("exp_in")
        with ExitStack() as st:
            wg = at(st, "s9_wg", [P, HALVES, X])
            bg = at(st, "s9_bg", [P, X])
            bias = at(st, "s9_bias", [P, D])
            x2 = at(st, "s9_x2", [P, 2, D])
            fixed = at(st, "s9_fixed", [P, 2, HALVES, P])
            z = at(st, "s9_z", [P, 2, D])
            part = at(st, "s9_part", [P, 2, D])
            below = at(st, "s9_below", [P, 2, D])
            x3 = at(st, "s9_x3", [P, 2, D])
            stat = at(st, "s9_stat", [P, 2, 6])
            mv = at(st, "s9_mv", [P, 2, 2])
            ve = at(st, "s9_ve", [P, 2, 1])
            rstd = at(st, "s9_rstd", [P, 2, 1])
            h = at(st, "s9_h", [P, 2, D])
            hT = at(st, "s9_hT", [P, 2, HALVES, P])
            lower_i = at(st, "s9_lower_i", [P, X, X], I32)
            lower = at(st, "s9_lower", [P, X, X])
            upto = at(st, "s9_upto", [P, P])
            base_i = at(st, "s9_base_i", [P, X], I32)
            gate = at(st, "s9_gate", [P, 2, X])
            wins = at(st, "s9_wins", [P, 2, X, X])
            ties = at(st, "s9_ties", [P, 2, X, X])
            rank = at(st, "s9_rank", [P, 2, X])
            mask = at(st, "s9_mask", [P, 2, X])
            place = at(st, "s9_place", [P, 2, X])
            both = at(st, "s9_both", [P, 2, 1])
            second = at(st, "s9_second", [P, 2, 1])
            staged = at(st, "s9_staged", [P, 2, 2], I32)
            moved = at(st, "s9_moved", [P, 2, D])
            psX = [bank(st, f"s9_psX{b}", D) for b in range(2)]
            psC = [bank(st, f"s9_psC{b}", 2 * X) for b in range(2)]
            psH = [bank(st, f"s9_psH{b}", HALVES, P) for b in range(2)]
            psR = [bank(st, f"s9_psR{b}", X) for b in range(2)]
            w_in, x_in, x3_out = sem("s9_w_in"), [sem(f"s9_x_in{b}") for b in range(2)], [sem(f"s9_x3_out{b}") for b in range(2)]
            held_go, held, unturned, z_done, below_done, exp_done = (sem(f"s9_{n}") for n in ("held_go", "held", "unturned", "z_done", "below_done", "exp_done"))
            ranked, rank_go, order_go = sem("s9_ranked"), sem("s9_rank_go"), sem("s9_order_go")
            part_done, x3_done, stats_done, stats_seen, moments, rstd_step = (sem(f"s9_{n}") for n in ("part_done", "x3_done", "stats", "stats_seen", "moments", "rstd_step"))
            normed, turned, hT_ready, scored, gated = (sem(f"s9_{n}") for n in ("normed", "turned", "hT_ready", "scored", "gated"))
            kept, kept_go, const_i, const = sem("s9_kept"), sem("s9_kept_go"), sem("s9_const_i"), sem("s9_const")
            compared, ordered, masked, counted, place_step, placed, scatter_go = (sem(f"s9_{n}") for n in ("compared", "ordered", "masked", "counted", "place_step", "placed", "scatter_go"))
            noted_go, moved_done = sem("s9_noted_go"), sem("s9_moved_done")
            scattered = [sem(f"s9_scattered{b}") for b in range(2)]
            with nc.Block() as block:
                @block.sync
                def _(sp):
                    def load(t, b):
                        sp.dma_start(x2[:, b, :], x2_rows[ds(t * P, P), :]).then_inc(x_in[b], 16)

                    def step(t, i, b, left):
                        if left == 2:
                            sp.wait_ge(part_done, t + 1)
                            load(t + 2, b)
                        sp.wait_ge(x3_done, t + 1)
                        sp.dma_start(x3_rows[ds(t * P, P), :], x3[:, b, :]).then_inc(x3_out[b], 16)

                    load(0, 0)
                    load(1, 1)
                    sp.dma_start(bias[:, :], a["att_bias"].broadcast_to([P, D])).then_inc(w_in, 16)
                    sp.dma_start(wg[:, :, :], a["gate_w"]).then_inc(w_in, 16)
                    sp.dma_start(bg[:, :], a["gate_b"].broadcast_to([P, X])).then_inc(w_in, 16)
                    sp.dma_start(w1_b1[:, :, :], a["exp_w1_b1"]).then_inc(exp_in, 16)
                    sp.dma_start(w2[:, :, :], a["exp_w2"]).then_inc(exp_in, 16)
                    sp.dma_start(b2[:, :, :].rearrange("p x d -> p (x d)"), a["exp_b2"].broadcast_to([P, X * D])).then_inc(exp_in, 16)
                    by_tiles(sp, step, peel=3)
                    for b in range(2):
                        sp.wait_ge(x3_out[b], 16 * PAIRS)

                @block.gpsimd
                def _(pool):
                    def step(t, i, b, left):
                        pool.wait_ge(moments, t + 1)
                        pool.tensor_tensor(ve[:, b, :], mv[:, b, 1:2], eps[:, :], ALU.add).then_inc(rstd_step, 1)
                        pool.wait_ge(rstd_step, 2 * t + 1)
                        pool.tensor_tensor(rstd[:, b, :], ve[:, b, :], neg_half[:, :], ALU.pow).then_inc(rstd_step, 1)
                        if not isinstance(t, int) or t > 1:
                            order(t - 2, b)
                        if not isinstance(t, int) or t > 4:
                            scatter(t - 5, 1 - b)

                    def order(t, b):
                        pool.wait_ge(compared, 2 * t + 2)
                        pool.sem_inc(order_go, 1)
                        pool.tensor_tensor(ties[:, b, :, :], ties[:, b, :, :], lower[:, :, :], ALU.mult).then_inc(ordered, 1)
                        pool.wait_ge(ordered, 2 * t + 1)
                        pool.tensor_tensor(wins[:, b, :, :], wins[:, b, :, :], ties[:, b, :, :], ALU.add).then_inc(ordered, 1)

                    def scatter(t, b):
                        pool.wait_ge(moved_done, 2 * t + 2)
                        pool.sem_inc(scatter_go, 1)
                        for j in range(2):
                            pool.indirect_dma_start(out=exp_rows[:, :], in_=moved[:, b, :], in_offset=None,
                                                    out_offset=bass.IndirectOffsetOnAxis(ap=staged[:, b, j:j + 1], axis=0)).then_inc(scattered[b], 16)

                    pool.iota(lower_i[:, :, :], pattern=[[1, X], [-1, X]], base=0, channel_multiplier=0).then_inc(const_i, 1)
                    pool.iota(base_i[:, :], pattern=[[CAP, X]], base=0, channel_multiplier=0).then_inc(const_i, 1)
                    pool.affine_select(out=upto[:, :], in_=ones[:, :], compare_op=ALU.is_gt, fill=0.0,
                                       base=0, pattern=[[1, P]], channel_multiplier=-1).then_inc(const_i, 1)
                    pool.wait_ge(const, 3)
                    by_tiles(pool, step, peel=3)
                    for t in range(NT - 2, NT):
                        order(t, t % 2)
                    for t in range(NT - 5, NT):
                        scatter(t, t % 2)
                    for b in range(2):
                        pool.wait_ge(scattered[b], 32 * PAIRS)

                @block.scalar
                def _(act):
                    def hold(t, b):
                        act.sem_inc(held_go, 1)
                        act.activation(fixed[:, b, :, :], sums[:, :, ds(t * P, P)], ACT.Copy).then_inc(held, 1)

                    def exp_below(t, b):
                        act.wait_ge(z_done, t + 1)
                        wait_past(act, x3_done, t - 1)
                        act.activation(below[:, b, :], z[:, b, :], ACT.Relu, scale=-1.0).then_inc(below_done, 1)
                        act.wait_ge(below_done, t + 1)
                        act.activation(below[:, b, :], below[:, b, :], ACT.Exp, scale=-1.0).then_inc(exp_done, 1)

                    def step(t, i, b, left):
                        if left == 2:
                            act.wait_ge(unturned, t + 1)
                            hold(t + 2, b)
                        if left:
                            exp_below(t + 1, 1 - b)
                        act.wait_ge(turned, t + 1)
                        wait_past(act, scored, t - 1)
                        act.activation(hT[:, b, :, :], psH[b], ACT.Copy).then_inc(hT_ready, 1)
                        act.wait_ge(normed, t + 1)
                        act.wait_ge(held, t + 1)
                        act.sem_inc(kept_go, 1)
                        act.activation(sums[:, :, ds(t * P, P)], h[:, b, :].rearrange("p (k c) -> p k c", k=HALVES), ACT.Copy).then_inc(kept, 1)
                        if not isinstance(t, int) or t > 3:
                            move(t - 4, i - 2, b)

                    def move(t, i, b):
                        act.wait_ge(kept, t + 1)
                        act.wait_ge(placed, t + 1)
                        wait_past(act, scattered[b], 32 * i)
                        act.sem_inc(kept_go, 1)
                        act.activation(staged[:, b, :], slots[:, ds(t, 1), :].rearrange("p o j -> p (o j)"), ACT.Copy).then_inc(moved_done, 1)
                        act.activation(moved[:, b, :].rearrange("p (k c) -> p k c", k=HALVES), sums[:, :, ds(t * P, P)], ACT.Copy).then_inc(moved_done, 1)

                    hold(0, 0)
                    hold(1, 1)
                    exp_below(0, 0)
                    by_tiles(act, step, peel=3)
                    for t in range(NT - 4, NT):
                        move(t, t // 2, t % 2)

                @block.tensor
                def _(pe):
                    def unturn(t, b):
                        pe.wait_ge(held, t + 1)
                        for k in range(HALVES):
                            mm = pe.transpose(psX[b][:, k * P:(k + 1) * P], fixed[:, b, k, :], ident[:, :])
                        mm.then_inc(unturned, 1)

                    def number(t, b):
                        pe.wait_ge(masked, t + 1)
                        pe.matmul(psC[b][:, 0:X], upto[:, :], mask[:, b, :], start=True, stop=True)
                        pe.matmul(psC[b][:, X:2 * X], ones[:, :], mask[:, b, :], start=True, stop=True).then_inc(counted, 1)

                    def step(t, i, b, left):
                        if left == 2:
                            pe.wait_ge(z_done, t + 1)
                            unturn(t + 2, b)
                        pe.wait_ge(normed, t + 1)
                        wait_past(pe, hT_ready, t - 1)
                        for k in range(HALVES):
                            mm = pe.transpose(psH[b][:, k, :], h[:, b, k * P:(k + 1) * P], ident[:, :])
                        mm.then_inc(turned, 1)
                        pe.wait_ge(hT_ready, t + 1)
                        wait_past(pe, gated, t - 1)
                        for k in range(HALVES):
                            mm = pe.matmul(psR[b], hT[:, b, k, :], wg[:, k, :], start=(k == 0), stop=(k == HALVES - 1))
                        mm.then_inc(scored, 1)
                        if not isinstance(t, int) or t > 1:
                            number(t - 2, b)

                    unturn(0, 0)
                    unturn(1, 1)
                    pe.wait_ge(w_in, 48)
                    pe.wait_ge(const_i, 3)
                    by_tiles(pe, step, peel=3)
                    number(NT - 2, NT % 2)
                    number(NT - 1, (NT - 1) % 2)

                @block.vector
                def _(v):
                    def total(t, i, b):
                        v.wait_ge(unturned, t + 1)
                        v.tensor_tensor(z[:, b, :], psX[b], bias[:, :], ALU.add).then_inc(z_done, 1)

                    def positive(t, i, b):
                        v.wait_ge(x_in[b], 16 * i + 16)
                        v.wait_ge(z_done, t + 1)
                        v.scalar_tensor_tensor(out=part[:, b, :], in0=z[:, b, :], scalar=0.0, in1=x2[:, b, :],
                                               op0=ALU.max, op1=ALU.add).then_inc(part_done, 1)

                    def residual(t, i, b):
                        v.wait_ge(exp_done, t + 1)
                        v.wait_ge(part_done, t + 1)
                        wait_past(v, x3_out[b], 16 * i)
                        v.scalar_tensor_tensor(out=x3[:, b, :], in0=below[:, b, :], scalar=-1.0, in1=part[:, b, :],
                                               op0=ALU.add, op1=ALU.add).then_inc(x3_done, 1)

                    def stats(t, b):
                        v.wait_ge(x3_done, t + 1)
                        v.bn_stats(stat[:, b, :], x3[:, b, :]).then_inc(stats_done, 1)

                    def moment(t, b):
                        v.wait_ge(stats_done, t + 1)
                        v.sem_inc(stats_seen, 1)
                        v.bn_aggr(mv[:, b, :], stat[:, b, :]).then_inc(moments, 1)

                    def normalise(t, b):
                        v.wait_ge(rstd_step, 2 * t + 2)
                        wait_past(v, turned, t - 1)
                        wait_past(v, kept, t - 1)
                        v.tensor_scalar(h[:, b, :], x3[:, b, :], mv[:, b, 0:1], rstd[:, b, :],
                                        ALU.subtract, ALU.mult).then_inc(normed, 1)

                    def score(t, b):
                        v.wait_ge(scored, t + 1)
                        v.tensor_tensor(gate[:, b, :], psR[b], bg[:, :], ALU.add).then_inc(gated, 1)

                    def compare(t, b):
                        v.wait_ge(gated, t + 1)
                        other = gate[:, b, :].unsqueeze(1).broadcast_to([P, X, X])
                        own = gate[:, b, :].unsqueeze(2).broadcast_to([P, X, X])
                        v.tensor_tensor(ties[:, b, :, :], other, own, ALU.is_equal).then_inc(compared, 1)
                        v.tensor_tensor(wins[:, b, :, :], other, own, ALU.is_gt).then_inc(compared, 1)

                    def choose(t, b):
                        v.wait_ge(ordered, 2 * t + 2)
                        v.sem_inc(rank_go, 1)
                        v.tensor_reduce(rank[:, b, :], wins[:, b, :, :], AX.X, ALU.add).then_inc(ranked, 1)

                    def mark(t, b):
                        v.wait_ge(ranked, t + 1)
                        v.tensor_scalar(mask[:, b, :], rank[:, b, :], 2.0, None, ALU.is_lt).then_inc(masked, 1)
                        v.tensor_scalar(mask_all[:, ds(t, 1), :].rearrange("p o x -> p (o x)"), rank[:, b, :], 2.0, None, ALU.is_lt)

                    def assign(t, b):
                        v.wait_ge(counted, t + 1)
                        if not isinstance(t, int) or t > 0:
                            v.wait_ge(place_step, 5 * t)
                        v.tensor_tensor(place[:, b, :], psC[b][:, 0:X], count[:, :], ALU.add).then_inc(place_step, 1)

                    def count_on(t, b):
                        v.wait_ge(place_step, 5 * t + 1)
                        v.tensor_tensor(count[:, :], count[:, :], psC[b][:, X:2 * X], ALU.add).then_inc(place_step, 1)
                        v.tensor_copy(place_all[:, ds(t, 1), :].rearrange("p o x -> p (o x)"), place[:, b, :]).then_inc(place_step, 1)

                    def of_chosen(t, b):
                        v.wait_ge(place_step, 5 * t + 3)
                        v.tensor_tensor(place[:, b, :], place[:, b, :], mask[:, b, :], ALU.mult).then_inc(place_step, 1)

                    def two_places(t, b):
                        v.wait_ge(place_step, 5 * t + 4)
                        v.tensor_reduce(both[:, b, :], place[:, b, :], AX.X, ALU.add)
                        v.tensor_reduce(second[:, b, :], place[:, b, :], AX.X, ALU.max).then_inc(place_step, 1)

                    def note(t, b):
                        v.wait_ge(place_step, 5 * t + 5)
                        v.sem_inc(noted_go, 1)
                        v.tensor_copy(slots[:, ds(t, 1), 1], second[:, b, :])
                        v.tensor_tensor(slots[:, ds(t, 1), 0], both[:, b, :], second[:, b, :], ALU.subtract).then_inc(placed, 1)

                    def step(t, i, b, left):
                        one, two, three, four = (True,) * 4 if not isinstance(t, int) else (t > 0, t > 1, t > 2, t > 3)
                        if left:
                            total(t + 1, i + b, 1 - b)
                        if four:
                            note(t - 4, b)
                        if left:
                            positive(t + 1, i + b, 1 - b)
                        normalise(t, b)
                        if three:
                            assign(t - 3, 1 - b)
                        if two:
                            choose(t - 2, b)
                        if one:
                            score(t - 1, 1 - b)
                        if left:
                            residual(t + 1, i + b, 1 - b)
                        if three:
                            count_on(t - 3, 1 - b)
                        if two:
                            mark(t - 2, b)
                        if one:
                            compare(t - 1, 1 - b)
                        if three:
                            of_chosen(t - 3, 1 - b)
                        if left:
                            stats(t + 1, 1 - b)
                        if three:
                            two_places(t - 3, 1 - b)
                        if left:
                            moment(t + 1, 1 - b)

                    def last_places(t):
                        b = t % 2
                        assign(t, b)
                        count_on(t, b)
                        of_chosen(t, b)
                        two_places(t, b)
                        note(t, b)

                    v.wait_ge(const_i, 3)
                    v.tensor_scalar(lower[:, :, :], lower_i[:, :, :], 0.5, None, ALU.is_gt).then_inc(const, 1)
                    v.tensor_copy(base[:, :], base_i[:, :]).then_inc(const, 1)
                    v.tensor_copy(count[:, :], base_i[:, :]).then_inc(const, 1)
                    v.wait_ge(const, 3)
                    v.wait_ge(w_in, 48)
                    total(0, 0, 0)
                    positive(0, 0, 0)
                    residual(0, 0, 0)
                    stats(0, 0)
                    moment(0, 0)
                    by_tiles(v, step, peel=3)
                    score(NT - 1, (NT - 1) % 2)
                    compare(NT - 1, (NT - 1) % 2)
                    note(NT - 4, NT % 2)
                    last_places(NT - 3)
                    for t in range(NT - 2, NT):
                        choose(t, t % 2)
                        mark(t, t % 2)
                        last_places(t)

        with ExitStack() as st:
            zeros = at(st, "s10_zeros", [P, D])
            line_i = at(st, "s10_line_i", [P, 1], I32)
            line = at(st, "s10_line", [P, 1])
            tile_i = at(st, "s10_tile_i", [1, TILES], I32)
            fill = at(st, "s10_fill", [P, X], I32)
            many_i = at(st, "s10_many_i", [P, X], I32)
            many = at(st, "s10_many", [P, X])
            end = at(st, "s10_end", [P, X])
            shift = at(st, "s10_shift", [P, X])
            both = at(st, "s10_both", [P, NT])
            second = at(st, "s10_second", [P, NT])
            over = at(st, "s10_over", [1, TILES, X])
            exp_f = at(st, "s10_exp_f", [1, TILES])
            begin = at(st, "s10_begin", [1, TILES])
            made10, zero_made, filled, step_done = sem("s10_made"), sem("s10_zero_made"), sem("s10_filled"), sem("s10_step_done")
            left_over_out, zeros_out = sem("s10_left_over_out"), sem("s10_zeros_out")
            with nc.Block() as block:
                @block.sync
                def _(sp):
                    sp.wait_ge(zero_made, 1)
                    sp.dma_start(exp_rows[X * CAP:X * CAP + X * P, :].rearrange("(k p) d -> p k d", p=P),
                                 zeros[:, :].unsqueeze(1).broadcast_to([P, X, D])).then_inc(left_over_out, 16)
                    sp.wait_ge(left_over_out, 16)

                @block.gpsimd
                def _(pool):
                    pool.iota(line_i[:, :], pattern=[[0, 1]], base=0, channel_multiplier=1).then_inc(made10, 1)
                    pool.iota(tile_i[:, :], pattern=[[1, TILES]], base=0, channel_multiplier=0).then_inc(made10, 1)
                    pool.wait_ge(zero_made, 1)
                    pool.wait_ge(filled, 1)
                    for e in range(X):
                        pool.indirect_dma_start(out=exp_rows[:, :], in_=zeros[:, :], in_offset=None,
                                                out_offset=bass.IndirectOffsetOnAxis(ap=fill[:, e:e + 1], axis=0)).then_inc(zeros_out, 16)
                    pool.wait_ge(zeros_out, 16 * X)

                @block.vector
                def _(v):
                    steps = [0]

                    def then(ins):
                        steps[0] += 1
                        ins.then_inc(step_done, 1)
                        v.wait_ge(step_done, steps[0])

                    v.memset(zeros[:, :], 0.0).then_inc(zero_made, 1)
                    v.wait_ge(made10, 2)
                    then(v.tensor_copy(line[:, :], line_i[:, :]))
                    v.tensor_scalar(fill[:, :], count[:, :], line[:, :], None, ALU.add).then_inc(filled, 1)
                    then(v.tensor_tensor(many[:, :], count[:, :], base[:, :], ALU.subtract))
                    then(v.tensor_scalar(many_i[:, :], many[:, :], float(P - 1), None, ALU.add))
                    then(v.tensor_scalar(many_i[:, :], many_i[:, :], P.bit_length() - 1, None, ALU.logical_shift_right))
                    then(v.tensor_copy(many[:, :], many_i[:, :]))
                    then(v.tensor_tensor_scan(end[:, :], ones[:, 0:X], many[:, :], 0.0, ALU.mult, ALU.add))
                    then(v.tensor_tensor(shift[:, :], end[:, :], many[:, :], ALU.subtract))
                    then(v.scalar_tensor_tensor(out=shift[:, :], in0=shift[:, :], scalar=float(P), in1=base[:, :],
                                                op0=ALU.mult, op1=ALU.subtract))
                    tile_of = tile_i[:, :].unsqueeze(2).broadcast_to([1, TILES, X])
                    then(v.tensor_tensor(over[:, :, :], tile_of, end[0:1, :].unsqueeze(1).broadcast_to([1, TILES, X]), ALU.is_ge))
                    then(v.tensor_reduce(exp_f[:, :], over[:, :, :], AX.X, ALU.add))
                    then(v.tensor_tensor(over[:, :, :], over[:, :, :], many[0:1, :].unsqueeze(1).broadcast_to([1, TILES, X]), ALU.mult))
                    then(v.tensor_reduce(begin[:, :], over[:, :, :], AX.X, ALU.add))
                    then(v.tensor_tensor(begin[:, :], tile_i[:, :], begin[:, :], ALU.subtract))
                    then(v.tensor_scalar(begin[:, :], begin[:, :], float(P), None, ALU.mult))
                    then(v.scalar_tensor_tensor(out=tile_row[:, :], in0=exp_f[:, :], scalar=float(CAP), in1=begin[:, :],
                                                op0=ALU.mult, op1=ALU.add))
                    then(v.tensor_scalar(tile_exp[:, :], exp_f[:, :], float(X - 1), None, ALU.min))
                    then(v.tensor_tensor(place_all[:, :, :], place_all[:, :, :], shift[:, :].unsqueeze(1).broadcast_to([P, NT, X]), ALU.add))
                    then(v.tensor_tensor(place_all[:, :, :], place_all[:, :, :], mask_all[:, :, :], ALU.mult))
                    then(v.tensor_reduce(both[:, :], place_all[:, :, :], AX.X, ALU.add))
                    then(v.tensor_reduce(second[:, :], place_all[:, :, :], AX.X, ALU.max))
                    then(v.tensor_tensor(slots[:, :, 0], both[:, :], second[:, :], ALU.subtract))
                    then(v.tensor_copy(slots[:, :, 1], second[:, :]))

        scores_of.close()

        with ExitStack() as st:
            rows = at(st, "s11_rows", [P, 2, D])
            hT = at(st, "s11_hT", [P, 2, HALVES, P])
            w1_now = at(st, "s11_w1_now", [P, 2, HALVES * H1 + H1 // P])
            w2_now = at(st, "s11_w2_now", [P, 2, H1 // P * D])
            b2_now = at(st, "s11_b2_now", [P, 2, D])
            hid = at(st, "s11_hid", [P, 2, H1 // P, P])
            y = at(st, "s11_y", [P, 2, D])
            psH = [bank(st, f"s11_psH{b}", HALVES, P) for b in range(2)]
            psG = [bank(st, f"s11_psG{b}", H1 // P, P) for b in range(2)]
            psY = [bank(st, f"s11_psY{b}", D) for b in range(2)]
            rows_in, y_out = [sem(f"s11_rows_in{b}") for b in range(2)], [sem(f"s11_y_out{b}") for b in range(2)]
            w1_go, w1_ready, w2_go, w2_ready, b2_ready = (sem(f"s11_{n}") for n in ("w1_go", "w1_ready", "w2_go", "w2_ready", "b2_ready"))
            turned, hT_ready, up_done, active, down_done, y_done = (sem(f"s11_{n}") for n in ("turned", "hT_ready", "up_done", "active", "down_done", "y_done"))

            def expert(eng, t):
                return eng.value_load(tile_exp[0:1, ds(t, 1)], min_val=0, max_val=X - 1)

            with nc.Block() as block:
                @block.sync
                def _(sp):
                    def load(t, b):
                        row = sp.value_load(tile_row[0:1, ds(t, 1)], min_val=0, max_val=X * CAP + X * P - P)
                        sp.dma_start(rows[:, b, :], exp_rows[ds(row, P), :]).then_inc(rows_in[b], 16)

                    def store(t, b):
                        sp.wait_ge(y_done, t + 1)
                        sp.dma_start(y_rows[ds(t * P, P), :], y[:, b, :]).then_inc(y_out[b], 16)

                    def step(t, i, b, left):
                        if left == 2:
                            sp.wait_ge(turned, t + 1)
                            load(t + 2, b)
                        if not isinstance(t, int) or t > 0:
                            store(t - 1, 1 - b)

                    load(0, 0)
                    load(1, 1)
                    by_tiles(sp, step, TILES // 2)
                    store(TILES - 1, (TILES - 1) % 2)
                    for b in range(2):
                        sp.wait_ge(y_out[b], 16 * (TILES // 2))

                @block.scalar
                def _(act):
                    def copy_hT(t, b):
                        act.wait_ge(turned, t + 1)
                        wait_past(act, up_done, t - 1)
                        act.activation(hT[:, b, :, :], psH[b], ACT.Copy).then_inc(hT_ready, 1)

                    def second_weights(t, b):
                        e = expert(act, t)
                        wait_past(act, down_done, t - 1)
                        act.sem_inc(w2_go, 1)
                        act.activation(w2_now[:, b, :], w2[:, ds(e, 1), :].rearrange("p o n -> p (o n)"), ACT.Copy).then_inc(w2_ready, 1)

                    def gelu(t, b):
                        act.wait_ge(up_done, t + 1)
                        wait_past(act, down_done, t - 1)
                        for c in range(H1 // P):
                            g = act.activation(hid[:, b, c, :], psG[b][:, c, :], ACT.Gelu,
                                               bias=w1_now[:, b, HALVES * H1 + c:HALVES * H1 + c + 1])
                        g.then_inc(active, 1)

                    def step(t, i, b, left):
                        if left:
                            second_weights(t + 1, 1 - b)
                            gelu(t + 1, 1 - b)
                        if left == 2:
                            copy_hT(t + 2, b)

                    act.wait_ge(exp_in, 48)
                    copy_hT(0, 0)
                    copy_hT(1, 1)
                    second_weights(0, 0)
                    gelu(0, 0)
                    by_tiles(act, step, TILES // 2)

                @block.tensor
                def _(pe):
                    def turn(t, i, b):
                        pe.wait_ge(rows_in[b], 16 * i + 16)
                        wait_past(pe, hT_ready, t - 1)
                        for k in range(HALVES):
                            mm = pe.transpose(psH[b][:, k, :], rows[:, b, k * P:(k + 1) * P], ident[:, :])
                        mm.then_inc(turned, 1)

                    def up(t, b):
                        pe.wait_ge(hT_ready, t + 1)
                        pe.wait_ge(w1_ready, t + 1)
                        wait_past(pe, active, t - 1)
                        for c in range(H1 // P):
                            for k in range(HALVES):
                                at_w = k * H1 + c * P
                                mm = pe.matmul(psG[b][:, c, :], w1_now[:, b, at_w:at_w + P], hT[:, b, k, :],
                                               start=(k == 0), stop=(k == HALVES - 1))
                        mm.then_inc(up_done, 1)

                    def down(t, b):
                        pe.wait_ge(active, t + 1)
                        pe.wait_ge(w2_ready, t + 1)
                        wait_past(pe, y_done, t - 1)
                        for c in range(H1 // P):
                            mm = pe.matmul(psY[b], hid[:, b, c, :], w2_now[:, b, c * D:(c + 1) * D],
                                           start=(c == 0), stop=(c == H1 // P - 1))
                        mm.then_inc(down_done, 1)

                    def step(t, i, b, left):
                        if left:
                            up(t + 1, 1 - b)
                        if left == 2:
                            turn(t + 2, i + 1, b)
                        down(t, b)

                    turn(0, 0, 0)
                    turn(1, 0, 1)
                    up(0, 0)
                    by_tiles(pe, step, TILES // 2)

                @block.vector
                def _(v):
                    def first_weights(t, b):
                        e = expert(v, t)
                        wait_past(v, up_done, t - 1)
                        wait_past(v, active, t - 1)
                        v.sem_inc(w1_go, 1)
                        v.tensor_copy(w1_now[:, b, :], w1_b1[:, ds(e, 1), :].rearrange("p o n -> p (o n)")).then_inc(w1_ready, 1)
                        return e

                    def last_bias(e, b):
                        v.tensor_copy(b2_now[:, b, :], b2[:, ds(e, 1), :].rearrange("p o n -> p (o n)")).then_inc(b2_ready, 1)

                    def step(t, i, b, left):
                        if left == 2:
                            e = first_weights(t + 2, b)
                        v.wait_ge(down_done, t + 1)
                        v.wait_ge(b2_ready, t + 1)
                        wait_past(v, y_out[b], 16 * i)
                        v.tensor_tensor(y[:, b, :], psY[b], b2_now[:, b, :], ALU.add).then_inc(y_done, 1)
                        if left == 2:
                            v.wait_ge(y_done, t + 1)
                            last_bias(e, b)

                    v.wait_ge(exp_in, 48)
                    for b in range(2):
                        last_bias(first_weights(b, b), b)
                    by_tiles(v, step, TILES // 2)

        with ExitStack() as st:
            x3 = at(st, "s12_x3", [P, RING, D])
            got = at(st, "s12_got", [P, RING, 2, D])
            staged = at(st, "s12_staged", [P, RING, 2], I32)
            total = at(st, "s12_total", [P, RING, D])
            staged_go, staged_done, pair_done, total_done = sem("s12_staged_go"), sem("s12_staged_done"), sem("s12_pair_done"), sem("s12_total_done")
            x3_in = [sem(f"s12_x3_in{s}") for s in range(RING)]
            gathered = [sem(f"s12_gathered{s}") for s in range(RING)]
            stored = [sem(f"s12_stored{s}") for s in range(RING)]
            ROUNDS = NT // RING

            def by_round(eng, step):
                for s in range(RING):
                    step(0, s)
                with eng.Fori(1, ROUNDS) as i:
                    for s in range(RING):
                        step(i, s)

            with nc.Block() as block:
                @block.sync
                def _(sp):
                    def step(i, s):
                        wait_past(sp, total_done, (i - 1) * RING + s + 1)
                        sp.dma_start(x3[:, s, :], x3_rows[ds((i * RING + s) * P, P), :]).then_inc(x3_in[s], 16)

                    for s in range(RING):
                        sp.dma_start(x3[:, s, :], x3_rows[s * P:(s + 1) * P, :]).then_inc(x3_in[s], 16)
                    with sp.Fori(1, ROUNDS) as i:
                        for s in range(RING):
                            step(i, s)

                @block.scalar
                def _(act):
                    def stage(i, s):
                        act.sem_inc(staged_go, 1)
                        act.activation(staged[:, s, :], slots[:, ds(i * RING + s, 1), :].rearrange("p o j -> p (o j)"), ACT.Copy).then_inc(staged_done, 1)

                    def store(i, s):
                        act.wait_ge(total_done, i * RING + s + 1)
                        act.dma_start(out[ds((i * RING + s) * P, P), :], total[:, s, :]).then_inc(stored[s], 16)

                    for s in range(RING):
                        stage(0, s)
                    with act.Fori(0, ROUNDS - 1) as i:
                        for s in range(RING):
                            act.wait_ge(gathered[s], 32 * i + 32)
                            stage(i + 1, s)
                            store(i, s)
                    for s in range(RING):
                        store(ROUNDS - 1, s)
                    for s in range(RING):
                        act.wait_ge(stored[s], 16 * ROUNDS)

                @block.gpsimd
                def _(pool):
                    def step(i, s):
                        if not isinstance(i, int):
                            pool.wait_ge(total_done, i * RING - RING + s + 1)
                        pool.wait_ge(staged_done, i * RING + s + 1)
                        pool.sem_inc(staged_go, 1)
                        for j in range(2):
                            pool.indirect_dma_start(out=got[:, s, j, :], out_offset=None, in_=y_rows[:, :],
                                                    in_offset=bass.IndirectOffsetOnAxis(ap=staged[:, s, j:j + 1], axis=0)).then_inc(gathered[s], 16)

                    by_round(pool, step)

                @block.vector
                def _(v):
                    def step(i, s):
                        v.wait_ge(gathered[s], 32 * i + 32)
                        v.tensor_tensor(got[:, s, 0, :], got[:, s, 0, :], got[:, s, 1, :], ALU.add).then_inc(pair_done, 1)
                        v.wait_ge(pair_done, i * RING + s + 1)
                        v.wait_ge(x3_in[s], 16 * i + 16)
                        wait_past(v, stored[s], 16 * i)
                        v.tensor_tensor(total[:, s, :], got[:, s, 0, :], x3[:, s, :], ALU.add).then_inc(total_done, 1)

                    by_round(v, step)




def lay_out(x, src, dst, edge_type_8, edge_weight, L0_gnn_weight, L0_ffn_wr, L0_ffn_br, L0_ffn_w1, L0_ffn_b1,
            L0_ffn_w2, L0_ffn_b2, L1_gnn_W, L1_gnn_att_src, L1_gnn_att_dst, L1_gnn_bias, L1_ffn_Wg, L1_ffn_bg,
            L1_ffn_W1, L1_ffn_b1, L1_ffn_W2, L1_ffn_b2, L0_ffn_attention_mask=None):
    import numpy as np

    def padded(v, value):
        return np.concatenate([v, np.full(P * ROW - E, value, v.dtype)])

    def by_row(v):
        return v.reshape(P, ROW)

    def by_chunk(v):
        return v.reshape(CHUNKS, P).T

    src, dst = padded(np.asarray(src), N), padded(np.asarray(dst), N)
    x = np.asarray(x)
    blocks = np.asarray(L0_gnn_weight).reshape(R, NB, SB, SB)
    rel_w = np.zeros((P, HALVES, R, P), np.float32)
    per = P // SB
    for k in range(HALVES):
        for j in range(per):
            o = slice(j * SB, (j + 1) * SB)
            rel_w[o, k, :, o] = blocks[:, k * per + j].transpose(1, 0, 2)
    edge = np.array([-1], np.int32)
    b = {
        "x": np.concatenate([x, np.zeros((NP - N, D), x.dtype)]),
        "rel_w": rel_w.reshape(P, HALVES, R * P),
        "src_row": by_row(src), "dst_row": by_row(dst),
        "dst_before": by_row(np.concatenate([edge, dst[:-1]])),
        "dst_after": by_row(np.concatenate([dst[1:], edge])),
        "src_chunk": by_chunk(src), "dst_chunk": by_chunk(dst),
        "dst_first": np.concatenate([dst[:1], dst[::WIDE]]).reshape(1, SPANS + 1),
        "type_chunk": by_chunk(padded(np.asarray(edge_type_8), 0)),
        "weight_chunk": by_chunk(padded(np.asarray(edge_weight), 0)),
        "wr": np.asarray(L0_ffn_wr).reshape(1, D), "br": np.asarray(L0_ffn_br).reshape(1, 1),
        "ffn_w1": np.asarray(L0_ffn_w1).reshape(HALVES, P, H0).transpose(1, 0, 2),
        "ffn_b1": np.asarray(L0_ffn_b1).reshape(H0 // P, P).T,
        "ffn_w2": np.asarray(L0_ffn_w2).reshape(H0 // P, P, D).transpose(1, 0, 2),
        "ffn_b2": np.asarray(L0_ffn_b2).reshape(1, D),
        "att_w": np.asarray(L1_gnn_W).reshape(HALVES, P, D).transpose(1, 0, 2),
        "att": np.stack([np.asarray(L1_gnn_att_src).reshape(D), np.asarray(L1_gnn_att_dst).reshape(D)]).reshape(1, 2 * D),
        "att_bias": np.asarray(L1_gnn_bias).reshape(1, D),
        "gate_w": np.asarray(L1_ffn_Wg).reshape(HALVES, P, X).transpose(1, 0, 2),
        "gate_b": np.asarray(L1_ffn_bg).reshape(1, X),
        "exp_w1_b1": np.concatenate([
            np.asarray(L1_ffn_W1).reshape(X, HALVES, P, H1).transpose(2, 0, 1, 3).reshape(P, X, HALVES * H1),
            np.asarray(L1_ffn_b1).reshape(X, H1 // P, P).transpose(2, 0, 1)], axis=2),
        "exp_w2": np.asarray(L1_ffn_W2).reshape(X, H1 // P, P, D).transpose(2, 0, 1, 3).reshape(P, X, H1 // P * D),
        "exp_b2": np.asarray(L1_ffn_b2).reshape(1, X * D),
    }
    return {f"in_{k}": np.ascontiguousarray(v) for k, v in b.items()}


def kernel(**inputs):
    import concourse.bacc as bacc
    from concourse.bass_utils import run_bass_kernel_spmd

    arrays = lay_out(**inputs)
    nc = bacc.Bacc("TRN2", target_bir_lowering=False, num_devices=1)
    aps = {n[3:]: nc.dram_tensor(n, v.shape, mybir.dt.from_np(v.dtype), kind="ExternalInput").ap() for n, v in arrays.items()}
    out = nc.dram_tensor("out", (NP, D), F32, kind="ExternalOutput").ap()
    gnn_kernel(nc, aps, out)
    r = run_bass_kernel_spmd(nc, [arrays], core_ids=[0])
    return r.results[0]["out"][:N]
```
